# Optimizing a Trainium2 kernel written in Bass

```python
import numpy as np
import jax
import jax.numpy as jnp

def _softmax(x, axis=-1):
    return jax.nn.softmax(x, axis=axis)

def _gelu(x):
    return jax.nn.gelu(x, approximate=True)

def _silu(x):
    return jax.nn.silu(x)

def _sigmoid(x):
    return jax.nn.sigmoid(x)

def _layernorm(x, axis=-1, eps=1e-05):
    m = jnp.mean(x, axis=axis, keepdims=True)
    v = jnp.var(x, axis=axis, keepdims=True)
    return (x - m) / jnp.sqrt(v + eps)

def _scatter_add(tgt, idx, src, axis=0):
    return tgt.at[idx].add(src)

def _segment_sum(src, seg, n):
    return jax.ops.segment_sum(src, seg, n)
kernel_name = 'mk_flamingo_gated_d2_seqx_r4_653246'

def setup_inputs(seed: int=0):
    np.random.seed(seed)
    _w = jnp.asarray

    def _rec_inputs():
        import jax
        import jax.numpy as jnp
        _rk = jax.random.key(seed)
        x = -0.000125 + 0.9999 * jax.random.normal(jax.random.fold_in(_rk, 1), (4, 512, 512), jnp.float32)
        _lenS = 512 - jax.random.randint(jax.random.fold_in(_rk, 7), (4,), 0, max(1, 512 // 4) + 1, jnp.int32)
        _lenS2 = 512 - jax.random.randint(jax.random.fold_in(_rk, 8), (4,), 0, max(1, 512 // 4) + 1, jnp.int32)
        itok_BxS_13_99985 = jax.random.randint(jax.random.fold_in(_rk, 11), (4, 512), 13, 99986, jnp.int32)
        _ctx_2048P = jax.random.normal(jax.random.fold_in(_rk, 12), (4, 16, 512), jnp.float32)
        _ctx_2048c = jax.random.dirichlet(jax.random.fold_in(_rk, 512), 0.3 * jnp.ones((16,), jnp.float32), (4, 512))
        _ctx_2048t = jnp.einsum('bsk,bkd->bsd', _ctx_2048c, _ctx_2048P)
        _ctx_2048t = _ctx_2048t * jax.lax.rsqrt(jnp.mean(jnp.square(_ctx_2048t)) + 1e-12) * 0.953939
        ctx_2048 = 6.82029e-06 + 0.0200006 * (_ctx_2048t + 0.3 * jax.random.normal(jax.random.fold_in(_rk, 612), (4, 512, 512), jnp.float32))
        _g = jax.random.normal(jax.random.fold_in(_rk, 9001), (2, 2), jnp.float32)
        _g = jnp.sign(_g) * jnp.maximum(jnp.abs(_g), 1.0) + (_g == 0) * 1.0
        g_xattn = _g[0]
        g_ffn = _g[1]
        return (x, itok_BxS_13_99985, ctx_2048, g_xattn, g_ffn)
    x, itok_BxS_13_99985, ctx_2048, g_xattn, g_ffn = _rec_inputs()

    def _L0_xattn_setup():
        import jax, jax.numpy as jnp
        import numpy as np
        B, S, D = (4, 1024, 512)
        E = 4
        F = 2048 // E
        VOCAB = 25000
        key = jax.random.key(seed)
        k1, k2, k3, k4, k5 = jax.random.split(key, 5)
        hidden_states = jax.random.normal(k1, (B, S, D), dtype=jnp.float32)
        token_ids = jax.random.randint(k2, (B, S), 0, VOCAB, dtype=jnp.int64)
        Wg = jax.random.normal(k3, (E, F, D), dtype=jnp.float32) * 0.02
        Wu = jax.random.normal(k4, (E, F, D), dtype=jnp.float32) * 0.02
        Wd = jax.random.normal(k5, (E, D, F), dtype=jnp.float32) * 0.02
        return {'hidden_states': hidden_states, 'token_ids': token_ids, 'Wg': Wg, 'Wu': Wu, 'Wd': Wd}
    _L0_xattn_all = _L0_xattn_setup()
    _L0_xattn_in = {k: v for k, v in _L0_xattn_all.items() if k in ()}
    del _L0_xattn_all

    def _L0_ffn_setup():
        import jax, jax.numpy as jnp
        import numpy as np
        D_MODEL, D_FF, NS, NR, KR = (512, 352, 2, 16, 4)
        B, S = (4, 512)

        def _moe_forward(u, shared_w1, shared_b1, shared_w2, shared_b2, routed_w1, routed_b1, routed_w2, routed_b2, centroids, bias):
            b, s, d = u.shape
            flat = u.reshape(-1, d)
            T = flat.shape[0]
            h = jax.nn.relu(jnp.einsum('td,ndf->ntf', flat, shared_w1) + shared_b1[:, None, :])
            shared_out = jnp.einsum('ntf,nfd->td', h, shared_w2) + shared_b2.sum(0)
            out = flat + shared_out
            scores = jax.nn.sigmoid(flat @ centroids.T) + bias
            vals, idx = jax.lax.top_k(scores, KR)
            gating = jnp.zeros_like(scores).at[jnp.arange(T)[:, None], idx].set(vals)
            gating = gating / jnp.clip(gating.sum(-1, keepdims=True), 1e-08)

            def step(acc, ew):
                w1, b1, w2, b2, g = ew
                hj = jax.nn.relu(flat @ w1 + b1)
                yj = hj @ w2 + b2
                return (acc + yj * g[:, None], None)
            rout0 = jnp.zeros_like(flat)
            rout, _ = jax.lax.scan(step, rout0, (routed_w1, routed_b1, routed_w2, routed_b2, gating.T))
            return (out + rout).reshape(b, s, d)
        key = jax.random.key(seed)
        ks = jax.random.split(key, 10)
        s1 = 1.0 / np.sqrt(D_MODEL)
        s2 = 1.0 / np.sqrt(D_FF)
        return {'u': jax.random.normal(ks[0], (B, S, D_MODEL), dtype=jnp.float32), 'shared_w1': jax.random.normal(ks[1], (NS, D_MODEL, D_FF), dtype=jnp.float32) * s1, 'shared_b1': jnp.zeros((NS, D_FF), dtype=jnp.float32), 'shared_w2': jax.random.normal(ks[2], (NS, D_FF, D_MODEL), dtype=jnp.float32) * s2, 'shared_b2': jnp.zeros((NS, D_MODEL), dtype=jnp.float32), 'routed_w1': jax.random.normal(ks[3], (NR, D_MODEL, D_FF), dtype=jnp.float32) * s1, 'routed_b1': jnp.zeros((NR, D_FF), dtype=jnp.float32), 'routed_w2': jax.random.normal(ks[4], (NR, D_FF, D_MODEL), dtype=jnp.float32) * s2, 'routed_b2': jnp.zeros((NR, D_MODEL), dtype=jnp.float32), 'centroids': jax.random.normal(ks[5], (NR, D_MODEL), dtype=jnp.float32) * s1, 'bias': jnp.zeros((NR,), dtype=jnp.float32)}
    _L0_ffn_all = _L0_ffn_setup()
    _L0_ffn_in = {k: v for k, v in _L0_ffn_all.items() if k in ('shared_w1', 'shared_b1', 'shared_w2', 'shared_b2', 'routed_w1', 'routed_b1', 'routed_w2', 'routed_b2', 'centroids', 'bias')}
    del _L0_ffn_all

    def _L1_xattn_setup():
        import jax, jax.numpy as jnp
        import numpy as np
        DIM = 512
        NHEADS = 32
        HEAD_DIM = DIM // NHEADS
        EPS = 1e-06

        def _rmsnorm(t):
            return t * jax.lax.rsqrt(jnp.mean(t * t, axis=-1, keepdims=True) + EPS)
        key = jax.random.key(seed)
        kx, kc, kq, kk, kv = jax.random.split(key, 5)
        x = jax.random.normal(kx, (2, 1024, DIM), dtype=jnp.float32)
        context = jax.random.normal(kc, (2, 128, DIM), dtype=jnp.float32)
        std = 0.02
        Wq = jax.random.normal(kq, (DIM, DIM), dtype=jnp.float32) * std
        Wk = jax.random.normal(kk, (DIM, DIM), dtype=jnp.float32) * std
        Wv = jax.random.normal(kv, (DIM, DIM), dtype=jnp.float32) * std
        return {'x': x, 'context': context, 'Wq': Wq, 'Wk': Wk, 'Wv': Wv}
    _L1_xattn_all = _L1_xattn_setup()
    _L1_xattn_in = {k: v for k, v in _L1_xattn_all.items() if k in ('Wq', 'Wk', 'Wv')}
    del _L1_xattn_all

    def _L1_ffn_setup():
        import jax, jax.numpy as jnp
        import numpy as np
        D_MODEL = 512
        NUM_TILES = 64
        D_SLICE = D_MODEL // NUM_TILES
        TILES_PER_CLUSTER = 8
        NUM_CLUSTERS = NUM_TILES // TILES_PER_CLUSTER
        GRID = 16
        LN_EPS = 1e-05
        DIMS = (np.arange(NUM_TILES)[:, None] * D_SLICE + np.arange(D_SLICE)[None, :]) % D_MODEL
        DIMS = jnp.asarray(DIMS, dtype=jnp.int32)

        def _forward(x, ln_gamma, ln_beta, spline_bases, spline_slopes, output_scale):
            B, S, D = x.shape
            N = B * S
            mu = jnp.mean(x, axis=-1, keepdims=True)
            var = jnp.mean(jnp.square(x - mu), axis=-1, keepdims=True)
            xn = (x - mu) * jax.lax.rsqrt(var + LN_EPS) * ln_gamma + ln_beta
            xf = xn.reshape(N, D)
            slope_sign = jnp.sign(jnp.mean(spline_slopes, axis=-1))
            tile_sigs = jnp.zeros((NUM_TILES, D), dtype=x.dtype)
            tile_sigs = tile_sigs.at[jnp.arange(NUM_TILES)[:, None], DIMS].set(slope_sign)
            cluster_sigs = jnp.sign(tile_sigs.reshape(NUM_CLUSTERS, TILES_PER_CLUSTER, D).mean(axis=1))
            cluster_assign = jnp.arange(NUM_TILES, dtype=jnp.int32) // TILES_PER_CLUSTER
            input_sigs = jnp.sign(xf)
            cluster_scores = input_sigs @ cluster_sigs.T
            best_cluster = jnp.argmax(cluster_scores, axis=-1)
            tile_scores = input_sigs @ tile_sigs.T
            in_cluster = cluster_assign[None, :] == best_cluster[:, None]
            tile_idx = jnp.argmax(jnp.where(in_cluster, tile_scores, -jnp.inf), axis=-1)
            tok_dims = DIMS[tile_idx]
            x_slice = jnp.take_along_axis(xf, tok_dims, axis=1)
            tok_min = x_slice.min(axis=1)
            tok_max = x_slice.max(axis=1)
            onehot = tile_idx[None, :] == jnp.arange(NUM_TILES)[:, None]
            tile_min = jnp.where(onehot, tok_min[None, :], jnp.inf).min(axis=1)
            tile_max = jnp.where(onehot, tok_max[None, :], -jnp.inf).max(axis=1)
            mn = tile_min[tile_idx][:, None]
            mx = tile_max[tile_idx][:, None]
            u = jnp.clip((x_slice - mn) / (mx - mn + 1e-08), 0.0, 1.0 - 1e-06)
            gi = jnp.clip((u * GRID).astype(jnp.int32), 0, GRID - 1)
            j = jnp.arange(D_SLICE)[None, :]
            b = spline_bases[tile_idx[:, None], j, gi]
            s = spline_slopes[tile_idx[:, None], j, gi]
            x_local = (u - gi.astype(u.dtype) / GRID) * GRID
            delta = (b + s * x_local) * output_scale[tile_idx][:, None]
            out = jnp.zeros_like(xf).at[jnp.arange(N)[:, None], tok_dims].set(delta)
            return x + out.reshape(B, S, D)
        key = jax.random.key(seed)
        k1, k2, k3, k4, k5, k6 = jax.random.split(key, 6)
        x = jax.random.normal(k1, (4, 1024, D_MODEL), dtype=jnp.float32)
        ln_gamma = 1.0 + 0.1 * jax.random.normal(k2, (D_MODEL,), dtype=jnp.float32)
        ln_beta = 0.1 * jax.random.normal(k3, (D_MODEL,), dtype=jnp.float32)
        spline_bases = 0.1 * jax.random.normal(k4, (NUM_TILES, D_SLICE, GRID), dtype=jnp.float32)
        spline_slopes = 0.1 + 0.1 * jax.random.normal(k5, (NUM_TILES, D_SLICE, GRID), dtype=jnp.float32)
        output_scale = 1.0 + 0.1 * jax.random.normal(k6, (NUM_TILES,), dtype=jnp.float32)
        return {'x': x, 'ln_gamma': ln_gamma, 'ln_beta': ln_beta, 'spline_bases': spline_bases, 'spline_slopes': spline_slopes, 'output_scale': output_scale}
    _L1_ffn_all = _L1_ffn_setup()
    _L1_ffn_in = {k: v for k, v in _L1_ffn_all.items() if k in ('ln_gamma', 'ln_beta', 'spline_bases', 'spline_slopes', 'output_scale')}
    del _L1_ffn_all
    return {'x': x, 'itok_BxS_13_99985': itok_BxS_13_99985, 'ctx_2048': ctx_2048, 'g_xattn': g_xattn, 'g_ffn': g_ffn, 'L0_ffn_shared_w1': _L0_ffn_in['shared_w1'], 'L0_ffn_shared_b1': _L0_ffn_in['shared_b1'], 'L0_ffn_shared_w2': _L0_ffn_in['shared_w2'], 'L0_ffn_shared_b2': _L0_ffn_in['shared_b2'], 'L0_ffn_routed_w1': _L0_ffn_in['routed_w1'], 'L0_ffn_routed_b1': _L0_ffn_in['routed_b1'], 'L0_ffn_routed_w2': _L0_ffn_in['routed_w2'], 'L0_ffn_routed_b2': _L0_ffn_in['routed_b2'], 'L0_ffn_centroids': _L0_ffn_in['centroids'], 'L0_ffn_bias': _L0_ffn_in['bias'], 'L1_xattn_Wq': _L1_xattn_in['Wq'], 'L1_xattn_Wk': _L1_xattn_in['Wk'], 'L1_xattn_Wv': _L1_xattn_in['Wv'], 'L1_ffn_ln_gamma': _L1_ffn_in['ln_gamma'], 'L1_ffn_ln_beta': _L1_ffn_in['ln_beta'], 'L1_ffn_spline_bases': _L1_ffn_in['spline_bases'], 'L1_ffn_spline_slopes': _L1_ffn_in['spline_slopes'], 'L1_ffn_output_scale': _L1_ffn_in['output_scale']}

def reference(x, itok_BxS_13_99985, ctx_2048, g_xattn, g_ffn, L0_ffn_shared_w1, L0_ffn_shared_b1, L0_ffn_shared_w2, L0_ffn_shared_b2, L0_ffn_routed_w1, L0_ffn_routed_b1, L0_ffn_routed_w2, L0_ffn_routed_b2, L0_ffn_centroids, L0_ffn_bias, L1_xattn_Wq, L1_xattn_Wk, L1_xattn_Wv, L1_ffn_ln_gamma, L1_ffn_ln_beta, L1_ffn_spline_bases, L1_ffn_spline_slopes, L1_ffn_output_scale):
    import jax
    import jax.numpy as jnp

    def _L0_xattn_ref(hidden_states, token_ids, Wg, Wu, Wd):
        import jax, jax.numpy as jnp
        import numpy as np
        B, S, D = (4, 1024, 512)
        E = 4
        F = 2048 // E
        VOCAB = 25000
        tokens_per_expert = VOCAB // E
        tid = jnp.clip(token_ids, 0, VOCAB - 1)
        expert_ids = jnp.minimum(tid // tokens_per_expert, E - 1)
        out = jnp.zeros_like(hidden_states)
        for e in range(E):
            g = jax.nn.silu(jnp.einsum('bsd,fd->bsf', hidden_states, Wg[e]))
            u = jnp.einsum('bsd,fd->bsf', hidden_states, Wu[e])
            y = jnp.einsum('bsf,df->bsd', g * u, Wd[e])
            out = jnp.where((expert_ids == e)[..., None], y, out)
        return out

    def _L0_ffn_ref(u, shared_w1, shared_b1, shared_w2, shared_b2, routed_w1, routed_b1, routed_w2, routed_b2, centroids, bias):
        import jax, jax.numpy as jnp
        import numpy as np
        D_MODEL, D_FF, NS, NR, KR = (512, 352, 2, 16, 4)
        B, S = (4, 512)

        def _moe_forward(u, shared_w1, shared_b1, shared_w2, shared_b2, routed_w1, routed_b1, routed_w2, routed_b2, centroids, bias):
            b, s, d = u.shape
            flat = u.reshape(-1, d)
            T = flat.shape[0]
            h = jax.nn.relu(jnp.einsum('td,ndf->ntf', flat, shared_w1) + shared_b1[:, None, :])
            shared_out = jnp.einsum('ntf,nfd->td', h, shared_w2) + shared_b2.sum(0)
            out = flat + shared_out
            scores = jax.nn.sigmoid(flat @ centroids.T) + bias
            vals, idx = jax.lax.top_k(scores, KR)
            gating = jnp.zeros_like(scores).at[jnp.arange(T)[:, None], idx].set(vals)
            gating = gating / jnp.clip(gating.sum(-1, keepdims=True), 1e-08)

            def step(acc, ew):
                w1, b1, w2, b2, g = ew
                hj = jax.nn.relu(flat @ w1 + b1)
                yj = hj @ w2 + b2
                return (acc + yj * g[:, None], None)
            rout0 = jnp.zeros_like(flat)
            rout, _ = jax.lax.scan(step, rout0, (routed_w1, routed_b1, routed_w2, routed_b2, gating.T))
            return (out + rout).reshape(b, s, d)
        return _moe_forward(u, shared_w1, shared_b1, shared_w2, shared_b2, routed_w1, routed_b1, routed_w2, routed_b2, centroids, bias)

    def _L1_xattn_ref(x, context, Wq, Wk, Wv):
        import jax, jax.numpy as jnp
        import numpy as np
        DIM = 512
        NHEADS = 32
        HEAD_DIM = DIM // NHEADS
        EPS = 1e-06

        def _rmsnorm(t):
            return t * jax.lax.rsqrt(jnp.mean(t * t, axis=-1, keepdims=True) + EPS)
        b, n, _ = x.shape
        m = context.shape[1]
        q = x @ Wq.T
        k_raw = context @ Wk.T
        v_raw = context @ Wv.T
        q = q.reshape(b, n, NHEADS, HEAD_DIM).transpose(0, 2, 1, 3)
        kv = jnp.concatenate([k_raw, v_raw], axis=-1)
        kv = kv.reshape(b, m, NHEADS, HEAD_DIM, 2)
        k = kv[..., 0].transpose(0, 2, 1, 3)
        v = kv[..., 1].transpose(0, 2, 1, 3)
        q = _rmsnorm(q)
        k = _rmsnorm(k)
        scale = HEAD_DIM ** (-0.5)
        scores = jnp.einsum('bhnd,bhmd->bhnm', q, k) * scale
        attn = jax.nn.softmax(scores, axis=-1)
        out = jnp.einsum('bhnm,bhmd->bhnd', attn, v)
        return out.transpose(0, 2, 1, 3).reshape(b, n, NHEADS * HEAD_DIM)

    def _L1_ffn_ref(x, ln_gamma, ln_beta, spline_bases, spline_slopes, output_scale):
        import jax, jax.numpy as jnp
        import numpy as np
        D_MODEL = 512
        NUM_TILES = 64
        D_SLICE = D_MODEL // NUM_TILES
        TILES_PER_CLUSTER = 8
        NUM_CLUSTERS = NUM_TILES // TILES_PER_CLUSTER
        GRID = 16
        LN_EPS = 1e-05
        DIMS = (np.arange(NUM_TILES)[:, None] * D_SLICE + np.arange(D_SLICE)[None, :]) % D_MODEL
        DIMS = jnp.asarray(DIMS, dtype=jnp.int32)

        def _forward(x, ln_gamma, ln_beta, spline_bases, spline_slopes, output_scale):
            B, S, D = x.shape
            N = B * S
            mu = jnp.mean(x, axis=-1, keepdims=True)
            var = jnp.mean(jnp.square(x - mu), axis=-1, keepdims=True)
            xn = (x - mu) * jax.lax.rsqrt(var + LN_EPS) * ln_gamma + ln_beta
            xf = xn.reshape(N, D)
            slope_sign = jnp.sign(jnp.mean(spline_slopes, axis=-1))
            tile_sigs = jnp.zeros((NUM_TILES, D), dtype=x.dtype)
            tile_sigs = tile_sigs.at[jnp.arange(NUM_TILES)[:, None], DIMS].set(slope_sign)
            cluster_sigs = jnp.sign(tile_sigs.reshape(NUM_CLUSTERS, TILES_PER_CLUSTER, D).mean(axis=1))
            cluster_assign = jnp.arange(NUM_TILES, dtype=jnp.int32) // TILES_PER_CLUSTER
            input_sigs = jnp.sign(xf)
            cluster_scores = input_sigs @ cluster_sigs.T
            best_cluster = jnp.argmax(cluster_scores, axis=-1)
            tile_scores = input_sigs @ tile_sigs.T
            in_cluster = cluster_assign[None, :] == best_cluster[:, None]
            tile_idx = jnp.argmax(jnp.where(in_cluster, tile_scores, -jnp.inf), axis=-1)
            tok_dims = DIMS[tile_idx]
            x_slice = jnp.take_along_axis(xf, tok_dims, axis=1)
            tok_min = x_slice.min(axis=1)
            tok_max = x_slice.max(axis=1)
            onehot = tile_idx[None, :] == jnp.arange(NUM_TILES)[:, None]
            tile_min = jnp.where(onehot, tok_min[None, :], jnp.inf).min(axis=1)
            tile_max = jnp.where(onehot, tok_max[None, :], -jnp.inf).max(axis=1)
            mn = tile_min[tile_idx][:, None]
            mx = tile_max[tile_idx][:, None]
            u = jnp.clip((x_slice - mn) / (mx - mn + 1e-08), 0.0, 1.0 - 1e-06)
            gi = jnp.clip((u * GRID).astype(jnp.int32), 0, GRID - 1)
            j = jnp.arange(D_SLICE)[None, :]
            b = spline_bases[tile_idx[:, None], j, gi]
            s = spline_slopes[tile_idx[:, None], j, gi]
            x_local = (u - gi.astype(u.dtype) / GRID) * GRID
            delta = (b + s * x_local) * output_scale[tile_idx][:, None]
            out = jnp.zeros_like(xf).at[jnp.arange(N)[:, None], tok_dims].set(delta)
            return x + out.reshape(B, S, D)
        return _forward(x, ln_gamma, ln_beta, spline_bases, spline_slopes, output_scale)
    x = x + jnp.tanh(g_xattn[0]) * _L0_xattn_ref(_layernorm(x, axis=-1), itok_BxS_13_99985, ctx_2048, ctx_2048, ctx_2048)
    x = x + jnp.tanh(g_ffn[0]) * _L0_ffn_ref(_layernorm(x, axis=-1), L0_ffn_shared_w1, L0_ffn_shared_b1, L0_ffn_shared_w2, L0_ffn_shared_b2, L0_ffn_routed_w1, L0_ffn_routed_b1, L0_ffn_routed_w2, L0_ffn_routed_b2, L0_ffn_centroids, L0_ffn_bias)
    x = x + jnp.tanh(g_xattn[1]) * _L1_xattn_ref(_layernorm(x, axis=-1), ctx_2048, L1_xattn_Wq, L1_xattn_Wk, L1_xattn_Wv)
    x = x + jnp.tanh(g_ffn[1]) * _L1_ffn_ref(_layernorm(x, axis=-1), L1_ffn_ln_gamma, L1_ffn_ln_beta, L1_ffn_spline_bases, L1_ffn_spline_slopes, L1_ffn_output_scale)
    return x

_drawn_inputs = setup_inputs


def setup_inputs(seed=0):
    import zlib

    import numpy as np

    out = dict(_drawn_inputs(seed))
    spreads = {'g_ffn': (-1.0, 0.2),
     'L0_ffn_shared_b1': (0.0, 0.1),
     'L0_ffn_shared_b2': (0.0, 0.1),
     'L0_ffn_routed_b1': (0.0, 0.1),
     'L0_ffn_routed_b2': (0.0, 0.1),
     'L0_ffn_bias': (0.0, 0.1)}
    factors = {'L1_ffn_output_scale': 3.246}
    for name, (base, spread) in spreads.items():
        noise = np.random.default_rng([zlib.crc32(name.encode()), seed]).standard_normal(out[name].shape)
        drawn = base * np.exp(spread * noise) if base else spread * noise
        out[name] = jnp.asarray(drawn.astype(out[name].dtype))
    for name, factor in factors.items():
        out[name] = (out[name] * factor).astype(out[name].dtype)
    return out
```

```python
import numpy as np
import concourse.bass as bass
from concourse import mybir
from contextlib import ExitStack

f32 = mybir.dt.float32
f16 = mybir.dt.float16
i32 = mybir.dt.int32
u32 = mybir.dt.uint32
ALU = mybir.AluOpType
ACT = mybir.ActivationFunctionType
AX = mybir.AxisListType

P = 128
BATCH, SEQ, D = 4, 512, 512
TOK = BATCH * SEQ
NT = TOK // P
KD = D // P
E1, RANGE1, TOP1 = 4, 25000 // 4, 3
FF, FB = 352, 3
FLAST = FF - 2 * P
NS, NR, KR = 2, 16, 4
NH, HD = 32, 16
GRID, NTILE, DSL, NCL = 16, 64, 8, 8
EPS = 1e-5
EPS_RMS = 1e-6
CAP = TOK
N1 = NT + E1
N2 = NT * KR + NR
SA, SW = 16.0, 64.0
UNSCALE = 1.0 / (SA * SW)


class It:

    def __init__(self, half, parity):
        self.half, self.p = half, parity
        self.n = half * 2 + parity

    def back(self, k):
        q = self.p - k
        return It(self.half + (q // 2), q % 2)


class Sync:

    def __init__(self, nc):
        self.nc, self.sems, self.phase = nc, {}, 0

    def sem(self, name):
        if name not in self.sems:
            self.sems[name] = self.nc.alloc_semaphore(f"{name}_{self.phase}")
        return self.sems[name]

    def clear(self):
        self.nc.clear_and_free_semaphores(list(self.sems.values()))
        self.nc.all_engine_barrier()
        self.sems, self.phase = {}, self.phase + 1

    def done(self, ins, name):
        ins.then_inc(self.sem(name), 1)

    def moved(self, ins, name, it):
        ins.then_inc(self.sem(f"{name}{it.p}"), 16)

    def wait(self, eng, name, it, each=1):
        self.reach(eng, name, it, (it.n + 1) * each)

    def wait_moved(self, eng, name, it, each=1):
        self.reach(eng, f"{name}{it.p}", it, (it.half + 1) * (16 * each))

    def reach(self, eng, name, it, value):
        if not isinstance(it.n, int) or it.n >= 0:
            eng.wait_ge(self.sem(name), value)
            if not isinstance(it.n, int) and eng_name(eng) == "SP":
                self.static(eng)

    def static(self, eng):
        eng.sem_inc(self.sem("spare_" + eng_name(eng)), 1)


def eng_name(eng):
    return str(eng.engine).split(".")[-1]


class Line:

    def __init__(self, sync, eng, name):
        self.s, self.eng, self.link, self.per, self.k = sync, eng, name, None, 0

    def start(self, it):
        if self.k and self.per is None:
            self.per = self.k
        assert self.per is None or self.k in (0, self.per)
        self.it, self.k = it, 0

    def __call__(self, ins, name=None):
        if name:
            self.s.done(ins, name)
            self.s.wait(self.eng, name, self.it)
        else:
            self.k += 1
            ins.then_inc(self.s.sem(self.link), 1)
            first = self.per is None
            self.eng.wait_ge(self.s.sem(self.link), self.k if first else self.it.n * self.per + self.k)


def pipeline(eng, n, stages):
    most = max(lag for _, lag in stages)
    beats, first = n + most, (most + 3) // 2 * 2
    full = max(0, (n - first) // 2)

    def beat(it):
        for stage, lag in stages:
            at = it.back(lag)
            if not isinstance(at.n, int) or 0 <= at.n < n:
                stage(at)

    for i in range(min(first, beats)):
        beat(It(i // 2, i % 2))
    if full:
        with eng.Fori(0, full) as h:
            for p in range(2):
                beat(It(h + first // 2, p))
    for i in range(first + 2 * full, beats):
        beat(It(i // 2, i % 2))


def bcast(ap, dims):
    return bass.AP(ap.tensor, ap.offset, [list(ap.ap[0])] + [[s, c] for s, c in dims])


def build(nc, a, out):
    with ExitStack() as ctx:
        S = Sync(nc)

        def sb(mem, name, shape, dt=f32):
            return mem.enter_context(nc.sbuf_tensor("sb_" + name, shape, dt))

        def ps(mem, name, shape, dt=f32):
            return mem.enter_context(nc.psum_tensor("ps_" + name, shape, dt))

        def dram(name, shape, dt=f32):
            return nc.dram_tensor(name, shape, dt).ap()

        R = {
            "list1": dram("list1", (N1 * P, 1), i32),
            "list2": dram("list2", (NR * CAP + N2 * P, 1), i32),
            "y1s": dram("y1s", (N1 * P, D)),
            "xn2": dram("xn2", (TOK, 2 * D), f16),
            "x2a": dram("x2a", (TOK, D)),
            "ys": dram("ys", (N2 * P, D)),
            "kst": dram("kst", (NT, P, 4 * D), f16),
            "vst": dram("vst", (NT, P, NH * (HD + 1))),
            "qst": dram("qst", (NT, P, 4 * D), f16),
            "x2": dram("x2", (TOK, D)),
            "sign": dram("sign", (D,)),
        }
        K = {
            "ident": sb(ctx, "ident", [P, P], f16),
            "tri": sb(ctx, "tri", [P, P], f16),
            "ones": sb(ctx, "ones", [P, P], f16),
            "iota": sb(ctx, "iota", [P, 16]),
            "tok": sb(ctx, "tok", [P, NT], i32),
            "gate": sb(ctx, "gate", [P, 8]),
            "pos1": sb(ctx, "pos1", [P, NT], i32),
            "pos2": sb(ctx, "pos2", [P, NT * KR], i32),
            "g2f": sb(ctx, "g2f", [P, NT * KR]),
            "tab1": sb(ctx, "tab1", [1, N1], i32),
            "tab2": sb(ctx, "tab2", [1, 2, N2], i32),
            "mhalf": sb(ctx, "mhalf", [P, 1]),
            "iotan": sb(ctx, "iotan", [1, N2]),
        }
        for phase in (phase_setup, phase_layer1, phase_shared, phase_routed, phase_keys, phase_queries):
            phase(nc, S, sb, ps, a, R, K)
            S.clear()
        phase_attention(nc, S, sb, ps, a, R, K, out)


def make_table(line, v, mem, sb, tag, e, n, count, K, expert, row, pos, posi):
    cols = pos.shape[1]
    gt = sb(mem, tag + "gt", [P, e, 16])
    lim = sb(mem, tag + "lim", [P, 16])
    nt = sb(mem, tag + "nt", [P, e])
    cum = [sb(mem, tag + f"cum{i}", [P, e]) for i in range(2)]
    skip = sb(mem, tag + "skip", [P, e])
    end = sb(mem, tag + "end", [P, e])
    ge = sb(mem, tag + "ge", [1, n, e])
    ef = sb(mem, tag + "ef", [1, n])
    st = sb(mem, tag + "st", [1, n])
    gp = sb(mem, tag + "gp", [P, cols, e])
    sp = sb(mem, tag + "sp", [P, cols])
    line(v.tensor_scalar(lim[:, :], K["iota"][:, :], float(P), None, ALU.mult))
    line(v.tensor_tensor(gt[:, :, :], bcast(count, [(count.ap[1][0], e), (0, 16)]),
                         bcast(lim[:, 0:1], [(0, e), (1, 16)]), ALU.is_gt))
    line(v.tensor_reduce(nt[:, :], gt[:, :, :], AX.X, ALU.add))
    line(v.tensor_copy(cum[0][:, :], nt[:, :]))
    cur, d = 0, 1
    while d < e:
        line(v.tensor_copy(cum[1 - cur][:, 0:d], cum[cur][:, 0:d]))
        line(v.tensor_tensor(cum[1 - cur][:, d:e], cum[cur][:, d:e], cum[cur][:, 0:e - d], ALU.add))
        cur, d = 1 - cur, 2 * d
    line(v.tensor_scalar(skip[:, :], nt[:, :], -float(P), float(CAP), ALU.mult, ALU.add))
    line(v.tensor_scalar(end[:, :], K["iota"][:, 0:e], float(CAP), float(CAP), ALU.mult, ALU.add))
    line(v.tensor_tensor(ge[:, :, :], bcast(K["iotan"][0:1, 0:1], [(1, n), (0, e)]),
                         bcast(cum[cur][0:1, 0:1], [(0, n), (1, e)]), ALU.is_ge))
    line(v.tensor_reduce(ef[:, :], ge[:, :, :], AX.X, ALU.add))
    line(v.tensor_scalar(expert, ef[:, :], float(e - 1), None, ALU.min))
    if row is not None:
        line(v.tensor_tensor(ge[:, :, :], ge[:, :, :], bcast(skip[0:1, 0:1], [(0, n), (1, e)]), ALU.mult))
        line(v.tensor_reduce(st[:, :], ge[:, :, :], AX.X, ALU.add))
        line(v.scalar_tensor_tensor(row, K["iotan"][0:1, 0:n], float(P), st[:, :], ALU.mult, ALU.add))
    line(v.tensor_tensor(gp[:, :, :], bcast(pos, [(1, cols), (0, e)]), bcast(end[:, 0:1], [(0, cols), (1, e)]), ALU.is_ge))
    line(v.tensor_tensor(gp[:, :, :], gp[:, :, :], bcast(skip[:, 0:1], [(0, cols), (1, e)]), ALU.mult))
    line(v.tensor_reduce(sp[:, :], gp[:, :, :], AX.X, ALU.add))
    line(v.tensor_tensor(posi, pos, sp[:, :], ALU.subtract))


def phase_setup(nc, S, sb, ps, a, R, K):
    with ExitStack() as mem:
        ids = sb(mem, "ids", [P, NT], i32)
        idf = sb(mem, "idf", [P, NT])
        ge = sb(mem, "ge", [P, E1 + 1, NT])
        oh = sb(mem, "oh", [P, E1, NT], f16)
        tot = sb(mem, "tot", [P, E1, NT])
        inc = [sb(mem, f"inc{i}", [P, E1, NT]) for i in range(2)]
        pos = sb(mem, "pos", [P, E1, NT])
        sel = sb(mem, "sel", [P, E1, NT])
        posf = sb(mem, "posf", [P, NT])
        zero = sb(mem, "zero", [P, (NR * CAP + N2 * P) // P], i32)
        posb = [sb(mem, f"posb{i}", [P, 1], i32) for i in range(NT)]
        toks = [sb(mem, f"toks{i}", [P, 1], i32) for i in range(NT)]
        g4 = sb(mem, "g4", [P, 4])
        pp = ps(mem, "pp", [P, 2, E1 * NT])
        blk = mem.enter_context(nc.Block())

        @blk.sync
        def _(e):
            loads = [("ident", K["ident"]), ("tri", K["tri"]), ("ones", K["ones"]), ("iota", K["iota"]),
                     ("tok", K["tok"]), ("iotan", K["iotan"])]
            for name, t in loads:
                e.dma_start(t[:, :], a["c_" + name]).then_inc(S.sem("su_consts"), 16)
            e.dma_start(ids[:, :], a["ids"]).then_inc(S.sem("su_ids"), 16)
            e.dma_start(g4[:, :], bass.AP(a["gates"].tensor, 0, [[0, P], [1, 4]])).then_inc(S.sem("su_gates"), 16)
            e.wait_ge(S.sem("su_zero"), 1)
            for name in ("list1", "list2"):
                rows = R[name].shape[0]
                e.dma_start(R[name].rearrange("(p c) o -> p (c o)", p=P), zero[:, 0:rows // P])\
                    .then_inc(S.sem("su_list0"), 16)
            e.wait_ge(S.sem("su_list0"), 32)

        @blk.vector
        def _(v):
            line = Line(S, v, "su_dve")
            line.start(It(0, 0))
            line(v.memset(zero[:, :], 0), "su_zero")
            line(v.memset(K["mhalf"][:, :], -0.5))
            line(v.memset(ge[:, 0, :], 1.0))
            line(v.memset(ge[:, E1, :], 0.0))
            v.wait_ge(S.sem("su_consts"), 16 * 6)
            v.wait_ge(S.sem("su_ids"), 16)
            line(v.tensor_copy(idf[:, :], ids[:, :]))
            for i in range(1, E1):
                line(v.tensor_scalar(ge[:, i, :], idf[:, :], float(i * RANGE1), None, ALU.is_ge))
            line(v.tensor_tensor(oh[:, :, :], ge[:, 0:E1, :], ge[:, 1:E1 + 1, :], ALU.subtract), "su_onehot")
            v.wait_ge(S.sem("su_count"), 1)
            line(v.tensor_copy(tot[:, :, :].rearrange("p e t -> p (e t)"), pp[:, 1, :]))
            line(v.tensor_copy(inc[0][:, :, :], tot[:, :, :]))
            cur, d = 0, 1
            while d < NT:
                line(v.tensor_copy(inc[1 - cur][:, :, 0:d], inc[cur][:, :, 0:d]))
                line(v.tensor_tensor(inc[1 - cur][:, :, d:], inc[cur][:, :, d:], inc[cur][:, :, 0:NT - d], ALU.add))
                cur, d = 1 - cur, 2 * d
            line(v.tensor_tensor(pos[:, :, :], inc[cur][:, :, :], tot[:, :, :], ALU.subtract))
            line(v.tensor_tensor(pos[:, :, :].rearrange("p e t -> p (e t)"), pp[:, 0, :],
                                 pos[:, :, :].rearrange("p e t -> p (e t)"), ALU.add))
            for i in range(1, E1):
                line(v.tensor_scalar(pos[:, i, :], pos[:, i, :], float(i * CAP), None, ALU.add))
            line(v.tensor_tensor(sel[:, :, :], pos[:, :, :], oh[:, :, :], ALU.mult))
            line(v.tensor_reduce(posf[:, :], sel[:, :, :].rearrange("p e t -> p t e"), AX.X, ALU.add))
            make_table(line, v, mem, sb, "t1", E1, N1, inc[cur][:, :, NT - 1], K, K["tab1"][0:1, :], None,
                       posf[:, :], K["pos1"][:, :])
            for i in range(NT):
                v.tensor_copy(toks[i][:, :], K["tok"][:, i:i + 1])
                line(v.tensor_copy(posb[i][:, :], K["pos1"][:, i:i + 1]))
            line(v.memset(sel[:, 0, 0:1], 0.0), "su_pos")

        @blk.tensor
        def _(e):
            e.wait_ge(S.sem("su_consts"), 16 * 6)
            e.wait_ge(S.sem("su_onehot"), 1)
            o = oh[:, :, :].rearrange("p e t -> p (e t)")
            e.matmul(pp[:, 0, :], K["tri"][:, :], o, start=True, stop=True)
            e.matmul(pp[:, 1, :], K["ones"][:, :], o, start=True, stop=True).then_inc(S.sem("su_count"), 1)

        @blk.scalar
        def _(e):
            e.wait_ge(S.sem("su_gates"), 16)
            e.activation(K["gate"][:, 0:4], g4[:, :], ACT.Tanh).then_inc(S.sem("su_tanh"), 1)
            e.wait_ge(S.sem("su_tanh"), 1)
            e.activation(K["gate"][:, 4:5], K["gate"][:, 0:1], ACT.Copy, scale=UNSCALE)
            e.activation(K["gate"][:, 5:6], K["gate"][:, 1:2], ACT.Copy, scale=1.0 / SA)
            e.activation(K["gate"][:, 6:7], K["gate"][:, 1:2], ACT.Copy, scale=UNSCALE)

        @blk.gpsimd
        def _(e):
            e.wait_ge(S.sem("su_pos"), 1)
            e.wait_ge(S.sem("su_list0"), 32)
            for i in range(NT):
                e.indirect_dma_start(out=R["list1"], out_offset=bass.IndirectOffsetOnAxis(ap=posb[i][:, :], axis=0),
                                     in_=toks[i][:, :], in_offset=None).then_inc(S.sem("su_scatter"), 16)
            e.wait_ge(S.sem("su_scatter"), 16 * NT)


def load_split(S, sync_, act, dve, jobs, stage, tag):
    def load(e):
        for n, (src, hi, lo, cols) in enumerate(jobs):
            it = It(n // 2, n % 2)
            S.wait(e, tag + "lo", it.back(2))
            S.moved(e.dma_start(stage[it.p][:, 0:cols], src), tag + "w", it)

    def high(e):
        for n, (src, hi, lo, cols) in enumerate(jobs):
            it = It(n // 2, n % 2)
            S.wait_moved(e, tag + "w", it)
            S.done(e.activation(hi, stage[it.p][:, 0:cols], ACT.Copy, scale=SW), tag + "hi")

    def low(e):
        for n, (src, hi, lo, cols) in enumerate(jobs):
            it = It(n // 2, n % 2)
            S.wait(e, tag + "hi", it)
            S.done(e.scalar_tensor_tensor(lo, stage[it.p][:, 0:cols], SW, hi, ALU.mult, ALU.subtract), tag + "lo")
    load(sync_) if sync_ else None
    high(act) if act else None
    low(dve) if dve else None


def norm_parts(line, v, S, T, x, tag, it):
    line(v.bn_stats(T["st"][:, :], x))
    S.static(v)
    line(v.bn_aggr(T["mv"][:, :], T["st"][:, :]))
    line(v.tensor_scalar(T["ve"][:, :], T["mv"][:, 1:2], EPS, None, ALU.add), tag + "var")
    S.wait(v, tag + "rstd", it)
    line(v.tensor_scalar(T["rs"][:, :], T["rstd"][:, :], SA, None, ALU.mult))
    line(v.tensor_scalar(T["xs"][it.p][:, :], x, T["mv"][:, 0:1], T["rs"][:, :], ALU.subtract, ALU.mult), tag + "xs")


def pool_rstd(e, S, T, K, tag, it):
    S.wait(e, tag + "var", it)
    S.done(e.tensor_tensor(T["rstd"][:, :], T["ve"][:, :], K["mhalf"][:, :], ALU.pow), tag + "rstd")


def transposes(e, dst, src, ident, n):
    for j in range(n):
        last = e.transpose(dst[:, j, :], src[:, j * P:(j + 1) * P], ident)
    return last


def phase_layer1(nc, S, sb, ps, a, R, K):
    with ExitStack() as mem:
        ch = sb(mem, "ch", [P, E1 * KD * D], f16)
        cl = sb(mem, "cl", [P, E1 * KD * D], f16)
        stage = [sb(mem, f"l1stage{i}", [P, KD * D]) for i in range(2)]
        idx = [sb(mem, f"l1idx{i}", [P, 1], i32) for i in range(2)]
        x = [sb(mem, f"l1x{i}", [P, D]) for i in range(2)]
        T = {"st": sb(mem, "l1st", [P, 6]), "mv": sb(mem, "l1mv", [P, 2]), "ve": sb(mem, "l1ve", [P, 1]),
             "rstd": sb(mem, "l1rstd", [P, 1]), "rs": sb(mem, "l1rs", [P, 1]),
             "xs": [sb(mem, f"l1xs{i}", [P, D]) for i in range(2)]}
        xhl = [sb(mem, f"l1xhl{i}", [P, 2 * D], f16) for i in range(2)]
        xT = [sb(mem, f"l1xT{i}", [P, 2 * KD, P], f16) for i in range(2)]
        sg = [sb(mem, f"l1sg{i}", [P, KD * P]) for i in range(2)]
        sq = [sb(mem, f"l1sq{i}", [P, KD * P]) for i in range(2)]
        h = [sb(mem, f"l1h{i}", [P, KD * P]) for i in range(2)]
        hh = [sb(mem, f"l1hh{i}", [P, KD * P], f16) for i in range(2)]
        hl = [sb(mem, f"l1hl{i}", [P, KD * P], f16) for i in range(2)]
        y = [sb(mem, f"l1y{i}", [P, D]) for i in range(2)]
        pT = [ps(mem, f"l1pT{i}", [P, 2 * KD, P], f16) for i in range(2)]
        pP = [ps(mem, f"l1pP{i}", [P, KD * P]) for i in range(2)]
        pY = [ps(mem, f"l1pY{i}", [P, D]) for i in range(2)]
        W = KD * D
        jobs = [(a["ctxT"][i], ch[:, i * W:(i + 1) * W], cl[:, i * W:(i + 1) * W], W) for i in range(E1)]
        blk = mem.enter_context(nc.Block())

        @blk.sync
        def _(e):
            load_split(S, e, None, None, jobs, stage, "l1")

            def indices(it):
                S.wait_moved(e, "l1gather", it.back(2))
                S.static(e)
                S.moved(e.dma_start(idx[it.p][:, :], R["list1"][bass.ds(it.n * P, P), :]), "l1idx", it)

            def store(it):
                S.wait(e, "l1y", it)
                S.static(e)
                S.moved(e.dma_start(R["y1s"][bass.ds(it.n * P, P), :], y[it.p][:, :]), "l1store", it)
            pipeline(e, N1, [(indices, 0), (store, 6)])
            for p in range(2):
                S.wait_moved(e, "l1store", It(N1 // 2 - 1, p))

        @blk.gpsimd
        def _(e):
            def gather(it):
                S.wait_moved(e, "l1idx", it)
                S.wait(e, "l1xs", it.back(2))
                S.static(e)
                S.moved(e.indirect_dma_start(
                    out=x[it.p][:, :], out_offset=None, in_=a["x"],
                    in_offset=bass.IndirectOffsetOnAxis(ap=idx[it.p][:, :], axis=0)), "l1gather", it)
            pipeline(e, N1, [(gather, 0), (lambda it: pool_rstd(e, S, T, K, "l1", it), 1)])

        @blk.scalar
        def _(e):
            load_split(S, None, e, None, jobs, stage, "l1")

            def yout(it):
                S.wait(e, "l1mm2", it)
                S.wait_moved(e, "l1store", it.back(2))
                S.done(e.activation(y[it.p][:, :], pY[it.p][:, :], ACT.Copy, scale=UNSCALE), "l1y")

            def high(it):
                S.wait(e, "l1xs", it)
                S.wait(e, "l1T", it.back(2))
                S.done(e.activation(xhl[it.p][:, 0:D], T["xs"][it.p][:, :], ACT.Copy), "l1xh")

            def hidden(it):
                S.wait(e, "l1mm1", it)
                S.wait(e, "l1h", it.back(2))
                S.done(e.activation(sg[it.p][:, :], pP[it.p][:, :], ACT.Sigmoid, scale=UNSCALE), "l1sg")
                S.done(e.activation(sq[it.p][:, :], pP[it.p][:, :], ACT.Square, scale=UNSCALE * SA ** 0.5), "l1sq")
                S.wait(e, "l1h", it)
                S.wait(e, "l1mm2", it.back(2))
                S.done(e.activation(hh[it.p][:, :], h[it.p][:, :], ACT.Copy), "l1hh")
            pipeline(e, N1, [(yout, 5), (high, 1), (hidden, 3)])

        @blk.vector
        def _(v):
            load_split(S, None, None, v, jobs, stage, "l1")
            front, mid, back = (Line(S, v, f"l1dve{i}") for i in range(3))

            def norm(it):
                front.start(it)
                S.wait_moved(v, "l1gather", it)
                norm_parts(front, v, S, T, x[it.p][:, :], "l1", it)
                S.wait(v, "l1xh", it)
                front(v.tensor_tensor(xhl[it.p][:, D:], T["xs"][it.p][:, :], xhl[it.p][:, 0:D], ALU.subtract), "l1xl")

            def evacuate(it):
                mid.start(it)
                S.wait(v, "l1T", it)
                S.wait(v, "l1mm1", it.back(2))
                mid(v.tensor_copy(xT[it.p][:, :, :], pT[it.p][:, :, :]), "l1xT")

            def hidden(it):
                back.start(it)
                S.wait(v, "l1sq", it)
                S.wait(v, "l1hh", it.back(2))
                back(v.tensor_tensor(h[it.p][:, :], sg[it.p][:, :], sq[it.p][:, :], ALU.mult), "l1h")
                S.wait(v, "l1hh", it)
                back(v.tensor_tensor(hl[it.p][:, :], h[it.p][:, :], hh[it.p][:, :], ALU.subtract), "l1hl")
            pipeline(v, N1, [(norm, 1), (evacuate, 2), (hidden, 3)])

        @blk.tensor
        def _(e):
            S.wait(e, "l1lo", It(E1 // 2 - 1, 1))

            def up(it):
                ex = e.value_load(K["tab1"][0:1, bass.ds(it.n, 1)], min_val=0, max_val=E1 - 1)
                S.wait(e, "l1xT", it)
                S.wait(e, "l1sq", it.back(2))
                for f in range(KD):
                    terms = [(w, x0, k) for k in range(KD) for w, x0 in ((ch, 0), (ch, KD), (cl, 0))]
                    for j, (w, x0, k) in enumerate(terms):
                        last = e.matmul(pP[it.p][:, f * P:(f + 1) * P], w[:, bass.ds(ex * W + (k * D + f * P), P)],
                                        xT[it.p][:, x0 + k, :], start=j == 0, stop=j == len(terms) - 1)
                S.done(last, "l1mm1")

            def turn(it):
                S.wait(e, "l1xl", it)
                S.wait(e, "l1xT", it.back(2))
                S.done(transposes(e, pT[it.p], xhl[it.p], K["ident"][:, :], 2 * KD), "l1T")

            def down(it):
                ex = e.value_load(K["tab1"][0:1, bass.ds(it.n, 1)], min_val=0, max_val=E1 - 1)
                S.wait(e, "l1hl", it)
                S.wait(e, "l1y", it.back(2))
                terms = [(hx, w, k) for k in range(KD) for hx, w in ((hh, ch), (hh, cl), (hl, ch))]
                for j, (hx, w, k) in enumerate(terms):
                    last = e.matmul(pY[it.p][:, :], hx[it.p][:, k * P:(k + 1) * P], w[:, bass.ds(ex * W + k * D, D)],
                                    start=j == 0, stop=j == len(terms) - 1)
                S.done(last, "l1mm2")
            pipeline(e, N1, [(up, 3), (turn, 2), (down, 4)])


def split_terms(first, second, blocks):
    return [(x, w, k) for k in range(blocks) for x, w in ((first[0], second[0]), (first[0], second[1]), (first[1], second[0]))]


def phase_shared(nc, S, sb, ps, a, R, K):
    W1, W2 = KD * FF, FB * D
    with ExitStack() as mem:
        w1 = [sb(mem, f"shw1{i}", [P, NS * W1], f16) for i in range(2)]
        w2 = [sb(mem, f"shw2{i}", [P, NS * W2], f16) for i in range(2)]
        cen = [sb(mem, f"shcen{i}", [P, KD * NR], f16) for i in range(2)]
        stage = [sb(mem, f"shstage{i}", [P, W2]) for i in range(2)]
        b1r = sb(mem, "shb1r", [P, NS * FB])
        b1 = sb(mem, "shb1", [P, NS * FB])
        bias = sb(mem, "shbias", [P, NR])
        base = sb(mem, "shbase", [P, NR])
        pidx = [sb(mem, f"shpidx{i}", [P, 1], i32) for i in range(2)]
        tokb = [sb(mem, f"shtok{i}", [P, 1], i32) for i in range(2)]
        posb = [sb(mem, f"shposb{i}", [P, KR], i32) for i in range(2)]
        xin = [sb(mem, f"shxin{i}", [P, D]) for i in range(2)]
        y1 = [sb(mem, f"shy1{i}", [P, D]) for i in range(2)]
        x1 = sb(mem, "shx1", [P, D])
        r1 = sb(mem, "shr1", [P, NT * D])
        T = {"st": sb(mem, "shst", [P, 6]), "mv": sb(mem, "shmv", [P, 2]), "ve": sb(mem, "shve", [P, 1]),
             "rstd": sb(mem, "shrstd", [P, 1]), "rs": sb(mem, "shrs", [P, 1]),
             "xs": [sb(mem, f"shxs{i}", [P, D]) for i in range(2)]}
        xhl = [sb(mem, f"shxhl{i}", [P, 2 * D], f16) for i in range(2)]
        xT = [sb(mem, f"shxT{i}", [P, 2 * KD, P], f16) for i in range(2)]
        h = [sb(mem, f"shh{i}", [P, NS, FB * P]) for i in range(2)]
        hh = [sb(mem, f"shhh{i}", [P, NS, FB * P], f16) for i in range(2)]
        hl = [sb(mem, f"shhl{i}", [P, NS, FB * P], f16) for i in range(2)]
        xo = [sb(mem, f"shxo{i}", [P, D]) for i in range(2)]
        sig = [sb(mem, f"shsig{i}", [P, NR]) for i in range(2)]
        sc = sb(mem, "shsc", [P, NR])
        top = sb(mem, "shtop", [P, 8])
        ti = sb(mem, "shti", [P, 8], u32)
        tf = sb(mem, "shtf", [P, 8])
        oh = [sb(mem, f"shoh{i}", [P, KR, NR]) for i in range(2)]
        m = [sb(mem, f"shm{i}", [P, NR], f16) for i in range(2)]
        pos = sb(mem, "shpos", [P, NR])
        pk = sb(mem, "shpk", [P, KR, NR])
        pf = sb(mem, "shpf", [P, KR])
        pos2f = sb(mem, "shpos2f", [P, NT * KR])
        gs = sb(mem, "shgs", [P, 1])
        gr = sb(mem, "shgr", [P, 1])
        pT = [ps(mem, f"shpT{i}", [P, 2 * KD, P], f16) for i in range(2)]
        pH = [ps(mem, f"shpH{i}", [P, FB * P]) for i in range(NS)]
        pY = [ps(mem, f"shpY{i}", [P, D]) for i in range(2)]
        pR = ps(mem, "shpR", [P, NR])
        pC = ps(mem, "shpC", [P, 2, NR])
        jobs = [(a["sw1"][i], w1[0][:, i * W1:(i + 1) * W1], w1[1][:, i * W1:(i + 1) * W1], W1) for i in range(NS)]
        jobs += [(a["sw2"][i], w2[0][:, i * W2:(i + 1) * W2], w2[1][:, i * W2:(i + 1) * W2], W2) for i in range(NS)]
        jobs += [(a["cenT"], cen[0][:, :], cen[1][:, :], KD * NR)]
        blk = mem.enter_context(nc.Block())

        @blk.sync
        def _(e):
            load_split(S, e, None, None, jobs, stage, "sh")
            e.dma_start(b1r[:, :], a["sb1"]).then_inc(S.sem("sh_small"), 16)
            e.dma_start(bias[:, :], bass.AP(a["bias"].tensor, 0, [[0, P], [1, NR]])).then_inc(S.sem("sh_small"), 16)

            def load(it):
                S.wait(e, "shr1", it.back(2))
                S.static(e)
                S.moved(e.dma_start(xin[it.p][:, :], a["x"][bass.ds(it.n * P, P), :]), "shxin", it)

            def store_norm(it):
                S.wait(e, "shxl", it)
                S.static(e)
                S.moved(e.dma_start(R["xn2"][bass.ds(it.n * P, P), :], xhl[it.p][:, :]), "shxnout", it)

            def store(it):
                S.wait(e, "shxo", it)
                S.static(e)
                S.moved(e.dma_start(R["x2a"][bass.ds(it.n * P, P), :], xo[it.p][:, :]), "shstore", it)
            pipeline(e, NT, [(load, 0), (store_norm, 1), (store, 5)])
            for p in range(2):
                S.wait_moved(e, "shstore", It(NT // 2 - 1, p))
                S.wait_moved(e, "shxnout", It(NT // 2 - 1, p))

        @blk.gpsimd
        def _(e):
            def gather(it):
                S.wait_moved(e, "shgather", it.back(2))
                S.static(e)
                S.done(e.tensor_copy(pidx[it.p][:, :], K["pos1"][:, bass.ds(it.n, 1)]), "shpidx")
                S.wait(e, "shpidx", it)
                S.wait(e, "shr1", it.back(2))
                S.static(e)
                S.moved(e.indirect_dma_start(
                    out=y1[it.p][:, :], out_offset=None, in_=R["y1s"],
                    in_offset=bass.IndirectOffsetOnAxis(ap=pidx[it.p][:, :], axis=0)), "shgather", it)

            def scatter(it):
                S.wait_moved(e, "shscatter", it.back(2), KR)
                S.static(e)
                S.done(e.tensor_copy(tokb[it.p][:, :], K["tok"][:, bass.ds(it.n, 1)]), "shtokb")
                S.wait(e, "shtokb", it)
                S.wait(e, "shposb", it)
                S.static(e)
                for k in range(KR):
                    S.moved(e.indirect_dma_start(
                        out=R["list2"], out_offset=bass.IndirectOffsetOnAxis(ap=posb[it.p][:, k:k + 1], axis=0),
                        in_=tokb[it.p][:, :], in_offset=None), "shscatter", it)
            pipeline(e, NT, [(gather, 0), (lambda it: pool_rstd(e, S, T, K, "sh", it), 1), (scatter, 4)])
            for p in range(2):
                S.wait_moved(e, "shscatter", It(NT // 2 - 1, p), KR)

        @blk.scalar
        def _(e):
            load_split(S, None, e, None, jobs, stage, "sh")
            e.wait_ge(S.sem("sh_small"), 32)
            S.done(e.activation(b1[:, :], b1r[:, :], ACT.Copy, scale=SA), "sh_b1")
            e.wait_ge(S.sem("sh_b1"), 1)
            e.wait_ge(S.sem("sh_init"), 1)

            def high(it):
                S.wait(e, "shxs", it)
                S.wait(e, "shT", it.back(2))
                S.wait_moved(e, "shxnout", it.back(2))
                S.done(e.activation(xhl[it.p][:, 0:D], T["xs"][it.p][:, :], ACT.Copy), "shxh")

            def hidden(it):
                S.wait(e, "shrouted", it)
                S.done(e.activation(sig[it.p][:, :], pR[:, :], ACT.Sigmoid, scale=UNSCALE), "shsig")
                S.wait(e, "shup", it)
                S.wait(e, "shhl", it.back(2))
                for s in range(NS):
                    for f in range(FB):
                        n = FLAST if f == FB - 1 else P
                        last = e.activation(h[it.p][0:n, s, f * P:(f + 1) * P], pH[s][0:n, f * P:(f + 1) * P],
                                            ACT.Relu, bias=b1[0:n, s * FB + f:s * FB + f + 1], scale=UNSCALE * SA)
                S.done(last, "shh")
                S.wait(e, "shh", it)
                S.wait(e, "shdown", it.back(2))
                S.done(e.activation(hh[it.p][:, :, :], h[it.p][:, :, :], ACT.Copy), "shhh")
            pipeline(e, NT, [(high, 1), (hidden, 3)])

        @blk.vector
        def _(v):
            init = Line(S, v, "shinit")
            init.start(It(0, 0))
            for i in range(2):
                init(v.memset(h[i][FLAST:P, :, :], 0.0))
                init(v.memset(h[i][FLAST:FLAST + 1, :, 2 * P:], SA))
            init(v.tensor_scalar(base[:, :], K["iota"][:, :], float(CAP), None, ALU.mult))
            init(v.memset(sc[:, :], 0.0), "sh_init")
            load_split(S, None, None, v, jobs, stage, "sh")
            v.wait_ge(S.sem("sh_small"), 32)
            front, mid, rt, back, last_, fin = (Line(S, v, f"shdve{i}") for i in range(6))

            def norm(it):
                front.start(it)
                S.wait_moved(v, "shgather", it)
                S.wait_moved(v, "shxin", it)
                front(v.scalar_tensor_tensor(x1[:, :], y1[it.p][:, :], K["gate"][:, 0:1], xin[it.p][:, :],
                                             ALU.mult, ALU.add))
                norm_parts(front, v, S, T, x1[:, :], "sh", it)
                front(v.scalar_tensor_tensor(r1[:, bass.ds(it.n * D, D)], T["xs"][it.p][:, :], K["gate"][:, 5:6],
                                             x1[:, :], ALU.mult, ALU.add), "shr1")
                S.wait(v, "shxh", it)
                front(v.tensor_tensor(xhl[it.p][:, D:], T["xs"][it.p][:, :], xhl[it.p][:, 0:D], ALU.subtract), "shxl")

            def evacuate(it):
                mid.start(it)
                S.wait(v, "shT", it)
                S.wait(v, "shup", it.back(2))
                mid(v.tensor_copy(xT[it.p][:, :, :], pT[it.p][:, :, :]), "shxT")

            def choose(it):
                rt.start(it)
                S.wait(v, "shsig", it)
                rt(v.tensor_tensor(sc[:, :], sig[it.p][:, :], bias[:, :], ALU.add))
                S.static(v)
                rt(v.max(top[:, :], sc[:, :]))
                S.static(v)
                rt(v.max_index(ti[:, :], top[:, :], sc[:, :]))
                rt(v.tensor_copy(tf[:, :], ti[:, :]))
                rt(v.tensor_tensor(oh[it.p][:, :, :], bcast(K["iota"][:, 0:1], [(0, KR), (1, NR)]),
                                   bcast(tf[:, 0:1], [(1, KR), (0, NR)]), ALU.is_equal))
                with nc.allow_low_precision(reason="sums of at most one one"):
                    rt(v.tensor_reduce(m[it.p][:, :], oh[it.p][:, :, :].rearrange("p k e -> p e k"), AX.X, ALU.add), "shm")
                rt(v.tensor_reduce(gs[:, :], top[:, 0:KR], AX.X, ALU.add))
                rt(v.tensor_scalar(gs[:, :], gs[:, :], 1e-8, None, ALU.max))
                rt(v.reciprocal(gr[:, :], gs[:, :]))
                rt(v.tensor_scalar(K["g2f"][:, bass.ds(it.n * KR, KR)], top[:, 0:KR],
                                   gr[:, :], K["gate"][:, 1:2], ALU.mult, ALU.mult))

            def place(it):
                last_.start(it)
                S.wait(v, "shcount", it)
                last_(v.tensor_tensor(pos[:, :], pC[:, 0, :], base[:, :], ALU.add))
                last_(v.tensor_tensor(base[:, :], pC[:, 1, :], base[:, :], ALU.add), "shbase")
                last_(v.tensor_tensor(pk[:, :, :], oh[it.p][:, :, :], bcast(pos[:, 0:1], [(0, KR), (1, NR)]), ALU.mult))
                last_(v.tensor_reduce(pf[:, :], pk[:, :, :], AX.X, ALU.add))
                last_(v.tensor_copy(pos2f[:, bass.ds(it.n * KR, KR)], pf[:, :]))
                S.wait_moved(v, "shscatter", it.back(2), KR)
                last_(v.tensor_copy(posb[it.p][:, :], pf[:, :]), "shposb")

            def hidden(it):
                back.start(it)
                S.wait(v, "shhh", it)
                S.wait(v, "shdown", it.back(2))
                back(v.tensor_tensor(hl[it.p][:, :, :], h[it.p][:, :, :], hh[it.p][:, :, :], ALU.subtract), "shhl")

            def finish(it):
                fin.start(it)
                S.wait(v, "shdown", it)
                S.wait_moved(v, "shstore", it.back(2))
                fin(v.tensor_scalar(xo[it.p][:, :], pY[it.p][:, :], K["gate"][:, 6:7], None, ALU.mult))
                fin(v.tensor_tensor(xo[it.p][:, :], xo[it.p][:, :], r1[:, bass.ds(it.n * D, D)], ALU.add), "shxo")
            pipeline(v, NT, [(finish, 5), (norm, 1), (choose, 3), (evacuate, 2), (hidden, 3), (place, 3)])
            v.wait_ge(S.sem("shbase"), NT)
            tail = Line(S, v, "shtail")
            tail.start(It(0, 0))
            cnt = sb(mem, "shcnt", [P, NR])
            tail(v.scalar_tensor_tensor(cnt[:, :], K["iota"][:, :], -float(CAP), base[:, :], ALU.mult, ALU.add))
            make_table(tail, v, mem, sb, "t2", NR, N2, cnt[:, :], K, K["tab2"][0:1, 0, :], K["tab2"][0:1, 1, :],
                       pos2f[:, :], K["pos2"][:, :])

        @blk.tensor
        def _(e):
            e.wait_ge(S.sem("shlo"), len(jobs))

            def up(it):
                S.wait(e, "shxT", it)
                S.wait(e, "shsig", it.back(1))
                xs = (xT[it.p][:, 0:KD, :], xT[it.p][:, KD:, :])
                terms = split_terms(xs, cen, KD)
                for j, (x, w, k) in enumerate(terms):
                    last = e.matmul(pR[:, :], x[:, k, :], w[:, k * NR:(k + 1) * NR], start=j == 0, stop=j == len(terms) - 1)
                S.done(last, "shrouted")
                S.wait(e, "shh", it.back(1))
                for s in range(NS):
                    for f in range(FB):
                        n = FLAST if f == FB - 1 else P
                        terms = split_terms(w1, xs, KD)
                        for j, (w, x, k) in enumerate(terms):
                            o = s * W1 + k * FF + f * P
                            last = e.matmul(pH[s][0:n, f * P:(f + 1) * P], w[:, o:o + n], x[:, k, :],
                                            start=j == 0, stop=j == len(terms) - 1)
                S.done(last, "shup")

            def turn(it):
                S.wait(e, "shxl", it)
                S.wait(e, "shxT", it.back(2))
                S.done(transposes(e, pT[it.p], xhl[it.p], K["ident"][:, :], 2 * KD), "shT")

            def down(it):
                S.wait(e, "shhl", it)
                S.wait(e, "shxo", it.back(2))
                terms = [(x, w, k, s) for s in range(NS) for x, w, k in split_terms((hh[it.p], hl[it.p]), w2, FB)]
                for j, (x, w, k, s) in enumerate(terms):
                    n = FLAST + 1 if k == FB - 1 else P
                    last = e.matmul(pY[it.p][:, :], x[0:n, s, k * P:(k + 1) * P], w[0:n, s * W2 + k * D:s * W2 + (k + 1) * D],
                                    start=j == 0, stop=j == len(terms) - 1)
                S.done(last, "shdown")

            def count(it):
                S.wait(e, "shm", it)
                S.wait(e, "shbase", it.back(1))
                e.matmul(pC[:, 0, :], K["tri"][:, :], m[it.p][:, :], start=True, stop=True)
                S.done(e.matmul(pC[:, 1, :], K["ones"][:, :], m[it.p][:, :], start=True, stop=True), "shcount")
            pipeline(e, NT, [(up, 3), (turn, 2), (count, 3), (down, 4)])


def phase_routed(nc, S, sb, ps, a, R, K):
    W1, W2 = KD * FF, FB * D
    with ExitStack() as mem:
        w1 = [sb(mem, f"row1{i}", [P, NR * W1], f16) for i in range(2)]
        w2 = [sb(mem, f"row2{i}", [P, NR * W2], f16) for i in range(2)]
        b1 = sb(mem, "rob1", [P, NR * FB])
        last_row = R["list2"].shape[0] - P
        with ExitStack() as mem2:
            stage = [sb(mem2, f"rostage{i}", [P, W2]) for i in range(2)]
            b1r = sb(mem2, "rob1r", [P, NR * FB])
            jobs = [(a["rw1"][i], w1[0][:, i * W1:(i + 1) * W1], w1[1][:, i * W1:(i + 1) * W1], W1) for i in range(NR)]
            jobs += [(a["rw2"][i], w2[0][:, i * W2:(i + 1) * W2], w2[1][:, i * W2:(i + 1) * W2], W2) for i in range(NR)]
            blk = mem2.enter_context(nc.Block())

            @blk.sync
            def _(e):
                e.dma_start(b1r[:, :], a["rb1"]).then_inc(S.sem("ro_b1r"), 16)
                load_split(S, e, None, None, jobs, stage, "ro")

            @blk.scalar
            def _(e):
                load_split(S, None, e, None, jobs, stage, "ro")
                e.wait_ge(S.sem("ro_b1r"), 16)
                e.activation(b1[:, :], b1r[:, :], ACT.Copy, scale=SA)

            @blk.vector
            def _(v):
                load_split(S, None, None, v, jobs, stage, "ro")
        idx = [sb(mem, f"roidx{i}", [P, 1], i32) for i in range(2)]
        xg = [sb(mem, f"roxg{i}", [P, 2 * D], f16) for i in range(2)]
        xT = [sb(mem, f"roxT{i}", [P, 2 * KD, P], f16) for i in range(2)]
        h = [sb(mem, f"roh{i}", [P, FB * P]) for i in range(2)]
        hh = [sb(mem, f"rohh{i}", [P, FB * P], f16) for i in range(2)]
        hl = [sb(mem, f"rohl{i}", [P, FB * P], f16) for i in range(2)]
        y = [sb(mem, f"roy{i}", [P, D]) for i in range(2)]
        pT = [ps(mem, f"ropT{i}", [P, 2 * KD, P], f16) for i in range(2)]
        pH = [ps(mem, f"ropH{i}", [P, FB * P]) for i in range(2)]
        pY = [ps(mem, f"ropY{i}", [P, D]) for i in range(2)]
        blk = mem.enter_context(nc.Block())

        @blk.sync
        def _(e):
            def indices(it):
                row = e.value_load(K["tab2"][0:1, 1, bass.ds(it.n, 1)], min_val=0, max_val=last_row)
                S.wait_moved(e, "rogather", it.back(2))
                S.static(e)
                S.moved(e.dma_start(idx[it.p][:, :], R["list2"][bass.ds(row, P), :]), "roidx", it)

            def store(it):
                S.wait(e, "roy", it)
                S.static(e)
                S.moved(e.dma_start(R["ys"][bass.ds(it.n * P, P), :], y[it.p][:, :]), "rostore", it)
            pipeline(e, N2, [(indices, 0), (store, 5)])
            for p in range(2):
                S.wait_moved(e, "rostore", It(N2 // 2 - 1, p))

        @blk.gpsimd
        def _(e):
            def gather(it):
                S.wait_moved(e, "roidx", it)
                S.wait(e, "roT", it.back(2))
                S.static(e)
                S.moved(e.indirect_dma_start(
                    out=xg[it.p][:, :], out_offset=None, in_=R["xn2"],
                    in_offset=bass.IndirectOffsetOnAxis(ap=idx[it.p][:, :], axis=0)), "rogather", it)
            pipeline(e, N2, [(gather, 0)])

        @blk.scalar
        def _(e):
            e.wait_ge(S.sem("ro_init"), 1)

            def yout(it):
                S.wait(e, "rodown", it)
                S.wait_moved(e, "rostore", it.back(2))
                S.done(e.activation(y[it.p][:, :], pY[it.p][:, :], ACT.Copy, scale=UNSCALE), "roy")

            def hidden(it):
                ex = e.value_load(K["tab2"][0:1, 0, bass.ds(it.n, 1)], min_val=0, max_val=NR - 1)
                S.wait(e, "roup", it)
                S.wait(e, "rohl", it.back(2))
                S.static(e)
                for f in range(FB):
                    n = FLAST if f == FB - 1 else P
                    last = e.activation(h[it.p][0:n, f * P:(f + 1) * P], pH[it.p][0:n, f * P:(f + 1) * P],
                                        ACT.Relu, bias=b1[0:n, bass.ds(ex * FB + f, 1)], scale=UNSCALE * SA)
                S.done(last, "roh")
                S.wait(e, "roh", it)
                S.wait(e, "rodown", it.back(2))
                S.done(e.activation(hh[it.p][:, :], h[it.p][:, :], ACT.Copy), "rohh")
            pipeline(e, N2, [(yout, 5), (hidden, 3)])

        @blk.vector
        def _(v):
            init = Line(S, v, "roinit")
            init.start(It(0, 0))
            for i in range(2):
                init(v.memset(h[i][FLAST:P, :], 0.0))
                init(v.memset(h[i][FLAST:FLAST + 1, 2 * P:], SA), "ro_init" if i else None)
            mid, back = (Line(S, v, f"rodve{i}") for i in range(2))

            def evacuate(it):
                mid.start(it)
                S.wait(v, "roT", it)
                S.wait(v, "roup", it.back(2))
                mid(v.tensor_copy(xT[it.p][:, :, :], pT[it.p][:, :, :]), "roxT")

            def hidden(it):
                back.start(it)
                S.wait(v, "rohh", it)
                back(v.tensor_tensor(hl[it.p][:, :], h[it.p][:, :], hh[it.p][:, :], ALU.subtract), "rohl")
            pipeline(v, N2, [(evacuate, 2), (hidden, 3)])

        @blk.tensor
        def _(e):
            def up(it):
                ex = e.value_load(K["tab2"][0:1, 0, bass.ds(it.n, 1)], min_val=0, max_val=NR - 1)
                S.wait(e, "roxT", it)
                S.wait(e, "roh", it.back(2))
                xs = (xT[it.p][:, 0:KD, :], xT[it.p][:, KD:, :])
                for f in range(FB):
                    n = FLAST if f == FB - 1 else P
                    terms = split_terms(w1, xs, KD)
                    for j, (w, x, k) in enumerate(terms):
                        last = e.matmul(pH[it.p][0:n, f * P:(f + 1) * P], w[:, bass.ds(ex * W1 + (k * FF + f * P), n)],
                                        x[:, k, :], start=j == 0, stop=j == len(terms) - 1)
                S.done(last, "roup")

            def turn(it):
                S.wait_moved(e, "rogather", it)
                S.wait(e, "roxT", it.back(2))
                S.done(transposes(e, pT[it.p], xg[it.p], K["ident"][:, :], 2 * KD), "roT")

            def down(it):
                ex = e.value_load(K["tab2"][0:1, 0, bass.ds(it.n, 1)], min_val=0, max_val=NR - 1)
                S.wait(e, "rohl", it)
                S.wait(e, "roy", it.back(2))
                terms = split_terms((hh[it.p], hl[it.p]), w2, FB)
                for j, (x, w, k) in enumerate(terms):
                    n = FLAST + 1 if k == FB - 1 else P
                    last = e.matmul(pY[it.p][:, :], x[0:n, k * P:(k + 1) * P], w[0:n, bass.ds(ex * W2 + k * D, D)],
                                    start=j == 0, stop=j == len(terms) - 1)
                S.done(last, "rodown")
            pipeline(e, N2, [(up, 3), (turn, 2), (down, 4)])


def head_norm(line, v, S, tag, it, p_raw, sq, ss, rr, out, scale):
    S.wait(v, tag + "sq", it)
    line(v.tensor_reduce(ss, sq.rearrange("p (h d) -> p h d", d=HD), AX.X, ALU.add))
    line(v.tensor_scalar(ss, ss, 1.0 / HD, EPS_RMS, ALU.mult, ALU.add), tag + "ms")
    S.wait(v, tag + "rt", it)
    line(v.reciprocal(rr, ss))
    line(v.tensor_scalar(rr, rr, scale, None, ALU.mult))
    line(v.tensor_tensor(out.rearrange("p (h d) -> p h d", d=HD), p_raw.rearrange("p (h d) -> p h d", d=HD),
                         bcast(rr, [(1, NH), (0, HD)]), ALU.mult), tag + "n")


def part_pair(ap, first, step):
    return bass.AP(ap.tensor, ap.offset + first * HD, [list(ap.ap[0]), [4 * HD, NH], [step * HD, 2], [1, HD]])


def twice(ap):
    return bcast(ap, [(HD, NH), (0, 2), (1, HD)])


def phase_keys(nc, S, sb, ps, a, R, K):
    W = KD * D
    with ExitStack() as mem:
        c = [sb(mem, f"kyc{i}", [P, BATCH * W], f16) for i in range(2)]
        wk = [sb(mem, f"kywk{i}", [P, W], f16) for i in range(2)]
        wv = [sb(mem, f"kywv{i}", [P, W], f16) for i in range(2)]
        stage = [sb(mem, f"kystage{i}", [P, W]) for i in range(2)]
        sq = sb(mem, "kysq", [P, D])
        ss = sb(mem, "kyss", [P, NH])
        rr = sb(mem, "kyrr", [P, NH])
        kn = [sb(mem, f"kykn{i}", [P, D]) for i in range(2)]
        kp = [sb(mem, f"kykp{i}", [P, 4 * D], f16) for i in range(2)]
        kt = [sb(mem, f"kykt{i}", [P, 4 * D], f16) for i in range(2)]
        vt = [sb(mem, f"kyvt{i}", [P, NH * (HD + 1)]) for i in range(2)]
        pK = [ps(mem, f"kypK{i}", [P, D]) for i in range(2)]
        pV = [ps(mem, f"kypV{i}", [P, D]) for i in range(2)]
        pT = ps(mem, "kypT", [P, NH // 2, P], f16)
        jobs = [(a["wkT"], wk[0][:, :], wk[1][:, :], W), (a["wvT"], wv[0][:, :], wv[1][:, :], W)]
        jobs += [(a["ctxT"][i], c[0][:, i * W:(i + 1) * W], c[1][:, i * W:(i + 1) * W], W) for i in range(BATCH)]
        blk = mem.enter_context(nc.Block())

        @blk.sync
        def _(e):
            load_split(S, e, None, None, jobs, stage, "kyw")

            def store(it):
                S.wait(e, "kyvt", it)
                S.static(e)
                S.moved(e.dma_start(R["vst"][bass.ds(it.n, 1)].rearrange("a p c -> (a p) c"), vt[it.p][:, :]), "kyvout", it)
                S.wait(e, "kykt", it)
                S.static(e)
                S.moved(e.dma_start(R["kst"][bass.ds(it.n, 1)].rearrange("a p c -> (a p) c"), kt[it.p][:, :]), "kykout", it)
            pipeline(e, NT, [(store, 0)])
            for p in range(2):
                S.wait_moved(e, "kyvout", It(NT // 2 - 1, p))
                S.wait_moved(e, "kykout", It(NT // 2 - 1, p))

        @blk.scalar
        def _(e):
            load_split(S, None, e, None, jobs, stage, "kyw")
            e.wait_ge(S.sem("ky_init"), 1)

            def values(it):
                S.wait(e, "kyproj", it)
                S.wait(e, "kyms", it.back(1))
                S.done(e.activation(sq[:, :], pK[it.p][:, :], ACT.Square, scale=1.0 / SW ** 2), "kysq")
                S.wait_moved(e, "kyvout", it.back(2))
                S.done(e.activation(vt[it.p][:, :].rearrange("p (h d) -> p h d", d=HD + 1)[:, :, 0:HD],
                                    pV[it.p][:, :].rearrange("p (h d) -> p h d", d=HD), ACT.Copy, scale=1.0 / SW ** 2), "kyvt")
                S.wait(e, "kyms", it)
                S.done(e.activation(ss[:, :], ss[:, :], ACT.Sqrt), "kyrt")
                S.wait(e, "kyn", it)
                S.wait(e, "kyT", it.back(2))
                S.done(e.activation(part_pair(kp[it.p][:, :], 0, 2), twice(kn[it.p][:, :]), ACT.Copy), "kyhi")
            pipeline(e, NT, [(values, 0)])

        @blk.vector
        def _(v):
            init = Line(S, v, "kyinit")
            init.start(It(0, 0))
            init(v.memset(vt[0][:, :], 1.0))
            init(v.memset(vt[1][:, :], 1.0), "ky_init")
            load_split(S, None, None, v, jobs, stage, "kyw")
            front, back = Line(S, v, "kydve0"), Line(S, v, "kydve1")

            def norm(it):
                front.start(it)
                S.wait(v, "kyhi", it.back(2))
                head_norm(front, v, S, "ky", it, pK[it.p][:, :], sq[:, :], ss[:, :], rr[:, :], kn[it.p][:, :], SA / SW ** 2)
                S.wait(v, "kyhi", it)
                front(v.tensor_tensor(part_pair(kp[it.p][:, :], 1, 2), twice(kn[it.p][:, :]),
                                      bcast(kp[it.p][:, :], [(4 * HD, NH), (0, 2), (1, HD)]), ALU.subtract), "kylo")

            def evacuate(it):
                back.start(it)
                S.wait(v, "kyT", it)
                S.wait_moved(v, "kykout", it.back(2))
                back(v.tensor_copy(kt[it.p][:, :], pT[:, :, :].rearrange("p j n -> p (j n)")), "kykt")
            pipeline(v, NT, [(evacuate, 1), (norm, 0)])

        @blk.tensor
        def _(e):
            e.wait_ge(S.sem("kywlo"), len(jobs))

            def project(it):
                S.wait(e, "kyn", it.back(2))
                S.wait(e, "kyvt", it.back(2))
                at = (it.n // 4) * W + (it.n % 4) * P
                for out, w in ((pK, wk), (pV, wv)):
                    terms = split_terms(c, w, KD)
                    for j, (x, y, k) in enumerate(terms):
                        last = e.matmul(out[it.p][:, :], x[:, bass.ds(at + k * D, P)], y[:, k * D:(k + 1) * D],
                                        start=j == 0, stop=j == len(terms) - 1)
                S.done(last, "kyproj")

            def turn(it):
                S.wait(e, "kylo", it)
                S.wait(e, "kykt", it.back(1))
                S.done(transposes(e, pT, kp[it.p], K["ident"][:, :], NH // 2), "kyT")
            pipeline(e, NT, [(project, 0), (turn, 1)])


def phase_queries(nc, S, sb, ps, a, R, K):
    W = KD * D
    with ExitStack() as mem:
        wq = [sb(mem, f"quw{i}", [P, W], f16) for i in range(2)]
        stage = [sb(mem, f"qustage{i}", [P, W]) for i in range(2)]
        pidx = [sb(mem, f"qupidx{i}", [P, KR], i32) for i in range(2)]
        xin = [sb(mem, f"quxin{i}", [P, D]) for i in range(2)]
        yg = [sb(mem, f"quyg{i}", [P, KR, D]) for i in range(2)]
        x2 = [sb(mem, f"qux2{i}", [P, D]) for i in range(2)]
        T = {"st": sb(mem, "qust", [P, 6]), "mv": sb(mem, "qumv", [P, 2]), "ve": sb(mem, "quve", [P, 1]),
             "rstd": sb(mem, "qurstd", [P, 1]), "rs": sb(mem, "qurs", [P, 1]),
             "xs": [sb(mem, f"quxs{i}", [P, D]) for i in range(2)]}
        xhl = [sb(mem, f"quxhl{i}", [P, 2 * D], f16) for i in range(2)]
        xT = [sb(mem, f"quxT{i}", [P, 2 * KD, P], f16) for i in range(2)]
        sq = sb(mem, "qusq", [P, D])
        ss = sb(mem, "quss", [P, NH])
        rr = sb(mem, "qurr", [P, NH])
        qn = [sb(mem, f"quqn{i}", [P, D]) for i in range(2)]
        qp = [sb(mem, f"quqp{i}", [P, 4 * D], f16) for i in range(2)]
        qt = [sb(mem, f"quqt{i}", [P, 4 * D], f16) for i in range(2)]
        pT = [ps(mem, f"qupT{i}", [P, 2 * KD, P], f16) for i in range(2)]
        pQ = [ps(mem, f"qupQ{i}", [P, D]) for i in range(2)]
        pS = [ps(mem, f"qupS{i}", [P, NH // 2, P], f16) for i in range(2)]
        jobs = [(a["wqT"], wq[0][:, :], wq[1][:, :], W)]
        blk = mem.enter_context(nc.Block())

        @blk.sync
        def _(e):
            load_split(S, e, None, None, jobs, stage, "qw")

            def load(it):
                S.wait(e, "qux2", it.back(2))
                S.static(e)
                S.moved(e.dma_start(xin[it.p][:, :], R["x2a"][bass.ds(it.n * P, P), :]), "quxin", it)

            def store_x(it):
                S.wait(e, "qux2", it)
                S.static(e)
                S.moved(e.dma_start(R["x2"][bass.ds(it.n * P, P), :], x2[it.p][:, :]), "quxout", it)

            def store(it):
                S.wait(e, "quqt", it)
                S.static(e)
                S.moved(e.dma_start(R["qst"][bass.ds(it.n, 1)].rearrange("a p c -> (a p) c"), qt[it.p][:, :]), "ququt", it)
            pipeline(e, NT, [(load, 0), (store_x, 1), (store, 4)])
            for p in range(2):
                S.wait_moved(e, "quxout", It(NT // 2 - 1, p))
                S.wait_moved(e, "ququt", It(NT // 2 - 1, p))

        @blk.gpsimd
        def _(e):
            def gather(it):
                S.wait_moved(e, "qugather", it.back(2), KR)
                S.static(e)
                S.done(e.tensor_copy(pidx[it.p][:, :], K["pos2"][:, bass.ds(it.n * KR, KR)]), "qupidx")
                S.wait(e, "qupidx", it)
                S.wait(e, "qux2", it.back(2))
                S.static(e)
                for k in range(KR):
                    S.moved(e.indirect_dma_start(
                        out=yg[it.p][:, k, :], out_offset=None, in_=R["ys"],
                        in_offset=bass.IndirectOffsetOnAxis(ap=pidx[it.p][:, k:k + 1], axis=0)), "qugather", it)
            pipeline(e, NT, [(gather, 0), (lambda it: pool_rstd(e, S, T, K, "qu", it), 1)])

        @blk.scalar
        def _(e):
            load_split(S, None, e, None, jobs, stage, "qw")

            def high(it):
                S.wait(e, "quxs", it)
                S.wait(e, "quT", it.back(2))
                S.done(e.activation(xhl[it.p][:, 0:D], T["xs"][it.p][:, :], ACT.Copy), "quxh")

            def parts(it):
                S.wait(e, "quproj", it)
                S.wait(e, "qrms", it.back(1))
                S.done(e.activation(sq[:, :], pQ[it.p][:, :], ACT.Square, scale=UNSCALE), "qrsq")
                S.wait(e, "qrms", it)
                S.done(e.activation(ss[:, :], ss[:, :], ACT.Sqrt), "qrrt")
                S.wait(e, "qrn", it)
                S.wait(e, "quS", it.back(2))
                S.done(e.activation(part_pair(qp[it.p][:, :], 0, 1), twice(qn[it.p][:, :]), ACT.Copy), "quhi")

            def evacuate(it):
                S.wait(e, "quS", it)
                S.wait_moved(e, "ququt", it.back(2))
                S.done(e.activation(qt[it.p][:, :], pS[it.p][:, :, :].rearrange("p j n -> p (j n)"), ACT.Copy), "quqt")
            pipeline(e, NT, [(evacuate, 4), (high, 1), (parts, 3)])

        @blk.vector
        def _(v):
            load_split(S, None, None, v, jobs, stage, "qw")
            front, mid, back = (Line(S, v, f"qudve{i}") for i in range(3))

            def norm(it):
                front.start(it)
                S.wait_moved(v, "qugather", it, KR)
                S.wait_moved(v, "quxin", it)
                S.wait_moved(v, "quxout", it.back(2))
                for k in range(KR):
                    front(v.scalar_tensor_tensor(x2[it.p][:, :], yg[it.p][:, k, :], K["g2f"][:, bass.ds(it.n * KR + k, 1)],
                                                 (xin if k == 0 else x2)[it.p][:, :], ALU.mult, ALU.add),
                          "qux2" if k == KR - 1 else None)
                norm_parts(front, v, S, T, x2[it.p][:, :], "qu", it)
                S.wait(v, "quxh", it)
                front(v.tensor_tensor(xhl[it.p][:, D:], T["xs"][it.p][:, :], xhl[it.p][:, 0:D], ALU.subtract), "quxl")

            def evacuate(it):
                mid.start(it)
                S.wait(v, "quT", it)
                S.wait(v, "quproj", it.back(2))
                mid(v.tensor_copy(xT[it.p][:, :, :], pT[it.p][:, :, :]), "quxT")

            def heads(it):
                back.start(it)
                S.wait(v, "quhi", it.back(2))
                head_norm(back, v, S, "qr", it, pQ[it.p][:, :], sq[:, :], ss[:, :], rr[:, :], qn[it.p][:, :], SA * UNSCALE)
                S.wait(v, "quhi", it)
                back(v.tensor_tensor(part_pair(qp[it.p][:, :], 2, 1), twice(qn[it.p][:, :]),
                                     bcast(qp[it.p][:, :], [(4 * HD, NH), (0, 2), (1, HD)]), ALU.subtract), "qulo")
            pipeline(v, NT, [(norm, 1), (evacuate, 2), (heads, 3)])

        @blk.tensor
        def _(e):
            e.wait_ge(S.sem("qwlo"), len(jobs))

            def project(it):
                S.wait(e, "quxT", it)
                S.wait(e, "qrn", it.back(2))
                terms = split_terms((xT[it.p][:, 0:KD, :], xT[it.p][:, KD:, :]), wq, KD)
                for j, (x, w, k) in enumerate(terms):
                    last = e.matmul(pQ[it.p][:, :], x[:, k, :], w[:, k * D:(k + 1) * D],
                                    start=j == 0, stop=j == len(terms) - 1)
                S.done(last, "quproj")

            def turn(it):
                S.wait(e, "quxl", it)
                S.wait(e, "quxT", it.back(2))
                S.done(transposes(e, pT[it.p], xhl[it.p], K["ident"][:, :], 2 * KD), "quT")

            def stack(it):
                S.wait(e, "qulo", it)
                S.wait(e, "quqt", it.back(2))
                S.done(transposes(e, pS[it.p], qp[it.p], K["ident"][:, :], NH // 2), "quS")
            pipeline(e, NT, [(project, 3), (turn, 2), (stack, 4)])


def phase_attention(nc, S, sb, ps, a, R, K, out):
    G = NH // 4
    NG = BATCH * G
    with ExitStack() as keep:
        o = sb(keep, "o", [P, NT * D])
        ident = sb(keep, "ident32", [P, P])
        with ExitStack() as mem:
            q = [sb(mem, f"atq{i}", [P, 4, 2, P], f16) for i in range(2)]
            k = [sb(mem, f"atk{i}", [P, 4, 2, 2, P], f16) for i in range(2)]
            vv = [sb(mem, f"atv{i}", [P, 4, 4 * (HD + 1)]) for i in range(2)]
            pr = [sb(mem, f"atp{i}", [P, 2 * SEQ]) for i in range(4)]
            oT = [sb(mem, f"atoT{i}", [P, SEQ]) for i in range(2)]
            rc = sb(mem, "atrc", [P, 4, 4])
            pS = [ps(mem, f"atpS{i}", [P, 2 * SEQ]) for i in range(2)]
            pO = [ps(mem, f"atpO{i}", [P, SEQ]) for i in range(2)]
            pX = ps(mem, "atpX", [P, 4, P])
            blk = mem.enter_context(nc.Block())

            @blk.sync
            def _(e):
                e.dma_start(ident[:, :], a["c_ident32"]).then_inc(S.sem("at_ident"), 16)
                e.wait_ge(S.sem("at_init"), 1)

                def load(it):
                    b, g = it.n // G, it.n % G
                    S.wait(e, "atqk", it.back(2), 8)
                    S.wait(e, "atpv", it.back(2), 4)
                    S.static(e)
                    tiles = R["qst"].rearrange("(b t) p c -> b p t c", b=BATCH)
                    S.moved(e.dma_start(q[it.p][:, :, :, :].rearrange("p t j n -> p t (j n)"),
                                        tiles[bass.ds(b, 1), :, :, bass.ds(g * 2 * P, 2 * P)].rearrange("b p t c -> (b p) t c")),
                            "atin", it)
                    tiles = R["kst"].rearrange("(b t) p c -> b p t c", b=BATCH)
                    for s in range(2):
                        r = slice(64 * s, 64 * s + 64)
                        S.moved(e.dma_start(k[it.p][r, :, s, :, :].rearrange("p t j n -> p t (j n)"),
                                            tiles[bass.ds(b, 1), r, :, bass.ds(g * 2 * P, 2 * P)].rearrange("b p t c -> (b p) t c")),
                                "atin", it)
                    tiles = R["vst"].rearrange("(b t) p c -> b p t c", b=BATCH)
                    V = 4 * (HD + 1)
                    S.moved(e.dma_start(vv[it.p][:, :, :], tiles[bass.ds(b, 1), :, :, bass.ds(g * V, V)].rearrange("b p t c -> (b p) t c")),
                            "atin", it)
                pipeline(e, NG, [(load, 0)])

            @blk.tensor
            def _(e):
                e.wait_ge(S.sem("at_ident"), 16)

                def scores(it, m):
                    for j in range(2):
                        u = 2 * m + j
                        if not isinstance(it.n, int) or it.n * 8 + u >= 2:
                            e.wait_ge(S.sem("atexp"), it.n * 8 + (u - 1))
                        for s in range(2):
                            last = e.matmul(pS[j][:, s * SEQ:(s + 1) * SEQ], k[it.p][:, m, s, j, :],
                                            q[it.p][:, :, j, :], start=True, stop=True)
                        S.done(last, "atqk")

                def weigh(it, m):
                    e.wait_ge(S.sem("atexp"), it.n * 8 + (2 * m + 2))
                    if m == 0:
                        S.wait(e, "atoT", it.back(2))
                    for i in range(4):
                        n = HD + 1
                        last = e.matmul(pO[it.p][32 * i:32 * i + n, :], vv[it.p][:, m, i * n:(i + 1) * n],
                                        pr[(2 * m + i // 2) % 4][:, (i % 2) * SEQ:(i % 2 + 1) * SEQ],
                                        start=m == 0, stop=m == 3)
                    S.done(last, "atpv")

                def first(it):
                    S.wait_moved(e, "atin", it, 4)
                    scores(it, 0)

                def rest(it):
                    for m in range(1, 4):
                        scores(it, m)
                        weigh(it, m - 1)

                def turn(it):
                    S.wait(e, "atoT", it)
                    S.wait(e, "ato", it.back(1))
                    for t in range(4):
                        last = e.transpose(pX[:, t, :], oT[it.p][:, t * P:(t + 1) * P], ident[:, :])
                    S.done(last, "atX")
                pipeline(e, NG, [(first, 1), (lambda it: weigh(it, 3), 2), (rest, 1), (turn, 2)])

            @blk.scalar
            def _(e):
                def exps(it):
                    for u in range(8):
                        e.wait_ge(S.sem("atqk"), it.n * 8 + (u + 1))
                        if not isinstance(it.n, int) or it.n * 4 + u // 2 >= 2:
                            e.wait_ge(S.sem("atpv"), it.n * 4 + (u // 2 - 1))
                        S.done(e.activation(pr[u % 4][:, :], pS[u % 2][:, :], ACT.Exp, scale=HD ** -0.5 / SA ** 2), "atexp")
                pipeline(e, NG, [(exps, 1)])

            @blk.vector
            def _(v):
                init = Line(S, v, "atinit")
                init.start(It(0, 0))
                for i in range(2):
                    init(v.memset(k[i][:, :, :, :, :].rearrange("p t s j n -> p (t s j n)"), 0.0))
                    init(v.memset(pO[i][:, :], 0.0), "at_init" if i else None)
                line = Line(S, v, "atdve")

                def into(b, g):
                    x = o[:, :].rearrange("p (b t h c) -> p b t h c", b=BATCH, t=4, h=G)
                    return x[:, bass.ds(b, 1), :, bass.ds(g, 1), :].rearrange("p b t h (i d) -> p (b t) (h i) d", i=4)

                def evacuate(it):
                    v.wait_ge(S.sem("atpv"), it.n * 4 + 4)
                    S.wait(v, "atX", it.back(2))
                    S.done(v.tensor_copy(oT[it.p][:, :], pO[it.p][:, :]), "atoT")

                def normalise(it):
                    line.start(it)
                    b, g = it.n // G, it.n % G
                    S.wait(v, "atX", it)
                    x = pX[:, 0, 0:1]
                    line(v.reciprocal(rc[:, :, :], bass.AP(x.tensor, x.offset + HD, [list(x.ap[0]), [P, 4], [32, 4]])))
                    line(v.tensor_tensor(
                        into(b, g), bass.AP(x.tensor, x.offset, [list(x.ap[0]), [P, 4], [32, 4], [1, HD]]),
                        bcast(rc[:, 0, 0:1], [(4, 4), (1, 4), (0, HD)]), ALU.mult), "ato")
                pipeline(v, NG, [(evacuate, 2), (normalise, 2)])

        phase_last(nc, S, sb, ps, a, R, K, o, ident, out)


def phase_last(nc, S, sb, ps, a, R, K, o, ident, out):
    BIG = 1e30
    with ExitStack() as mem:
        sl = sb(mem, "lasl", [NTILE, DSL * GRID])
        ssum = sb(mem, "lassum", [NTILE, DSL])
        ssg = sb(mem, "lassg", [NTILE, DSL])
        sgn = sb(mem, "lasgn", [P, D])
        gam = sb(mem, "lagam", [P, D])
        bet = sb(mem, "labet", [P, D])
        tab = sb(mem, "latab", [P, 2 * DSL * GRID + 1])
        xin = [sb(mem, f"laxin{i}", [P, D]) for i in range(2)]
        x3 = sb(mem, "lax3", [P, D])
        z = sb(mem, "laz", [P, D])
        xf = [sb(mem, f"laxf{i}", [P, D]) for i in range(2)]
        sg = [sb(mem, f"lasg{i}", [P, D]) for i in range(2)]
        st, mv = sb(mem, "last", [P, 6]), sb(mem, "lamv", [P, 2])
        ve, rstd = sb(mem, "lave", [P, 1]), sb(mem, "larstd", [P, 1])
        ve2, rstd2 = sb(mem, "lave2", [P, 1]), sb(mem, "larstd2", [P, 1])
        ts, cs = sb(mem, "lats", [P, NTILE]), sb(mem, "lacs", [P, NCL])
        key, best = sb(mem, "lakey", [P, NTILE]), sb(mem, "labest", [P, 1])
        oh = sb(mem, "laoh", [P, NT * NTILE])
        oh16 = sb(mem, "laoh16", [P, NT * NTILE], f16)
        sel = sb(mem, "lasel", [P, D])
        xs = sb(mem, "laxs", [P, NT * DSL])
        lo, hi = sb(mem, "lalo", [P, NT]), sb(mem, "lahi", [P, NT])
        w1, w2 = sb(mem, "law1", [P, NT * NTILE]), sb(mem, "law2", [P, NT * NTILE])
        ext = [sb(mem, f"laext{i}", [P, NTILE]) for i in range(2)]
        col = [sb(mem, f"lacol{i}", [NTILE, 1]) for i in range(2)]
        colb = [sb(mem, f"lacolb{i}", [NTILE, P]) for i in range(2)]
        mn, mx = sb(mem, "lamn", [P, NT]), sb(mem, "lamx", [P, NT])
        num = sb(mem, "lanum", [P, NT * DSL])
        u = sb(mem, "lau", [P, NT * DSL])
        gi = sb(mem, "lagi", [P, NT * DSL])
        og = sb(mem, "laog", [P, NT * DSL * GRID])
        ohT = [sb(mem, f"laohT{i}", [P, P]) for i in range(2)]
        pick = sb(mem, "lapick", [P, 2, DSL * GRID])
        bs = sb(mem, "labs", [P, NT * 2 * DSL])
        osc = sb(mem, "laosc", [P, NT])
        dl = sb(mem, "ladl", [P, NT * DSL])
        res = [sb(mem, f"lares{i}", [P, D]) for i in range(2)]
        pEB = ps(mem, "lapEB", [P, 512])
        pE = pEB[0:NTILE, 0:2 * P].rearrange("p (a n) -> p a n", a=2)
        pB = pEB[:, 2 * P:3 * P].rearrange("p (a n) -> p a n", a=2)
        pH = [ps(mem, f"lapH{i}", [P, 1024], f16)[:, 0:P] for i in range(2)]
        pT = [[ps(mem, f"lapT{i}{j}", [P, 512]) for j in range(2)] for i in range(2)]
        blk = mem.enter_context(nc.Block())
        TG = DSL * GRID

        @blk.sync
        def _(e):
            e.dma_start(sl[:, :], a["slopes"]).then_inc(S.sem("la_sl"), 16)
            for t, name in ((gam, "gamma"), (bet, "beta")):
                e.dma_start(t[:, :], bass.AP(a[name].tensor, 0, [[0, P], [1, D]])).then_inc(S.sem("la_gb"), 16)
            for r in (slice(0, NTILE), slice(NTILE, P)):
                e.dma_start(tab[r, 0:TG], a["bases"]).then_inc(S.sem("la_tab"), 16)
                e.dma_start(tab[r, TG:2 * TG], a["slopes"]).then_inc(S.sem("la_tab"), 16)
                e.dma_start(tab[r, 2 * TG:], a["oscale"]).then_inc(S.sem("la_tab"), 16)
            e.wait_ge(S.sem("la_ssg"), 1)
            e.dma_start(R["sign"].rearrange("(t j) -> t j", j=DSL), ssg[:, :]).then_inc(S.sem("la_sign"), 16)
            e.wait_ge(S.sem("la_sign"), 16)
            e.dma_start(sgn[:, :], bass.AP(R["sign"].tensor, 0, [[0, P], [1, D]])).then_inc(S.sem("la_signb"), 16)

            def load(it):
                S.wait(e, "lax3", it.back(2))
                S.static(e)
                S.moved(e.dma_start(xin[it.p][:, :], R["x2"][bass.ds(it.n * P, P), :]), "laxin", it)
            pipeline(e, NT, [(load, 0)])

            def store(it):
                S.wait(e, "lares", it)
                S.static(e)
                S.moved(e.dma_start(out[bass.ds(it.n * P, P), :], res[it.p][:, :]), "laout", it)
            pipeline(e, NT, [(store, 0)])
            for p in range(2):
                S.wait_moved(e, "laout", It(NT // 2 - 1, p))

        @blk.gpsimd
        def _(e):
            def roots(it):
                S.wait(e, "lave", it)
                S.done(e.tensor_tensor(rstd[:, :], ve[:, :], K["mhalf"][:, :], ALU.pow), "larstd")
                S.wait(e, "lave2", it)
                S.done(e.tensor_tensor(rstd2[:, :], ve2[:, :], K["mhalf"][:, :], ALU.pow), "larstd2")
            pipeline(e, NT, [(roots, 0)])

        @blk.scalar
        def _(e):
            e.wait_ge(S.sem("la_ssum"), 1)
            e.activation(ssg[:, :], ssum[:, :], ACT.Sign).then_inc(S.sem("la_ssg"), 1)

            def signs(it):
                S.wait(e, "laxf", it)
                S.wait(e, "lam", it.back(2))
                S.done(e.activation(sg[it.p][:, :], xf[it.p][:, :], ACT.Sign), "lasg")
            pipeline(e, NT, [(signs, 0)])

            def turn(it):
                S.wait(e, "laH", it)
                S.wait(e, "laT", it.back(2))
                S.done(e.activation(ohT[it.p][:, :], pH[it.p], ACT.Copy), "laohT")
            pipeline(e, NT // 2, [(turn, 0)])

        @blk.vector
        def _(v):
            line = Line(S, v, "la0")
            line.start(It(0, 0))
            v.wait_ge(S.sem("la_sl"), 16)
            line(v.tensor_reduce(ssum[:, :], sl[:, :].rearrange("t (j g) -> t j g", g=GRID), AX.X, ALU.add))
            line(v.tensor_scalar(ssum[:, :], ssum[:, :], 1.0 / GRID, None, ALU.mult), "la_ssum")
            v.wait_ge(S.sem("la_gb"), 32)
            v.wait_ge(S.sem("la_signb"), 16)
            front, back = Line(S, v, "la1"), Line(S, v, "la2")

            def norm(it):
                front.start(it)
                at = bass.ds(it.n * D, D)
                S.wait_moved(v, "laxin", it)
                front(v.scalar_tensor_tensor(x3[:, :], o[:, at], K["gate"][:, 2:3], xin[it.p][:, :],
                                             ALU.mult, ALU.add), "lax3")
                front(v.bn_stats(st[:, :], x3[:, :]))
                S.static(v)
                front(v.bn_aggr(mv[:, :], st[:, :]))
                front(v.tensor_scalar(ve[:, :], mv[:, 1:2], EPS, None, ALU.add), "lave")
                S.wait(v, "larstd", it)
                front(v.tensor_scalar(z[:, :], x3[:, :], mv[:, 0:1], rstd[:, :], ALU.subtract, ALU.mult))
                front(v.scalar_tensor_tensor(o[:, at], z[:, :], K["gate"][:, 3:4], x3[:, :], ALU.mult, ALU.add))
                S.static(v)
                front(v.bn_stats(st[:, :], z[:, :]))
                S.static(v)
                front(v.bn_aggr(mv[:, :], st[:, :]))
                front(v.tensor_scalar(ve2[:, :], mv[:, 1:2], EPS, None, ALU.add), "lave2")
                S.wait(v, "larstd2", it)
                front(v.tensor_scalar(xf[it.p][:, :], z[:, :], mv[:, 0:1], rstd2[:, :], ALU.subtract, ALU.mult))
                front(v.tensor_tensor(xf[it.p][:, :], xf[it.p][:, :], gam[:, :], ALU.mult))
                front(v.tensor_tensor(xf[it.p][:, :], xf[it.p][:, :], bet[:, :], ALU.add), "laxf")

            def choose(it):
                back.start(it)
                S.wait(v, "lasg", it)
                back(v.tensor_tensor(sel[:, :], sg[it.p][:, :], sgn[:, :], ALU.mult), "lam")
                back(v.tensor_reduce(ts[:, :], sel[:, :].rearrange("p (t j) -> p t j", j=DSL), AX.X, ALU.add))
                back(v.tensor_reduce(cs[:, :], ts[:, :].rearrange("p (c t) -> p c t", t=NTILE // NCL), AX.X, ALU.add))
                back(v.scalar_tensor_tensor(cs[:, :], cs[:, :], 8.0, K["iota"][:, 0:NCL], ALU.mult, ALU.subtract))
                back(v.tensor_scalar(cs[:, :], cs[:, :], 256.0, None, ALU.mult))
                back(v.scalar_tensor_tensor(
                    key[:, :].rearrange("p (c t) -> p c t", c=NCL), ts[:, :].rearrange("p (c t) -> p c t", c=NCL), 8.0,
                    bcast(K["iota"][:, 0:1], [(0, NCL), (1, NTILE // NCL)]), ALU.mult, ALU.subtract))
                back(v.tensor_tensor(key[:, :].rearrange("p (c t) -> p c t", c=NCL), key[:, :].rearrange("p (c t) -> p c t", c=NCL),
                                     bcast(cs[:, 0:1], [(1, NCL), (0, NTILE // NCL)]), ALU.add))
                back(v.tensor_reduce(best[:, :], key[:, :], AX.X, ALU.max))
                back(v.tensor_scalar(oh[:, bass.ds(it.n * NTILE, NTILE)], key[:, :], best[:, :], None, ALU.is_equal), "laoh")
                back(v.tensor_tensor(sel[:, :].rearrange("p (t j) -> p t j", j=DSL), xf[it.p][:, :].rearrange("p (t j) -> p t j", j=DSL),
                                     wide(it), ALU.mult))
                back(v.tensor_reduce(xs[:, bass.ds(it.n * DSL, DSL)], sel[:, :].rearrange("p (t j) -> p j t", j=DSL), AX.X, ALU.add))
                back(v.tensor_reduce(lo[:, bass.ds(it.n, 1)], xs[:, bass.ds(it.n * DSL, DSL)], AX.X, ALU.min))
                back(v.tensor_reduce(hi[:, bass.ds(it.n, 1)], xs[:, bass.ds(it.n * DSL, DSL)], AX.X, ALU.max))

            def wide(it):
                return oh[:, :].rearrange("p (n t a) -> p n t a", t=NTILE, a=1)[:, bass.ds(it.n, 1), :, :]\
                    .rearrange("p n t a -> p (n t) a").to_broadcast((P, NTILE, DSL))
            pipeline(v, NT, [(norm, 0), (choose, 1)])

            tail = Line(S, v, "la3")
            tail.start(It(0, 0))
            tail(v.tensor_copy(oh16[:, :], oh[:, :]), "laoh16")
            three = lambda t: t[:, :].rearrange("p (n t) -> p n t", n=NT)
            for i, (val, op, big) in enumerate(((lo, ALU.min, BIG), (hi, ALU.max, -BIG))):
                tail(v.tensor_scalar(w1[:, :], oh[:, :], -big, big, ALU.mult, ALU.add))
                tail(v.tensor_tensor(three(w2), three(oh), bcast(val[:, 0:1], [(1, NT), (0, NTILE)]), ALU.mult))
                tail(v.tensor_tensor(w1[:, :], w1[:, :], w2[:, :], ALU.add))
                tail(v.tensor_reduce(ext[i][:, :], w1[:, :].rearrange("p (n t) -> p t n", n=NT), AX.X, op), f"laext{i}")
            for i, op in enumerate((ALU.min, ALU.max)):
                v.wait_ge(S.sem("laE"), 2)
                tail(v.tensor_reduce(col[i][:, :], pE[:, i, :], AX.X, op))
                tail(v.tensor_copy(colb[i][:, :], bcast(col[i][:, :], [(0, P)])), f"lacol{i}")
            for i, to in enumerate((mn, mx)):
                v.wait_ge(S.sem("laB"), 2)
                tail(v.tensor_tensor(three(w1), three(oh), bcast(pB[:, i, 0:1], [(0, NT), (1, NTILE)]), ALU.mult))
                tail(v.tensor_reduce(to[:, :], three(w1), AX.X, ALU.add))
            eight = lambda t: t[:, :].rearrange("p (n j) -> p n j", j=DSL)
            tail(v.tensor_tensor(eight(num), eight(xs), bcast(mn[:, 0:1], [(1, NT), (0, DSL)]), ALU.subtract))
            tail(v.tensor_tensor(mx[:, :], mx[:, :], mn[:, :], ALU.subtract))
            tail(v.tensor_scalar(mx[:, :], mx[:, :], 1e-8, None, ALU.add))
            tail(v.reciprocal(mx[:, :], mx[:, :]))
            tail(v.tensor_tensor(eight(u), eight(num), bcast(mx[:, 0:1], [(1, NT), (0, DSL)]), ALU.mult))
            tail(v.tensor_scalar(u[:, :], u[:, :], 0.0, float(np.float32(1.0 - 1e-6)), ALU.max, ALU.min))
            tail(v.tensor_scalar(u[:, :], u[:, :], float(GRID), None, ALU.mult))
            sixteen = og[:, :].rearrange("p (n g) -> p n g", g=GRID)
            grid = bcast(K["iota"][:, 0:1], [(0, NT * DSL), (1, GRID)])
            tail(v.tensor_tensor(sixteen, bcast(u[:, 0:1], [(1, NT * DSL), (0, GRID)]), grid, ALU.is_ge))
            tail(v.tensor_reduce(gi[:, :], sixteen, AX.X, ALU.add))
            tail(v.tensor_scalar(gi[:, :], gi[:, :], -1.0, None, ALU.add))
            tail(v.tensor_tensor(sixteen, bcast(gi[:, 0:1], [(1, NT * DSL), (0, GRID)]), grid, ALU.is_equal))
            tail(v.tensor_tensor(u[:, :], u[:, :], gi[:, :], ALU.subtract))
            rows = Line(S, v, "la4")

            def pickup(it):
                rows.start(it)
                S.wait(v, "laT", it)
                for j in range(2):
                    n = it.n * 2 + j
                    g = og[:, :].rearrange("p (a n g) -> p a n g", a=1, n=NT)[:, :, bass.ds(n, 1), :]\
                        .rearrange("p a n g -> p a (n g)").to_broadcast((P, 2, TG))
                    t = pT[it.p][j]
                    rows(v.tensor_tensor(pick[:, :, :], t[:, 0:2 * TG].rearrange("p (a g) -> p a g", a=2), g, ALU.mult))
                    rows(v.tensor_reduce(bs[:, bass.ds(n * 2 * DSL, 2 * DSL)],
                                         pick[:, :, :].rearrange("p a (j g) -> p (a j) g", g=GRID), AX.X, ALU.add))
                    rows(v.tensor_copy(osc[:, bass.ds(n, 1)], t[:, 2 * TG:2 * TG + 1]), "lapick" if j else None)
            pipeline(v, NT // 2, [(pickup, 0)])
            two = bs[:, :].rearrange("p (n a j) -> p n a j", a=2, j=DSL)
            tail(v.tensor_tensor(eight(dl), two[:, :, 1, :], eight(u), ALU.mult))
            tail(v.tensor_tensor(eight(dl), two[:, :, 0, :], eight(dl), ALU.add))
            tail(v.tensor_scalar(osc[:, :], osc[:, :], K["gate"][:, 3:4], None, ALU.mult))
            tail(v.tensor_tensor(eight(dl), eight(dl), bcast(osc[:, 0:1], [(1, NT), (0, DSL)]), ALU.mult))
            fin = Line(S, v, "la5")

            def finish(it):
                fin.start(it)
                S.wait_moved(v, "laout", it.back(2))
                d = dl[:, :].rearrange("p (n a j) -> p n a j", n=NT, a=1)[:, bass.ds(it.n, 1), :, :]\
                    .rearrange("p n a j -> p (n a) j").to_broadcast((P, NTILE, DSL))
                fin(v.tensor_tensor(res[it.p][:, :].rearrange("p (t j) -> p t j", j=DSL), wide(it), d, ALU.mult))
                fin(v.tensor_tensor(res[it.p][:, :], res[it.p][:, :], o[:, bass.ds(it.n * D, D)], ALU.add), "lares")
            pipeline(v, NT, [(finish, 0)])

        @blk.tensor
        def _(e):
            for i in range(2):
                e.wait_ge(S.sem(f"laext{i}"), 1)
                e.transpose(pE[:, i, :], ext[i][:, :], ident[:, :]).then_inc(S.sem("laE"), 1)
            for i in range(2):
                e.wait_ge(S.sem("lacol1"), 1)
                e.transpose(pB[:, i, :], colb[i][:, :], ident[0:NTILE, 0:NTILE]).then_inc(S.sem("laB"), 1)
            e.wait_ge(S.sem("la_tab"), 96)
            e.wait_ge(S.sem("laoh16"), 1)

            def turn(it):
                S.wait(e, "laohT", it.back(2))
                S.static(e)
                S.done(e.transpose(pH[it.p], oh16[:, bass.ds(it.n * P, P)], K["ident"][:, :]), "laH")

            def look(it):
                S.wait(e, "laohT", it)
                S.wait(e, "lapick", it.back(2))
                for j in range(2):
                    r = slice(NTILE * j, NTILE * j + NTILE)
                    last = e.matmul(pT[it.p][j][:, 0:2 * TG + 1], ohT[it.p][r, :], tab[r, :], start=True, stop=True)
                S.done(last, "laT")
            pipeline(e, NT // 2, [(turn, 0), (look, 1)])


def layout(x, itok, ctx, gx, gf, sw1, sb1, sw2, sb2, rw1, rb1, rw2, rb2, cen, bias, wq, wk, wv,
           gamma, beta, bases, slopes, oscale):
    def rows(w):
        w = w.reshape(w.shape[:-2] + (w.shape[-2] // P, P, w.shape[-1]))
        return np.ascontiguousarray(np.swapaxes(w, -3, -2)).reshape(w.shape[:-3] + (P, -1))

    def second(w, b):
        z = np.zeros(w.shape[:-2] + (FB * P - FF - 1, w.shape[-1]), w.dtype)
        return rows(np.concatenate([w, b[..., None, :], z], axis=-2))

    def column(b):
        z = np.zeros(b.shape[:-1] + (FB * P - FF,), b.dtype)
        b = np.concatenate([b, z], axis=-1)
        return np.ascontiguousarray(b.reshape(-1, P).T)

    kv = np.concatenate([wk, wv], axis=0).reshape(NH, HD, 2, D)
    wkh, wvh = (kv[:, :, s].reshape(NH * HD, D) for s in range(2))
    rowi = np.arange(P)
    return {
        "x": x.reshape(TOK, D),
        "ids": np.ascontiguousarray(itok.reshape(NT, P).T),
        "gates": np.concatenate([gx[0:1], gf[0:1], gx[1:2], gf[1:2]]),
        "ctxT": rows(np.ascontiguousarray(ctx.transpose(0, 2, 1))),
        "sw1": rows(sw1), "sb1": column(sb1), "sw2": second(sw2, sb2),
        "rw1": rows(rw1), "rb1": column(rb1), "rw2": second(rw2, rb2),
        "cenT": rows(np.ascontiguousarray(cen.T)), "bias": bias.reshape(1, NR),
        "wqT": rows(np.ascontiguousarray(wq.T)), "wkT": rows(np.ascontiguousarray(wkh.T)),
        "wvT": rows(np.ascontiguousarray(wvh.T)),
        "gamma": gamma.reshape(1, D), "beta": beta.reshape(1, D),
        "bases": bases.reshape(NTILE, DSL * GRID), "slopes": slopes.reshape(NTILE, DSL * GRID),
        "oscale": oscale.reshape(NTILE, 1),
        "c_ident": np.eye(P, dtype=np.float16),
        "c_ident32": np.eye(P, dtype=np.float32),
        "c_tri": (rowi[:, None] < rowi[None, :]).astype(np.float16),
        "c_ones": np.ones((P, P), np.float16),
        "c_iota": np.tile(np.arange(16, dtype=np.float32), (P, 1)),
        "c_tok": (np.arange(NT)[None, :] * P + rowi[:, None]).astype(np.int32),
        "c_iotan": np.arange(N2, dtype=np.float32)[None, :],
    }


def kernel(**inputs):
    import concourse.bacc as bacc
    from concourse.bass_utils import run_bass_kernel_spmd

    names = ["x", "itok_BxS_13_99985", "ctx_2048", "g_xattn", "g_ffn",
             "L0_ffn_shared_w1", "L0_ffn_shared_b1", "L0_ffn_shared_w2", "L0_ffn_shared_b2",
             "L0_ffn_routed_w1", "L0_ffn_routed_b1", "L0_ffn_routed_w2", "L0_ffn_routed_b2",
             "L0_ffn_centroids", "L0_ffn_bias", "L1_xattn_Wq", "L1_xattn_Wk", "L1_xattn_Wv",
             "L1_ffn_ln_gamma", "L1_ffn_ln_beta", "L1_ffn_spline_bases", "L1_ffn_spline_slopes", "L1_ffn_output_scale"]
    arrays = layout(*[np.asarray(inputs[n]) for n in names])
    arrays = {name: np.ascontiguousarray(v) for name, v in arrays.items()}
    nc = bacc.Bacc("TRN2", target_bir_lowering=False, num_devices=1)
    a = {name: nc.dram_tensor(name, v.shape, mybir.dt.from_np(v.dtype), kind="ExternalInput").ap()
         for name, v in arrays.items()}
    out = nc.dram_tensor("out", (TOK, D), f32, kind="ExternalOutput").ap()
    build(nc, a, out)
    r = run_bass_kernel_spmd(nc, [arrays], core_ids=[0])
    return r.results[0]["out"].reshape(BATCH, SEQ, D)
```

```python
import numpy as np
import concourse.bass as bass
from concourse import mybir
from contextlib import ExitStack

f32 = mybir.dt.float32
f16 = mybir.dt.float16
i32 = mybir.dt.int32
u32 = mybir.dt.uint32
ALU = mybir.AluOpType
ACT = mybir.ActivationFunctionType
AX = mybir.AxisListType

P = 128
BATCH, SEQ, D = 4, 512, 512
TOK = BATCH * SEQ
NT = TOK // P
KD = D // P
E1, RANGE1, TOP1 = 4, 25000 // 4, 3
FF, FB = 352, 3
FLAST = FF - 2 * P
NS, NR, KR = 2, 16, 4
NH, HD = 32, 16
GRID, NTILE, DSL, NCL = 16, 64, 8, 8
EPS = 1e-5
EPS_RMS = 1e-6
CAP = TOK
N1 = NT + E1
N2 = NT * KR + NR
SA, SW = 16.0, 64.0
UNSCALE = 1.0 / (SA * SW)


class It:

    def __init__(self, half, parity):
        self.half, self.p = half, parity
        self.n = half * 2 + parity

    def back(self, k):
        q = self.p - k
        return It(self.half + (q // 2), q % 2)


class Sync:

    def __init__(self, nc):
        self.nc, self.sems, self.phase = nc, {}, 0

    def sem(self, name):
        if name not in self.sems:
            self.sems[name] = self.nc.alloc_semaphore(f"{name}_{self.phase}")
        return self.sems[name]

    def clear(self):
        self.nc.clear_and_free_semaphores(list(self.sems.values()))
        self.nc.all_engine_barrier()
        self.sems, self.phase = {}, self.phase + 1

    def done(self, ins, name):
        ins.then_inc(self.sem(name), 1)

    def moved(self, ins, name, it):
        ins.then_inc(self.sem(f"{name}{it.p}"), 16)

    def wait(self, eng, name, it, each=1):
        self.reach(eng, name, it, (it.n + 1) * each)

    def wait_moved(self, eng, name, it, each=1):
        self.reach(eng, f"{name}{it.p}", it, (it.half + 1) * (16 * each))

    def reach(self, eng, name, it, value):
        if not isinstance(it.n, int) or it.n >= 0:
            eng.wait_ge(self.sem(name), value)
            if not isinstance(it.n, int) and eng_name(eng) == "SP":
                self.static(eng)

    def static(self, eng):
        eng.sem_inc(self.sem("spare_" + eng_name(eng)), 1)


def eng_name(eng):
    return str(eng.engine).split(".")[-1]


class Line:

    def __init__(self, sync, eng, name):
        self.s, self.eng, self.link, self.per, self.k = sync, eng, name, None, 0

    def start(self, it):
        if self.k and self.per is None:
            self.per = self.k
        assert self.per is None or self.k in (0, self.per)
        self.it, self.k = it, 0

    def __call__(self, ins, name=None):
        if name:
            self.s.done(ins, name)
            self.s.wait(self.eng, name, self.it)
        else:
            self.k += 1
            ins.then_inc(self.s.sem(self.link), 1)
            first = self.per is None
            self.eng.wait_ge(self.s.sem(self.link), self.k if first else self.it.n * self.per + self.k)


def pipeline(eng, n, stages, unroll=2):
    stages = [s if len(s) == 4 else (s[0], s[1], 0, n) for s in stages]
    most = max(lag for _, lag, _, _ in stages)
    beats = max(lag + stop for _, lag, _, stop in stages)

    def beat(it, active):
        for stage in active:
            stage[0](it.back(stage[1]))

    def active(i):
        return [s for s in stages if s[2] <= i - s[1] < s[3]]
    i, first = 0, (most + 3) // 2 * 2
    while i < beats:
        end = i
        while end < beats and active(end) == active(i):
            end += 1
        full = (end - i) // unroll if i >= first and i % 2 == 0 else 0
        if full > 1:
            now, start = active(i), i // 2
            with eng.Fori(0, full) as h:
                for j in range(unroll):
                    beat(It(h * (unroll // 2) + (start + j // 2), j % 2), now)
            i += unroll * full
        else:
            beat(It(i // 2, i % 2), active(i))
            i += 1


def bcast(ap, dims):
    return bass.AP(ap.tensor, ap.offset, [list(ap.ap[0])] + [[s, c] for s, c in dims])


def build(nc, a, out):
    with ExitStack() as ctx:
        S = Sync(nc)

        def sb(mem, name, shape, dt=f32):
            return mem.enter_context(nc.sbuf_tensor("sb_" + name, shape, dt))

        def ps(mem, name, shape, dt=f32):
            return mem.enter_context(nc.psum_tensor("ps_" + name, shape, dt))

        def dram(name, shape, dt=f32):
            return nc.dram_tensor(name, shape, dt).ap()

        R = {
            "list1": dram("list1", (N1 * P, 1), i32),
            "list2": dram("list2", (NR * CAP + N2 * P, 1), i32),
            "y1s": dram("y1s", (N1 * P, D)),
            "xn2": dram("xn2", (TOK, 2 * D), f16),
            "x2a": dram("x2a", (TOK, D)),
            "ys": dram("ys", (N2 * P, D)),
            "kst": dram("kst", (NT, P, 4 * D), f16),
            "vst": dram("vst", (NT, P, NH * (HD + 1))),
            "qst": dram("qst", (NT, P, 4 * D), f16),
            "x2": dram("x2", (TOK, D)),
            "sign": dram("sign", (D,)),
        }
        K = {
            "ident": sb(ctx, "ident", [P, P], f16),
            "tri": sb(ctx, "tri", [P, P], f16),
            "ones": sb(ctx, "ones", [P, P], f16),
            "iota": sb(ctx, "iota", [P, 16]),
            "tok": sb(ctx, "tok", [P, NT], i32),
            "gate": sb(ctx, "gate", [P, 8]),
            "pos1": sb(ctx, "pos1", [P, NT], i32),
            "pos2": sb(ctx, "pos2", [P, NT * KR], i32),
            "g2f": sb(ctx, "g2f", [P, NT * KR]),
            "tab1": sb(ctx, "tab1", [1, N1], i32),
            "tab2": sb(ctx, "tab2", [1, 2, N2], i32),
            "mhalf": sb(ctx, "mhalf", [P, 1]),
            "iotan": sb(ctx, "iotan", [1, N2]),
        }
        with ExitStack() as mem:
            W = KD * D
            part = {name: [sb(mem, f"{name}{i}", [P, n * W], f16) for i in range(2)]
                    for name, n in (("ctx", BATCH), ("wk", 1), ("wv", 1))}
            phase_setup(nc, S, sb, ps, a, R, K, part)
            S.clear()
            phase_layer1(nc, S, sb, ps, a, R, K, part)
            S.clear()
        for phase in (phase_shared, phase_routed, phase_queries):
            phase(nc, S, sb, ps, a, R, K)
            S.clear()
        phase_attention(nc, S, sb, ps, a, R, K, out)


def make_table(line, v, mem, sb, tag, e, n, count, K, expert, row, pos, posi):
    cols = pos.shape[1]
    gt = sb(mem, tag + "gt", [P, e, 16])
    lim = sb(mem, tag + "lim", [P, 16])
    nt = sb(mem, tag + "nt", [P, e])
    cum = [sb(mem, tag + f"cum{i}", [P, e]) for i in range(2)]
    skip = sb(mem, tag + "skip", [P, e])
    end = sb(mem, tag + "end", [P, e])
    ge = sb(mem, tag + "ge", [1, n, e])
    ef = sb(mem, tag + "ef", [1, n])
    st = sb(mem, tag + "st", [1, n])
    gp = sb(mem, tag + "gp", [P, cols, e])
    sp = sb(mem, tag + "sp", [P, cols])
    line(v.tensor_scalar(lim[:, :], K["iota"][:, :], float(P), None, ALU.mult))
    line(v.tensor_tensor(gt[:, :, :], bcast(count, [(count.ap[1][0], e), (0, 16)]),
                         bcast(lim[:, 0:1], [(0, e), (1, 16)]), ALU.is_gt))
    line(v.tensor_reduce(nt[:, :], gt[:, :, :], AX.X, ALU.add))
    line(v.tensor_copy(cum[0][:, :], nt[:, :]))
    cur, d = 0, 1
    while d < e:
        line(v.tensor_copy(cum[1 - cur][:, 0:d], cum[cur][:, 0:d]))
        line(v.tensor_tensor(cum[1 - cur][:, d:e], cum[cur][:, d:e], cum[cur][:, 0:e - d], ALU.add))
        cur, d = 1 - cur, 2 * d
    line(v.tensor_scalar(skip[:, :], nt[:, :], -float(P), float(CAP), ALU.mult, ALU.add))
    line(v.tensor_scalar(end[:, :], K["iota"][:, 0:e], float(CAP), float(CAP), ALU.mult, ALU.add))
    line(v.tensor_tensor(ge[:, :, :], bcast(K["iotan"][0:1, 0:1], [(1, n), (0, e)]),
                         bcast(cum[cur][0:1, 0:1], [(0, n), (1, e)]), ALU.is_ge))
    line(v.tensor_reduce(ef[:, :], ge[:, :, :], AX.X, ALU.add))
    line(v.tensor_scalar(expert, ef[:, :], float(e - 1), None, ALU.min))
    if row is not None:
        line(v.tensor_tensor(ge[:, :, :], ge[:, :, :], bcast(skip[0:1, 0:1], [(0, n), (1, e)]), ALU.mult))
        line(v.tensor_reduce(st[:, :], ge[:, :, :], AX.X, ALU.add))
        line(v.scalar_tensor_tensor(row, K["iotan"][0:1, 0:n], float(P), st[:, :], ALU.mult, ALU.add))
    line(v.tensor_tensor(gp[:, :, :], bcast(pos, [(1, cols), (0, e)]), bcast(end[:, 0:1], [(0, cols), (1, e)]), ALU.is_ge))
    line(v.tensor_tensor(gp[:, :, :], gp[:, :, :], bcast(skip[:, 0:1], [(0, cols), (1, e)]), ALU.mult))
    line(v.tensor_reduce(sp[:, :], gp[:, :, :], AX.X, ALU.add))
    line(v.tensor_tensor(posi, pos, sp[:, :], ALU.subtract))


def phase_setup(nc, S, sb, ps, a, R, K, part):
    with ExitStack() as mem:
        ids = sb(mem, "ids", [P, NT], i32)
        idf = sb(mem, "idf", [P, NT])
        ge = sb(mem, "ge", [P, E1 + 1, NT])
        oh = sb(mem, "oh", [P, E1, NT], f16)
        tot = sb(mem, "tot", [P, E1, NT])
        inc = [sb(mem, f"inc{i}", [P, E1, NT]) for i in range(2)]
        pos = sb(mem, "pos", [P, E1, NT])
        sel = sb(mem, "sel", [P, E1, NT])
        posf = sb(mem, "posf", [P, NT])
        zero = sb(mem, "zero", [P, (NR * CAP + N2 * P) // P], i32)
        posb = [sb(mem, f"posb{i}", [P, 1], i32) for i in range(NT)]
        toks = [sb(mem, f"toks{i}", [P, 1], i32) for i in range(NT)]
        g4 = sb(mem, "g4", [P, 4])
        pp = ps(mem, "pp", [P, 2, E1 * NT])
        W = KD * D
        stage = [sb(mem, f"sustage{i}", [P, W]) for i in range(2)]
        jobs = [(a["ctxT"][i], part["ctx"][0][:, i * W:(i + 1) * W], part["ctx"][1][:, i * W:(i + 1) * W], W)
                for i in range(BATCH)]
        jobs += [(a[w + "T"], part[w][0][:, :], part[w][1][:, :], W) for w in ("wk", "wv")]
        blk = mem.enter_context(nc.Block())

        @blk.sync
        def _(e):
            loads = [("ident", K["ident"]), ("tri", K["tri"]), ("ones", K["ones"]), ("iota", K["iota"]),
                     ("tok", K["tok"]), ("iotan", K["iotan"])]
            for name, t in loads:
                e.dma_start(t[:, :], a["c_" + name]).then_inc(S.sem("su_consts"), 16)
            e.dma_start(ids[:, :], a["ids"]).then_inc(S.sem("su_ids"), 16)
            e.dma_start(g4[:, :], bass.AP(a["gates"].tensor, 0, [[0, P], [1, 4]])).then_inc(S.sem("su_gates"), 16)
            e.wait_ge(S.sem("su_zero"), 1)
            for name in ("list1", "list2"):
                rows = R[name].shape[0]
                e.dma_start(R[name].rearrange("(p c) o -> p (c o)", p=P), zero[:, 0:rows // P])\
                    .then_inc(S.sem("su_list0"), 16)
            load_split(S, e, None, None, jobs, stage, "su")
            e.wait_ge(S.sem("su_list0"), 32)

        @blk.vector
        def _(v):
            line = Line(S, v, "su_dve")
            line.start(It(0, 0))
            line(v.memset(zero[:, :], 0), "su_zero")
            line(v.memset(K["mhalf"][:, :], -0.5))
            line(v.memset(ge[:, 0, :], 1.0))
            line(v.memset(ge[:, E1, :], 0.0))
            v.wait_ge(S.sem("su_consts"), 16 * 6)
            v.wait_ge(S.sem("su_ids"), 16)
            line(v.tensor_copy(idf[:, :], ids[:, :]))
            for i in range(1, E1):
                line(v.tensor_scalar(ge[:, i, :], idf[:, :], float(i * RANGE1), None, ALU.is_ge))
            line(v.tensor_tensor(oh[:, :, :], ge[:, 0:E1, :], ge[:, 1:E1 + 1, :], ALU.subtract), "su_onehot")
            v.wait_ge(S.sem("su_count"), 1)
            line(v.tensor_copy(tot[:, :, :].rearrange("p e t -> p (e t)"), pp[:, 1, :]))
            line(v.tensor_copy(inc[0][:, :, :], tot[:, :, :]))
            cur, d = 0, 1
            while d < NT:
                line(v.tensor_copy(inc[1 - cur][:, :, 0:d], inc[cur][:, :, 0:d]))
                line(v.tensor_tensor(inc[1 - cur][:, :, d:], inc[cur][:, :, d:], inc[cur][:, :, 0:NT - d], ALU.add))
                cur, d = 1 - cur, 2 * d
            line(v.tensor_tensor(pos[:, :, :], inc[cur][:, :, :], tot[:, :, :], ALU.subtract))
            line(v.tensor_tensor(pos[:, :, :].rearrange("p e t -> p (e t)"), pp[:, 0, :],
                                 pos[:, :, :].rearrange("p e t -> p (e t)"), ALU.add))
            for i in range(1, E1):
                line(v.tensor_scalar(pos[:, i, :], pos[:, i, :], float(i * CAP), None, ALU.add))
            line(v.tensor_tensor(sel[:, :, :], pos[:, :, :], oh[:, :, :], ALU.mult))
            line(v.tensor_reduce(posf[:, :], sel[:, :, :].rearrange("p e t -> p t e"), AX.X, ALU.add))
            make_table(line, v, mem, sb, "t1", E1, N1, inc[cur][:, :, NT - 1], K, K["tab1"][0:1, :], None,
                       posf[:, :], K["pos1"][:, :])
            for i in range(NT):
                v.tensor_copy(toks[i][:, :], K["tok"][:, i:i + 1])
                line(v.tensor_copy(posb[i][:, :], K["pos1"][:, i:i + 1]))
            line(v.memset(sel[:, 0, 0:1], 0.0), "su_pos")
            load_split(S, None, None, v, jobs, stage, "su")

        @blk.tensor
        def _(e):
            e.wait_ge(S.sem("su_consts"), 16 * 6)
            e.wait_ge(S.sem("su_onehot"), 1)
            o = oh[:, :, :].rearrange("p e t -> p (e t)")
            e.matmul(pp[:, 0, :], K["tri"][:, :], o, start=True, stop=True)
            e.matmul(pp[:, 1, :], K["ones"][:, :], o, start=True, stop=True).then_inc(S.sem("su_count"), 1)

        @blk.scalar
        def _(e):
            e.wait_ge(S.sem("su_gates"), 16)
            e.activation(K["gate"][:, 0:4], g4[:, :], ACT.Tanh).then_inc(S.sem("su_tanh"), 1)
            e.wait_ge(S.sem("su_tanh"), 1)
            e.activation(K["gate"][:, 4:5], K["gate"][:, 0:1], ACT.Copy, scale=UNSCALE)
            e.activation(K["gate"][:, 5:6], K["gate"][:, 1:2], ACT.Copy, scale=1.0 / SA)
            e.activation(K["gate"][:, 6:7], K["gate"][:, 1:2], ACT.Copy, scale=UNSCALE)
            load_split(S, None, e, None, jobs, stage, "su")

        @blk.gpsimd
        def _(e):
            e.wait_ge(S.sem("su_pos"), 1)
            e.wait_ge(S.sem("su_list0"), 32)
            for i in range(NT):
                e.indirect_dma_start(out=R["list1"], out_offset=bass.IndirectOffsetOnAxis(ap=posb[i][:, :], axis=0),
                                     in_=toks[i][:, :], in_offset=None).then_inc(S.sem("su_scatter"), 16)
            e.wait_ge(S.sem("su_scatter"), 16 * NT)


def load_split(S, sync_, act, dve, jobs, stage, tag):
    def load(e):
        for n, (src, hi, lo, cols) in enumerate(jobs):
            it = It(n // 2, n % 2)
            S.wait(e, tag + "lo", it.back(2))
            S.moved(e.dma_start(stage[it.p][:, 0:cols], src), tag + "w", it)

    def high(e):
        for n, (src, hi, lo, cols) in enumerate(jobs):
            it = It(n // 2, n % 2)
            S.wait_moved(e, tag + "w", it)
            S.done(e.activation(hi, stage[it.p][:, 0:cols], ACT.Copy, scale=SW), tag + "hi")

    def low(e):
        for n, (src, hi, lo, cols) in enumerate(jobs):
            it = It(n // 2, n % 2)
            S.wait(e, tag + "hi", it)
            S.done(e.scalar_tensor_tensor(lo, stage[it.p][:, 0:cols], SW, hi, ALU.mult, ALU.subtract), tag + "lo")
    load(sync_) if sync_ else None
    high(act) if act else None
    low(dve) if dve else None


def row_stats(line, v, S, T, x, tag):
    line(v.bn_stats(T["st"][:, :], x))
    S.static(v)
    line(v.bn_aggr(T["mv"][:, :], T["st"][:, :]))
    line(v.tensor_scalar(T["ve"][:, :], T["mv"][:, 1:2], EPS, None, ALU.add), tag + "var")


def normed(line, v, S, T, x, tag, it):
    S.wait(v, tag + "rstd", it)
    line(v.tensor_scalar(T["rs"][:, :], T["rstd"][:, :], SA, None, ALU.mult))
    line(v.tensor_scalar(T["xs"][it.p][:, :], x, T["mv"][:, 0:1], T["rs"][:, :], ALU.subtract, ALU.mult), tag + "xs")


def pool_rstd(e, S, T, K, tag, it):
    S.wait(e, tag + "var", it)
    S.done(e.tensor_tensor(T["rstd"][:, :], T["ve"][:, :], K["mhalf"][:, :], ALU.pow), tag + "rstd")


def transposes(e, dst, src, ident, n):
    for j in range(n):
        last = e.transpose(dst[:, j, :], src[:, j * P:(j + 1) * P], ident)
    return last


def head_squares(line, v, S, tag, it, sq, ss):
    S.wait(v, tag + "sq", it)
    line(v.tensor_reduce(ss, sq.rearrange("p (h d) -> p h d", d=HD), AX.X, ALU.add))
    line(v.tensor_scalar(ss, ss, 1.0 / HD, EPS_RMS, ALU.mult, ALU.add), tag + "ms")


def head_scale(line, v, S, tag, it, p_raw, rr, out, scale):
    line(v.tensor_scalar(rr, rr, scale, None, ALU.mult))
    line(v.tensor_tensor(out.rearrange("p (h d) -> p h d", d=HD), p_raw.rearrange("p (h d) -> p h d", d=HD),
                         bcast(rr, [(1, NH), (0, HD)]), ALU.mult), tag + "n")


def part_pair(ap, first, step):
    return bass.AP(ap.tensor, ap.offset + first * HD, [list(ap.ap[0]), [4 * HD, NH], [step * HD, 2], [1, HD]])


def twice(ap):
    return bcast(ap, [(HD, NH), (0, 2), (1, HD)])


def key_stages(nc, S, sb, ps, mem, R, K, part):
    W = KD * D
    sq = sb(mem, "kysq", [P, D])
    ss = sb(mem, "kyss", [P, NH])
    rr = sb(mem, "kyrr", [P, NH])
    raw = [sb(mem, f"kyraw{i}", [P, D]) for i in range(2)]
    kn = [sb(mem, f"kykn{i}", [P, D]) for i in range(2)]
    kp = [sb(mem, f"kykp{i}", [P, 4 * D], f16) for i in range(2)]
    kt = [sb(mem, f"kykt{i}", [P, 4 * D], f16) for i in range(2)]
    vt = [sb(mem, f"kyvt{i}", [P, NH * (HD + 1)]) for i in range(2)]
    pK = ps(mem, "kypK", [P, D])
    pV = ps(mem, "kypV", [P, D])
    pT = ps(mem, "kypT", [P, NH // 2, P], f16)

    def sync(e):
        def store(it):
            S.wait(e, "kyvt", it)
            S.static(e)
            S.moved(e.dma_start(R["vst"][bass.ds(it.n, 1)].rearrange("a p c -> (a p) c"), vt[it.p][:, :]), "kyvout", it)
            S.wait(e, "kykt", it)
            S.static(e)
            S.moved(e.dma_start(R["kst"][bass.ds(it.n, 1)].rearrange("a p c -> (a p) c"), kt[it.p][:, :]), "kykout", it)
        return [(store, 7, 0, NT)]

    def scalar(e):
        def square(it):
            S.wait(e, "kyproj", it)
            S.wait(e, "kyn", it.back(2))
            S.done(e.activation(raw[it.p][:, :], pK[:, :], ACT.Copy, scale=1.0 / SW ** 2), "kyraw")
            S.wait(e, "kyms", it.back(1))
            S.done(e.activation(sq[:, :], pK[:, :], ACT.Square, scale=1.0 / SW ** 2), "kysq")

        def values(it):
            S.wait_moved(e, "kyvout", it.back(2))
            S.done(e.activation(vt[it.p][:, :].rearrange("p (h d) -> p h d", d=HD + 1)[:, :, 0:HD],
                                pV[:, :].rearrange("p (h d) -> p h d", d=HD), ACT.Copy, scale=1.0 / SW ** 2), "kyvt")

        def parts(it):
            S.wait(e, "kyn", it)
            S.wait(e, "kyT", it.back(2))
            S.done(e.activation(part_pair(kp[it.p][:, :], 0, 2), twice(kn[it.p][:, :]), ACT.Copy), "kyhi")

        def evacuate(it):
            S.wait(e, "kyT", it)
            S.wait_moved(e, "kykout", it.back(2))
            S.done(e.activation(kt[it.p][:, :], pT[:, :, :].rearrange("p j n -> p (j n)"), ACT.Copy), "kykt")
        return [(square, 4, 0, NT), (values, 4, 0, NT), (parts, 5, 0, NT), (evacuate, 6, 0, NT)]

    def gpsimd(e):
        def root(it):
            S.wait(e, "kyms", it)
            S.wait(e, "kyn", it.back(1))
            S.done(e.tensor_tensor(rr[:, :], ss[:, :], bcast(K["mhalf"][:, :], [(0, NH)]), ALU.pow), "kyrt")
        return [(root, 4, 0, NT)]

    def init(line, v):
        line(v.memset(vt[0][:, :], 1.0))
        line(v.memset(vt[1][:, :], 1.0), "ky_init")

    def vector(v):
        heads0, heads1, heads2 = (Line(S, v, f"kydve{i}") for i in range(3))

        def squares(it):
            heads0.start(it)
            S.wait(v, "kyrt", it.back(1))
            head_squares(heads0, v, S, "ky", it, sq[:, :], ss[:, :])

        def scale(it):
            heads1.start(it)
            S.wait(v, "kyhi", it.back(2))
            S.wait(v, "kyrt", it)
            S.wait(v, "kyraw", it)
            head_scale(heads1, v, S, "ky", it, raw[it.p][:, :], rr[:, :], kn[it.p][:, :], SA)

        def parts(it):
            heads2.start(it)
            S.wait(v, "kyhi", it)
            heads2(v.tensor_tensor(part_pair(kp[it.p][:, :], 1, 2), twice(kn[it.p][:, :]),
                                   bcast(kp[it.p][:, :], [(4 * HD, NH), (0, 2), (1, HD)]), ALU.subtract), "kylo")
        return [(squares, 4, 0, NT), (scale, 5, 0, NT), (parts, 5, 0, NT)]

    def tensor(e):
        def project(it):
            S.wait(e, "kyraw", it.back(1))
            S.wait(e, "kysq", it.back(1))
            S.wait(e, "kyvt", it.back(1))
            at = (it.n // 4) * W + (it.n % 4) * P
            for out, w in ((pK, part["wk"]), (pV, part["wv"])):
                terms = split_terms(part["ctx"], w, KD)
                for j, (x, y, k) in enumerate(terms):
                    last = e.matmul(out[:, :], x[:, bass.ds(at + k * D, P)], y[:, k * D:(k + 1) * D],
                                    start=j == 0, stop=j == len(terms) - 1)
            S.done(last, "kyproj")

        def turn(it):
            S.wait(e, "kylo", it)
            S.wait(e, "kykt", it.back(1))
            S.done(transposes(e, pT, kp[it.p], K["ident"][:, :], NH // 2), "kyT")
        return (turn, 6, 0, NT), (project, 3, 0, NT)
    return {"sync": sync, "scalar": scalar, "gpsimd": gpsimd, "init": init, "vector": vector, "tensor": tensor}


def phase_layer1(nc, S, sb, ps, a, R, K, part):
    with ExitStack() as mem:
        ch, cl = part["ctx"]
        idx = [sb(mem, f"l1idx{i}", [P, 1], i32) for i in range(2)]
        x = [sb(mem, f"l1x{i}", [P, D]) for i in range(2)]
        T = {"st": sb(mem, "l1st", [P, 6]), "mv": sb(mem, "l1mv", [P, 2]), "ve": sb(mem, "l1ve", [P, 1]),
             "rstd": sb(mem, "l1rstd", [P, 1]), "rs": sb(mem, "l1rs", [P, 1]),
             "xs": [sb(mem, f"l1xs{i}", [P, D]) for i in range(2)]}
        xhl = [sb(mem, f"l1xhl{i}", [P, 2 * D], f16) for i in range(2)]
        xT = [sb(mem, f"l1xT{i}", [P, 2 * KD, P], f16) for i in range(2)]
        sg = [sb(mem, f"l1sg{i}", [P, KD * P]) for i in range(2)]
        sq = [sb(mem, f"l1sq{i}", [P, KD * P]) for i in range(2)]
        h = [sb(mem, f"l1h{i}", [P, KD * P]) for i in range(2)]
        hh = [sb(mem, f"l1hh{i}", [P, KD * P], f16) for i in range(2)]
        hl = [sb(mem, f"l1hl{i}", [P, KD * P], f16) for i in range(2)]
        y = [sb(mem, f"l1y{i}", [P, D]) for i in range(2)]
        pT = ps(mem, "l1pT", [P, 2 * KD, P], f16)
        pP = [ps(mem, f"l1pP{i}", [P, KD * P]) for i in range(2)]
        pY = ps(mem, "l1pY", [P, D])
        W = KD * D
        keys = key_stages(nc, S, sb, ps, mem, R, K, part)
        blk = mem.enter_context(nc.Block())

        @blk.sync
        def _(e):
            def indices(it):
                S.wait_moved(e, "l1gather", it.back(2))
                S.static(e)
                S.moved(e.dma_start(idx[it.p][:, :], R["list1"][bass.ds(it.n * P, P), :]), "l1idx", it)

            def store(it):
                S.wait(e, "l1y", it)
                S.static(e)
                S.moved(e.dma_start(R["y1s"][bass.ds(it.n * P, P), :], y[it.p][:, :]), "l1store", it)
            pipeline(e, N1, [(indices, 0), (store, 6)] + keys["sync"](e))
            for p in range(2):
                S.wait_moved(e, "kyvout", It(NT // 2 - 1, p))
                S.wait_moved(e, "kykout", It(NT // 2 - 1, p))
                S.wait_moved(e, "l1store", It(N1 // 2 - 1, p))

        @blk.gpsimd
        def _(e):
            def gather(it):
                S.wait_moved(e, "l1idx", it)
                S.wait(e, "l1xs", it.back(2))
                S.static(e)
                S.moved(e.indirect_dma_start(
                    out=x[it.p][:, :], out_offset=None, in_=a["x"],
                    in_offset=bass.IndirectOffsetOnAxis(ap=idx[it.p][:, :], axis=0)), "l1gather", it)
            pipeline(e, N1, [(lambda it: pool_rstd(e, S, T, K, "l1", it), 1), (gather, 0)] + keys["gpsimd"](e))

        @blk.scalar
        def _(e):
            e.wait_ge(S.sem("ky_init"), 1)

            def yout(it):
                S.wait(e, "l1mm2", it)
                S.wait_moved(e, "l1store", it.back(2))
                S.done(e.activation(y[it.p][:, :], pY[:, :], ACT.Copy, scale=K["gate"][:, 4:5]), "l1y")

            def high(it):
                S.wait(e, "l1xs", it)
                S.wait(e, "l1T", it.back(2))
                S.done(e.activation(xhl[it.p][:, 0:D], T["xs"][it.p][:, :], ACT.Copy), "l1xh")

            def hidden(it):
                S.wait(e, "l1mm1", it)
                S.wait(e, "l1h", it.back(2))
                S.done(e.activation(sg[it.p][:, :], pP[it.p][:, :], ACT.Sigmoid, scale=UNSCALE), "l1sg")
                S.done(e.activation(sq[it.p][:, :], pP[it.p][:, :], ACT.Square, scale=UNSCALE * SA ** 0.5), "l1sq")
                S.wait(e, "l1h", it)
                S.wait(e, "l1mm2", it.back(2))
                S.done(e.activation(hh[it.p][:, :], h[it.p][:, :], ACT.Copy), "l1hh")
            square, values, parts, out = keys["scalar"](e)
            pipeline(e, N1, [(yout, 5), square, parts, (high, 1), values, out, (hidden, 3)])

        @blk.vector
        def _(v):
            init = Line(S, v, "kyinit")
            init.start(It(0, 0))
            keys["init"](init, v)
            stats, front, low, mid, back = (Line(S, v, f"l1dve{i}") for i in range(5))

            def spread(it):
                stats.start(it)
                S.wait_moved(v, "l1gather", it)
                row_stats(stats, v, S, T, x[it.p][:, :], "l1")

            def norm(it):
                front.start(it)
                normed(front, v, S, T, x[it.p][:, :], "l1", it)

            def parts(it):
                low.start(it)
                S.wait(v, "l1xh", it)
                low(v.tensor_tensor(xhl[it.p][:, D:], T["xs"][it.p][:, :], xhl[it.p][:, 0:D], ALU.subtract), "l1xl")

            def evacuate(it):
                mid.start(it)
                S.wait(v, "l1T", it)
                S.wait(v, "l1mm1", it.back(2))
                mid(v.tensor_copy(xT[it.p][:, :, :], pT[:, :, :]), "l1xT")

            def hidden(it):
                back.start(it)
                S.wait(v, "l1sq", it)
                S.wait(v, "l1hh", it.back(2))
                back(v.tensor_tensor(h[it.p][:, :], sg[it.p][:, :], sq[it.p][:, :], ALU.mult), "l1h")
                S.wait(v, "l1hh", it)
                back(v.tensor_tensor(hl[it.p][:, :], h[it.p][:, :], hh[it.p][:, :], ALU.subtract), "l1hl")
            squares, scale, klow = keys["vector"](v)
            pipeline(v, N1, [scale, (spread, 1), squares, (norm, 1), klow, (evacuate, 2), (parts, 1), (hidden, 3)])

        @blk.tensor
        def _(e):
            def up(it):
                ex = e.value_load(K["tab1"][0:1, bass.ds(it.n, 1)], min_val=0, max_val=E1 - 1)
                S.wait(e, "l1xT", it)
                S.wait(e, "l1sq", it.back(2))
                for f in range(KD):
                    terms = [(w, x0, k) for k in range(KD) for w, x0 in ((ch, 0), (ch, KD), (cl, 0))]
                    for j, (w, x0, k) in enumerate(terms):
                        last = e.matmul(pP[it.p][:, f * P:(f + 1) * P], w[:, bass.ds(ex * W + (k * D + f * P), P)],
                                        xT[it.p][:, x0 + k, :], start=j == 0, stop=j == len(terms) - 1)
                S.done(last, "l1mm1")

            def turn(it):
                S.wait(e, "l1xl", it)
                S.wait(e, "l1xT", it.back(1))
                S.done(transposes(e, pT, xhl[it.p], K["ident"][:, :], 2 * KD), "l1T")

            def down(it):
                ex = e.value_load(K["tab1"][0:1, bass.ds(it.n, 1)], min_val=0, max_val=E1 - 1)
                S.wait(e, "l1hl", it)
                S.wait(e, "l1y", it.back(1))
                terms = [(hx, w, k) for k in range(KD) for hx, w in ((hh, ch), (hh, cl), (hl, ch))]
                for j, (hx, w, k) in enumerate(terms):
                    last = e.matmul(pY[:, :], hx[it.p][:, k * P:(k + 1) * P], w[:, bass.ds(ex * W + k * D, D)],
                                    start=j == 0, stop=j == len(terms) - 1)
                S.done(last, "l1mm2")
            key_turn, key_project = keys["tensor"](e)
            pipeline(e, N1, [(turn, 2), (up, 3), key_turn, key_project, (down, 4)])


def split_terms(first, second, blocks):
    return [(x, w, k) for k in range(blocks) for x, w in ((first[0], second[0]), (first[0], second[1]), (first[1], second[0]))]


def phase_shared(nc, S, sb, ps, a, R, K):
    W1, W2 = KD * FF, FB * D
    with ExitStack() as mem:
        w1 = [sb(mem, f"shw1{i}", [P, NS * W1], f16) for i in range(2)]
        w2 = [sb(mem, f"shw2{i}", [P, NS * W2], f16) for i in range(2)]
        cen = [sb(mem, f"shcen{i}", [P, KD * NR], f16) for i in range(2)]
        stage = [sb(mem, f"shstage{i}", [P, W2]) for i in range(2)]
        b1r = sb(mem, "shb1r", [P, NS * FB])
        b1 = sb(mem, "shb1", [P, NS * FB])
        bias = sb(mem, "shbias", [P, NR])
        base = sb(mem, "shbase", [P, NR])
        pidx = [sb(mem, f"shpidx{i}", [P, 1], i32) for i in range(2)]
        tokb = [sb(mem, f"shtok{i}", [P, 1], i32) for i in range(2)]
        posb = [sb(mem, f"shposb{i}", [P, KR], i32) for i in range(2)]
        xin = [sb(mem, f"shxin{i}", [P, D]) for i in range(2)]
        y1 = [sb(mem, f"shy1{i}", [P, D]) for i in range(2)]
        x1 = [sb(mem, f"shx1{i}", [P, D]) for i in range(2)]
        r1 = sb(mem, "shr1", [P, NT * D])
        T = {"st": sb(mem, "shst", [P, 6]), "mv": sb(mem, "shmv", [P, 2]), "ve": sb(mem, "shve", [P, 1]),
             "rstd": sb(mem, "shrstd", [P, 1]), "rs": sb(mem, "shrs", [P, 1]),
             "xs": [sb(mem, f"shxs{i}", [P, D]) for i in range(2)]}
        xhl = [sb(mem, f"shxhl{i}", [P, 2 * D], f16) for i in range(2)]
        xT = [sb(mem, f"shxT{i}", [P, 2 * KD, P], f16) for i in range(2)]
        h = [sb(mem, f"shh{i}", [P, NS, FB * P]) for i in range(2)]
        hh = [sb(mem, f"shhh{i}", [P, NS, FB * P], f16) for i in range(2)]
        hl = [sb(mem, f"shhl{i}", [P, NS, FB * P], f16) for i in range(2)]
        xo = [sb(mem, f"shxo{i}", [P, D]) for i in range(2)]
        sig = [sb(mem, f"shsig{i}", [P, NR]) for i in range(2)]
        sc = sb(mem, "shsc", [P, NR])
        top = sb(mem, "shtop", [P, 8])
        ti = sb(mem, "shti", [P, 8], u32)
        tf = sb(mem, "shtf", [P, 8])
        oh = [sb(mem, f"shoh{i}", [P, KR, NR]) for i in range(2)]
        m = [sb(mem, f"shm{i}", [P, NR], f16) for i in range(2)]
        pos = sb(mem, "shpos", [P, NR])
        pk = sb(mem, "shpk", [P, KR, NR])
        pf = sb(mem, "shpf", [P, KR])
        pos2f = sb(mem, "shpos2f", [P, NT * KR])
        gs = sb(mem, "shgs", [P, 1])
        gr = sb(mem, "shgr", [P, 1])
        pT = [ps(mem, f"shpT{i}", [P, 2 * KD, P], f16) for i in range(2)]
        pH = [ps(mem, f"shpH{i}", [P, FB * P]) for i in range(NS)]
        pY = [ps(mem, f"shpY{i}", [P, D]) for i in range(2)]
        pR = ps(mem, "shpR", [P, NR])
        pC = ps(mem, "shpC", [P, 2, NR])
        jobs = [(a["sw1"][i], w1[0][:, i * W1:(i + 1) * W1], w1[1][:, i * W1:(i + 1) * W1], W1) for i in range(NS)]
        jobs += [(a["sw2"][i], w2[0][:, i * W2:(i + 1) * W2], w2[1][:, i * W2:(i + 1) * W2], W2) for i in range(NS)]
        jobs += [(a["cenT"], cen[0][:, :], cen[1][:, :], KD * NR)]
        blk = mem.enter_context(nc.Block())

        @blk.sync
        def _(e):
            load_split(S, e, None, None, jobs, stage, "sh")
            e.dma_start(b1r[:, :], a["sb1"]).then_inc(S.sem("sh_small"), 16)
            e.dma_start(bias[:, :], bass.AP(a["bias"].tensor, 0, [[0, P], [1, NR]])).then_inc(S.sem("sh_small"), 16)

            def load(it):
                S.wait(e, "shx1", it.back(2))
                S.static(e)
                S.moved(e.dma_start(xin[it.p][:, :], a["x"][bass.ds(it.n * P, P), :]), "shxin", it)

            def store_norm(it):
                S.wait(e, "shxl", it)
                S.static(e)
                S.moved(e.dma_start(R["xn2"][bass.ds(it.n * P, P), :], xhl[it.p][:, :]), "shxnout", it)

            def store(it):
                S.wait(e, "shxo", it)
                S.static(e)
                S.moved(e.dma_start(R["x2a"][bass.ds(it.n * P, P), :], xo[it.p][:, :]), "shstore", it)
            pipeline(e, NT, [(load, 0), (store_norm, 2), (store, 6)])
            for p in range(2):
                S.wait_moved(e, "shstore", It(NT // 2 - 1, p))
                S.wait_moved(e, "shxnout", It(NT // 2 - 1, p))

        @blk.gpsimd
        def _(e):
            def gather(it):
                S.wait_moved(e, "shgather", it.back(2))
                S.static(e)
                S.done(e.tensor_copy(pidx[it.p][:, :], K["pos1"][:, bass.ds(it.n, 1)]), "shpidx")
                S.wait(e, "shpidx", it)
                S.wait(e, "shx1", it.back(2))
                S.static(e)
                S.moved(e.indirect_dma_start(
                    out=y1[it.p][:, :], out_offset=None, in_=R["y1s"],
                    in_offset=bass.IndirectOffsetOnAxis(ap=pidx[it.p][:, :], axis=0)), "shgather", it)

            def scatter(it):
                S.wait_moved(e, "shscatter", it.back(2), KR)
                S.static(e)
                S.done(e.tensor_copy(tokb[it.p][:, :], K["tok"][:, bass.ds(it.n, 1)]), "shtokb")
                S.wait(e, "shtokb", it)
                S.wait(e, "shposb", it)
                S.static(e)
                for k in range(KR):
                    S.moved(e.indirect_dma_start(
                        out=R["list2"], out_offset=bass.IndirectOffsetOnAxis(ap=posb[it.p][:, k:k + 1], axis=0),
                        in_=tokb[it.p][:, :], in_offset=None), "shscatter", it)

            def first_residual(it):
                S.wait_moved(e, "shgather", it)
                S.wait_moved(e, "shxin", it)
                S.wait(e, "shr1", it.back(2))
                S.static(e)
                S.done(e.tensor_tensor(x1[it.p][:, :], y1[it.p][:, :], xin[it.p][:, :], ALU.add), "shx1")

            pipeline(e, NT, [(lambda it: pool_rstd(e, S, T, K, "sh", it), 2), (gather, 0),
                             (first_residual, 1), (scatter, 6)])
            for p in range(2):
                S.wait_moved(e, "shscatter", It(NT // 2 - 1, p), KR)

        @blk.scalar
        def _(e):
            load_split(S, None, e, None, jobs, stage, "sh")
            e.wait_ge(S.sem("sh_small"), 32)
            S.done(e.activation(b1[:, :], b1r[:, :], ACT.Copy, scale=SA), "sh_b1")
            e.wait_ge(S.sem("sh_b1"), 1)
            e.wait_ge(S.sem("sh_init"), 1)

            def high(it):
                S.wait(e, "shxs", it)
                S.wait(e, "shT", it.back(2))
                S.wait_moved(e, "shxnout", it.back(2))
                S.done(e.activation(xhl[it.p][:, 0:D], T["xs"][it.p][:, :], ACT.Copy), "shxh")

            def hidden(it):
                S.wait(e, "shrouted", it)
                S.done(e.activation(sig[it.p][:, :], pR[:, :], ACT.Sigmoid, scale=UNSCALE), "shsig")
                S.wait(e, "shup", it)
                S.wait(e, "shhl", it.back(2))
                for s in range(NS):
                    for f in range(FB):
                        n = FLAST if f == FB - 1 else P
                        last = e.activation(h[it.p][0:n, s, f * P:(f + 1) * P], pH[s][0:n, f * P:(f + 1) * P],
                                            ACT.Relu, bias=b1[0:n, s * FB + f:s * FB + f + 1], scale=UNSCALE * SA)
                S.done(last, "shh")
                S.wait(e, "shh", it)
                S.wait(e, "shdown", it.back(2))
                S.done(e.activation(hh[it.p][:, :, :], h[it.p][:, :, :], ACT.Copy), "shhh")
            pipeline(e, NT, [(high, 2), (hidden, 4)])

        @blk.vector
        def _(v):
            init = Line(S, v, "shinit")
            init.start(It(0, 0))
            for i in range(2):
                init(v.memset(h[i][FLAST:P, :, :], 0.0))
                init(v.memset(h[i][FLAST:FLAST + 1, :, 2 * P:], SA))
            init(v.tensor_scalar(base[:, :], K["iota"][:, :], float(CAP), None, ALU.mult))
            init(v.memset(sc[:, :], 0.0), "sh_init")
            load_split(S, None, None, v, jobs, stage, "sh")
            v.wait_ge(S.sem("sh_small"), 32)
            stats, front, low, mid, rt, back, last_, fin = (Line(S, v, f"shdve{i}") for i in range(8))

            def spread(it):
                stats.start(it)
                S.wait(v, "shx1", it)
                row_stats(stats, v, S, T, x1[it.p][:, :], "sh")

            def norm(it):
                front.start(it)
                normed(front, v, S, T, x1[it.p][:, :], "sh", it)
                front(v.scalar_tensor_tensor(r1[:, bass.ds(it.n * D, D)], T["xs"][it.p][:, :], K["gate"][:, 5:6],
                                             x1[it.p][:, :], ALU.mult, ALU.add), "shr1")

            def parts(it):
                low.start(it)
                S.wait(v, "shxh", it)
                low(v.tensor_tensor(xhl[it.p][:, D:], T["xs"][it.p][:, :], xhl[it.p][:, 0:D], ALU.subtract), "shxl")

            def evacuate(it):
                mid.start(it)
                S.wait(v, "shT", it)
                S.wait(v, "shup", it.back(2))
                mid(v.tensor_copy(xT[it.p][:, :, :], pT[it.p][:, :, :]), "shxT")

            def choose(it):
                rt.start(it)
                S.wait(v, "shsig", it)
                rt(v.tensor_tensor(sc[:, :], sig[it.p][:, :], bias[:, :], ALU.add))
                S.static(v)
                rt(v.max(top[:, :], sc[:, :]))
                S.static(v)
                rt(v.max_index(ti[:, :], top[:, :], sc[:, :]))
                rt(v.tensor_copy(tf[:, :], ti[:, :]))
                rt(v.tensor_tensor(oh[it.p][:, :, :], bcast(K["iota"][:, 0:1], [(0, KR), (1, NR)]),
                                   bcast(tf[:, 0:1], [(1, KR), (0, NR)]), ALU.is_equal))
                with nc.allow_low_precision(reason="sums of at most one one"):
                    rt(v.tensor_reduce(m[it.p][:, :], oh[it.p][:, :, :].rearrange("p k e -> p e k"), AX.X, ALU.add), "shm")
                rt(v.tensor_reduce(gs[:, :], top[:, 0:KR], AX.X, ALU.add))
                rt(v.tensor_scalar(gs[:, :], gs[:, :], 1e-8, None, ALU.max))
                rt(v.reciprocal(gr[:, :], gs[:, :]))
                rt(v.tensor_scalar(K["g2f"][:, bass.ds(it.n * KR, KR)], top[:, 0:KR],
                                   gr[:, :], K["gate"][:, 1:2], ALU.mult, ALU.mult))

            def place(it):
                last_.start(it)
                S.wait(v, "shcount", it)
                last_(v.tensor_tensor(pos[:, :], pC[:, 0, :], base[:, :], ALU.add))
                last_(v.tensor_tensor(base[:, :], pC[:, 1, :], base[:, :], ALU.add), "shbase")
                last_(v.tensor_tensor(pk[:, :, :], oh[it.p][:, :, :], bcast(pos[:, 0:1], [(0, KR), (1, NR)]), ALU.mult))
                last_(v.tensor_reduce(pf[:, :], pk[:, :, :], AX.X, ALU.add))
                last_(v.tensor_copy(pos2f[:, bass.ds(it.n * KR, KR)], pf[:, :]))
                S.wait_moved(v, "shscatter", it.back(2), KR)
                last_(v.tensor_copy(posb[it.p][:, :], pf[:, :]), "shposb")

            def hidden(it):
                back.start(it)
                S.wait(v, "shhh", it)
                S.wait(v, "shdown", it.back(2))
                back(v.tensor_tensor(hl[it.p][:, :, :], h[it.p][:, :, :], hh[it.p][:, :, :], ALU.subtract), "shhl")

            def finish(it):
                fin.start(it)
                S.wait(v, "shdown", it)
                S.wait_moved(v, "shstore", it.back(2))
                fin(v.scalar_tensor_tensor(xo[it.p][:, :], pY[it.p][:, :], K["gate"][:, 6:7], r1[:, bass.ds(it.n * D, D)],
                                           ALU.mult, ALU.add), "shxo")
            pipeline(v, NT, [(spread, 2), (finish, 6), (norm, 2), (evacuate, 3), (place, 5), (parts, 2),
                             (choose, 4), (hidden, 4)])
            v.wait_ge(S.sem("shbase"), NT)
            tail = Line(S, v, "shtail")
            tail.start(It(0, 0))
            cnt = sb(mem, "shcnt", [P, NR])
            tail(v.scalar_tensor_tensor(cnt[:, :], K["iota"][:, :], -float(CAP), base[:, :], ALU.mult, ALU.add))
            make_table(tail, v, mem, sb, "t2", NR, N2, cnt[:, :], K, K["tab2"][0:1, 0, :], K["tab2"][0:1, 1, :],
                       pos2f[:, :], K["pos2"][:, :])

        @blk.tensor
        def _(e):
            e.wait_ge(S.sem("shlo"), len(jobs))

            def up(it):
                S.wait(e, "shxT", it)
                S.wait(e, "shsig", it.back(1))
                xs = (xT[it.p][:, 0:KD, :], xT[it.p][:, KD:, :])
                terms = split_terms(xs, cen, KD)
                for j, (x, w, k) in enumerate(terms):
                    last = e.matmul(pR[:, :], x[:, k, :], w[:, k * NR:(k + 1) * NR], start=j == 0, stop=j == len(terms) - 1)
                S.done(last, "shrouted")
                S.wait(e, "shh", it.back(1))
                for s in range(NS):
                    for f in range(FB):
                        n = FLAST if f == FB - 1 else P
                        terms = split_terms(w1, xs, KD)
                        for j, (w, x, k) in enumerate(terms):
                            o = s * W1 + k * FF + f * P
                            last = e.matmul(pH[s][0:n, f * P:(f + 1) * P], w[:, o:o + n], x[:, k, :],
                                            start=j == 0, stop=j == len(terms) - 1)
                S.done(last, "shup")

            def turn(it):
                S.wait(e, "shxl", it)
                S.wait(e, "shxT", it.back(2))
                S.done(transposes(e, pT[it.p], xhl[it.p], K["ident"][:, :], 2 * KD), "shT")

            def down(it):
                S.wait(e, "shhl", it)
                S.wait(e, "shxo", it.back(2))
                terms = [(x, w, k, s) for s in range(NS) for x, w, k in split_terms((hh[it.p], hl[it.p]), w2, FB)]
                for j, (x, w, k, s) in enumerate(terms):
                    n = FLAST + 1 if k == FB - 1 else P
                    last = e.matmul(pY[it.p][:, :], x[0:n, s, k * P:(k + 1) * P], w[0:n, s * W2 + k * D:s * W2 + (k + 1) * D],
                                    start=j == 0, stop=j == len(terms) - 1)
                S.done(last, "shdown")

            def count(it):
                S.wait(e, "shm", it)
                S.wait(e, "shbase", it.back(1))
                e.matmul(pC[:, 0, :], K["tri"][:, :], m[it.p][:, :], start=True, stop=True)
                S.done(e.matmul(pC[:, 1, :], K["ones"][:, :], m[it.p][:, :], start=True, stop=True), "shcount")
            pipeline(e, NT, [(turn, 3), (count, 5), (up, 4), (down, 5)])


def phase_routed(nc, S, sb, ps, a, R, K):
    W1, W2 = KD * FF, FB * D
    EW = 2 * (W1 + W2)
    with ExitStack() as mem:
        wt = sb(mem, "rowt", [P, NR * EW], f16)
        raw = wt[:, :].bitcast(f32)
        b1 = sb(mem, "rob1", [P, NR * FB])
        piece = [sb(mem, f"ropiece{i}", [P, W2 // 2]) for i in range(2)]
        last_row = R["list2"].shape[0] - P
        direct = NR - 2
        pieces = [("rw1", W1 // 2, c, c, W1) for c in (0, W1 // 2)] + [("rw2", W2 // 2, c, 2 * W1 + c, W2) for c in (0, W2 // 2)]
        idx = [sb(mem, f"roidx{i}", [P, 1], i32) for i in range(2)]
        xg = [sb(mem, f"roxg{i}", [P, 2 * D], f16) for i in range(2)]
        xT = [sb(mem, f"roxT{i}", [P, 2 * KD, P], f16) for i in range(2)]
        h = sb(mem, "roh", [P, FB * P])
        hh = [sb(mem, f"rohh{i}", [P, FB * P], f16) for i in range(2)]
        hl = [sb(mem, f"rohl{i}", [P, FB * P], f16) for i in range(2)]
        y = sb(mem, "roy", [P, D])
        pT = [ps(mem, f"ropT{i}", [P, 2 * KD, P], f16) for i in range(2)]
        pH = [ps(mem, f"ropH{i}", [P, FB * P]) for i in range(2)]
        pY = [ps(mem, f"ropY{i}", [P, D]) for i in range(2)]
        halves = ((0, 0, W1), (2 * W1, W1, W2))
        blk = mem.enter_context(nc.Block())

        def expert(n):
            return n * EW, (n + 2) * (EW // 2)

        @blk.sync
        def _(e):
            def weights(n, it):
                at = expert(n)[1]
                S.wait(e, "rohi", it.back(2), 2)
                S.moved(e.dma_start(raw[:, bass.ds(at, W1)], a["rw1"][bass.ds(n, 1)].rearrange("e p c -> (e p) c")), "roraw", it)
                S.moved(e.dma_start(raw[:, bass.ds(at + W1, W2)], a["rw2"][bass.ds(n, 1)].rearrange("e p c -> (e p) c")), "roraw", it)

            def small(it):
                for j, (src, cols, at, _, _) in enumerate(pieces):
                    n = (it.n - direct) * 4 + j
                    if n >= 2:
                        e.wait_ge(S.sem("ropl"), n - 1)
                    e.dma_start(piece[j % 2][:, 0:cols], a[src][it.n][:, at:at + cols]).then_inc(S.sem(f"ropiece{j % 2}"), 16)

            def indices(it):
                row = e.value_load(K["tab2"][0:1, 1, bass.ds(it.n, 1)], min_val=0, max_val=last_row)
                S.wait_moved(e, "rogather", it.back(2))
                S.static(e)
                S.moved(e.dma_start(idx[it.p][:, :], R["list2"][bass.ds(row, P), :]), "roidx", it)

            def store(it):
                S.wait(e, "roy", it)
                S.static(e)
                S.moved(e.dma_start(R["ys"][bass.ds(it.n * P, P), :], y[:, :]), "rostore", it)
            ahead = 2
            weights(0, It(0, 0))
            e.dma_start(b1[:, :], a["rb1"]).then_inc(S.sem("ro_b1"), 16)
            for n in range(1, ahead):
                weights(n, It(n // 2, n % 2))
            pipeline(e, N2, [(indices, 0), (store, 5), (lambda it: weights(it.n, it), -ahead, ahead, direct), (small, 0, direct, NR)])
            for p in range(2):
                S.wait_moved(e, "rostore", It(N2 // 2 - 1, p))

        @blk.gpsimd
        def _(e):
            def gather(it):
                S.wait_moved(e, "roidx", it)
                S.wait(e, "roT", it.back(2))
                S.static(e)
                S.moved(e.indirect_dma_start(
                    out=xg[it.p][:, :], out_offset=None, in_=R["xn2"],
                    in_offset=bass.IndirectOffsetOnAxis(ap=idx[it.p][:, :], axis=0)), "rogather", it)
            pipeline(e, N2, [(gather, 0)])

        @blk.scalar
        def _(e):
            e.wait_ge(S.sem("ro_init"), 1)

            def high(it):
                S.wait_moved(e, "roraw", it, 2)
                S.wait(e, "rolo", it.back(2), 2)
                to, at = expert(it.n)
                S.static(e)
                for o, x, cols in halves:
                    S.done(e.activation(wt[:, bass.ds(to + o, cols)], raw[:, bass.ds(at + x, cols)], ACT.Copy, scale=SW), "rohi")

            def small(it):
                for j, (src, cols, at, o, _) in enumerate(pieces):
                    n = (it.n - direct) * 4 + j
                    e.wait_ge(S.sem(f"ropiece{j % 2}"), 16 * (n // 2 + 1))
                    if n == 0 or n == 4:
                        e.wait_ge(S.sem("rolo"), 2 * (it.n - 1))
                    S.done(e.activation(wt[:, it.n * EW + o:it.n * EW + o + cols], piece[j % 2][:, 0:cols], ACT.Copy, scale=SW), "roph")

            def yout(it):
                S.wait(e, "rodown", it)
                S.wait_moved(e, "rostore", it.back(1))
                S.done(e.activation(y[:, :], pY[it.p][:, :], ACT.Copy, scale=UNSCALE), "roy")

            def hidden(it):
                ex = e.value_load(K["tab2"][0:1, 0, bass.ds(it.n, 1)], min_val=0, max_val=NR - 1)
                S.wait(e, "roup", it)
                S.wait(e, "rohl", it.back(1))
                S.static(e)
                for f in range(FB):
                    n = FLAST if f == FB - 1 else P
                    last = e.activation(h[0:n, f * P:(f + 1) * P], pH[it.p][0:n, f * P:(f + 1) * P],
                                        ACT.Relu, bias=b1[0:n, bass.ds(ex * FB + f, 1)], scale=UNSCALE * SA)
                S.done(last, "roh")
                S.wait(e, "roh", it)
                S.wait(e, "rodown", it.back(2))
                S.done(e.activation(hh[it.p][:, :], h[:, :], ACT.Copy), "rohh")
            pipeline(e, N2, [(yout, 5), (hidden, 3), (high, 0, 0, direct), (small, 0, direct, NR)])

        @blk.vector
        def _(v):
            init = Line(S, v, "roinit")
            init.start(It(0, 0))
            init(v.memset(h[FLAST:P, :], 0.0))
            init(v.memset(h[FLAST:FLAST + 1, 2 * P:], SA))
            v.wait_ge(S.sem("ro_b1"), 16)
            init(v.tensor_scalar(b1[:, :], b1[:, :], SA, None, ALU.mult), "ro_init")
            mid, back = (Line(S, v, f"rodve{i}") for i in range(2))

            def evacuate(it):
                mid.start(it)
                S.wait(v, "roT", it)
                S.wait(v, "roup", it.back(2))
                mid(v.tensor_copy(xT[it.p][:, :, :], pT[it.p][:, :, :]), "roxT")

            def hidden(it):
                back.start(it)
                S.wait(v, "rohh", it)
                back(v.tensor_tensor(hl[it.p][:, :], h[:, :], hh[it.p][:, :], ALU.subtract), "rohl")

            def low(it):
                to, at = expert(it.n)
                for i, (o, x, cols) in enumerate(halves):
                    v.wait_ge(S.sem("rohi"), it.n * 2 + i + 1)
                    S.done(v.scalar_tensor_tensor(wt[:, bass.ds(to + o + cols, cols)], raw[:, bass.ds(at + x, cols)], SW,
                                                  wt[:, bass.ds(to + o, cols)], ALU.mult, ALU.subtract), "rolo")

            def small(it):
                for j, (src, cols, at, o, half) in enumerate(pieces):
                    v.wait_ge(S.sem("roph"), (it.n - direct) * 4 + j + 1)
                    o = it.n * EW + o
                    last = v.scalar_tensor_tensor(wt[:, o + half:o + half + cols], piece[j % 2][:, 0:cols], SW,
                                                  wt[:, o:o + cols], ALU.mult, ALU.subtract)
                    S.done(last, "ropl")
            pipeline(v, N2, [(evacuate, 2), (hidden, 3), (low, 0, 0, direct), (small, 0, direct, NR)])

        @blk.tensor
        def _(e):
            ex = {}

            def look(it):
                for name, tile in (("up", it), ("down", it.back(1))):
                    if not isinstance(tile.n, int) or 0 <= tile.n < N2:
                        ex[name] = e.value_load(K["tab2"][0:1, 0, bass.ds(tile.n, 1)], min_val=0, max_val=NR - 1)

            def ready(it):
                S.wait(e, "rolo", it, 2)

            def small_ready(it):
                e.wait_ge(S.sem("ropl"), 4 * (it.n - direct + 1))

            def up(it):
                S.wait(e, "roxT", it)
                S.wait(e, "roh", it.back(2))
                xs = (xT[it.p][:, 0:KD, :], xT[it.p][:, KD:, :])
                for f in range(FB):
                    n = FLAST if f == FB - 1 else P
                    terms = split_terms((0, W1), xs, KD)
                    for j, (w, x, k) in enumerate(terms):
                        last = e.matmul(pH[it.p][0:n, f * P:(f + 1) * P], wt[:, bass.ds(ex["up"] * EW + (w + k * FF + f * P), n)],
                                        x[:, k, :], start=j == 0, stop=j == len(terms) - 1)
                S.done(last, "roup")

            def turn(it):
                S.wait_moved(e, "rogather", it)
                S.wait(e, "roxT", it.back(2))
                S.done(transposes(e, pT[it.p], xg[it.p], K["ident"][:, :], 2 * KD), "roT")

            def down(it):
                S.wait(e, "rohl", it)
                S.wait(e, "roy", it.back(2))
                terms = split_terms((hh[it.p], hl[it.p]), (0, W2), FB)
                for j, (x, w, k) in enumerate(terms):
                    n = FLAST + 1 if k == FB - 1 else P
                    last = e.matmul(pY[it.p][:, :], x[0:n, k * P:(k + 1) * P],
                                    wt[0:n, bass.ds(ex["down"] * EW + (2 * W1 + w + k * D), D)],
                                    start=j == 0, stop=j == len(terms) - 1)
                S.done(last, "rodown")
            pipeline(e, N2, [(look, 3, 0, N2 + 1), (turn, 2), (ready, 3, 0, direct), (small_ready, 3, direct, NR), (up, 3), (down, 4)],
                     unroll=4)


def phase_queries(nc, S, sb, ps, a, R, K):
    W = KD * D
    with ExitStack() as mem:
        wq = [sb(mem, f"quw{i}", [P, W], f16) for i in range(2)]
        stage = [sb(mem, f"qustage{i}", [P, W]) for i in range(2)]
        pidx = [sb(mem, f"qupidx{i}", [P, KR], i32) for i in range(2)]
        xin = [sb(mem, f"quxin{i}", [P, D]) for i in range(2)]
        yg = [sb(mem, f"quyg{i}", [P, KR, D]) for i in range(2)]
        x2 = [sb(mem, f"qux2{i}", [P, D]) for i in range(2)]
        T = {"st": sb(mem, "qust", [P, 6]), "mv": sb(mem, "qumv", [P, 2]), "ve": sb(mem, "quve", [P, 1]),
             "rstd": sb(mem, "qurstd", [P, 1]), "rs": sb(mem, "qurs", [P, 1]),
             "xs": [sb(mem, f"quxs{i}", [P, D]) for i in range(2)]}
        xhl = [sb(mem, f"quxhl{i}", [P, 2 * D], f16) for i in range(2)]
        xT = [sb(mem, f"quxT{i}", [P, 2 * KD, P], f16) for i in range(2)]
        sq = sb(mem, "qusq", [P, D])
        ss = sb(mem, "quss", [P, NH])
        rr = sb(mem, "qurr", [P, NH])
        qn = [sb(mem, f"quqn{i}", [P, D]) for i in range(2)]
        qp = [sb(mem, f"quqp{i}", [P, 4 * D], f16) for i in range(2)]
        qt = [sb(mem, f"quqt{i}", [P, 4 * D], f16) for i in range(2)]
        pT = [ps(mem, f"qupT{i}", [P, 2 * KD, P], f16) for i in range(2)]
        pQ = [ps(mem, f"qupQ{i}", [P, D]) for i in range(2)]
        pS = [ps(mem, f"qupS{i}", [P, NH // 2, P], f16) for i in range(2)]
        jobs = [(a["wqT"], wq[0][:, :], wq[1][:, :], W)]
        blk = mem.enter_context(nc.Block())

        @blk.sync
        def _(e):
            load_split(S, e, None, None, jobs, stage, "qw")

            def load(it):
                S.wait(e, "qux2", it.back(2))
                S.static(e)
                S.moved(e.dma_start(xin[it.p][:, :], R["x2a"][bass.ds(it.n * P, P), :]), "quxin", it)

            def store_x(it):
                S.wait(e, "qux2", it)
                S.static(e)
                S.moved(e.dma_start(R["x2"][bass.ds(it.n * P, P), :], x2[it.p][:, :]), "quxout", it)

            def store(it):
                S.wait(e, "quqt", it)
                S.static(e)
                S.moved(e.dma_start(R["qst"][bass.ds(it.n, 1)].rearrange("a p c -> (a p) c"), qt[it.p][:, :]), "ququt", it)
            pipeline(e, NT, [(load, 0), (store_x, 1), (store, 6)])
            for p in range(2):
                S.wait_moved(e, "quxout", It(NT // 2 - 1, p))
                S.wait_moved(e, "ququt", It(NT // 2 - 1, p))

        @blk.gpsimd
        def _(e):
            def gather(it):
                S.wait_moved(e, "qugather", it.back(2), KR)
                S.wait(e, "qux2", it.back(2))
                S.static(e)
                S.done(e.tensor_copy(pidx[it.p][:, :], K["pos2"][:, bass.ds(it.n * KR, KR)]), "qupidx")
                S.wait(e, "qupidx", it)
                S.static(e)
                for k in range(KR):
                    S.moved(e.indirect_dma_start(
                        out=yg[it.p][:, k, :], out_offset=None, in_=R["ys"],
                        in_offset=bass.IndirectOffsetOnAxis(ap=pidx[it.p][:, k:k + 1], axis=0)), "qugather", it)
            pipeline(e, NT, [(lambda it: pool_rstd(e, S, T, K, "qu", it), 2), (gather, 0)])

        @blk.scalar
        def _(e):
            load_split(S, None, e, None, jobs, stage, "qw")

            def high(it):
                S.wait(e, "quxs", it)
                S.wait(e, "quT", it.back(2))
                S.done(e.activation(xhl[it.p][:, 0:D], T["xs"][it.p][:, :], ACT.Copy), "quxh")

            def square(it):
                S.wait(e, "quproj", it)
                S.wait(e, "qrms", it.back(1))
                S.done(e.activation(sq[:, :], pQ[it.p][:, :], ACT.Square, scale=UNSCALE), "qrsq")

            def root(it):
                S.wait(e, "qrms", it)
                S.done(e.activation(ss[:, :], ss[:, :], ACT.Sqrt), "qrrt")

            def parts(it):
                S.wait(e, "qrn", it)
                S.wait(e, "quS", it.back(2))
                S.done(e.activation(part_pair(qp[it.p][:, :], 0, 1), twice(qn[it.p][:, :]), ACT.Copy), "quhi")

            def evacuate(it):
                S.wait(e, "quS", it)
                S.wait_moved(e, "ququt", it.back(2))
                S.done(e.activation(qt[it.p][:, :], pS[it.p][:, :, :].rearrange("p j n -> p (j n)"), ACT.Copy), "quqt")
            pipeline(e, NT, [(square, 5), (root, 5), (high, 2), (parts, 5), (evacuate, 6)])

        @blk.vector
        def _(v):
            load_split(S, None, None, v, jobs, stage, "qw")
            sum_, stats, front, low, mid, heads0, heads1, heads2 = (Line(S, v, f"qudve{i}") for i in range(8))

            def combine(it):
                sum_.start(it)
                S.wait_moved(v, "qugather", it, KR)
                S.wait_moved(v, "quxin", it)
                S.wait_moved(v, "quxout", it.back(2))
                for k in range(KR):
                    sum_(v.scalar_tensor_tensor(x2[it.p][:, :], yg[it.p][:, k, :], K["g2f"][:, bass.ds(it.n * KR + k, 1)],
                                                (xin if k == 0 else x2)[it.p][:, :], ALU.mult, ALU.add),
                         "qux2" if k == KR - 1 else None)

            def spread(it):
                stats.start(it)
                S.wait(v, "qux2", it)
                row_stats(stats, v, S, T, x2[it.p][:, :], "qu")

            def norm(it):
                front.start(it)
                normed(front, v, S, T, x2[it.p][:, :], "qu", it)

            def split(it):
                low.start(it)
                S.wait(v, "quxh", it)
                low(v.tensor_tensor(xhl[it.p][:, D:], T["xs"][it.p][:, :], xhl[it.p][:, 0:D], ALU.subtract), "quxl")

            def evacuate(it):
                mid.start(it)
                S.wait(v, "quT", it)
                S.wait(v, "quproj", it.back(2))
                mid(v.tensor_copy(xT[it.p][:, :, :], pT[it.p][:, :, :]), "quxT")

            def squares(it):
                heads0.start(it)
                head_squares(heads0, v, S, "qr", it, sq[:, :], ss[:, :])

            def scale(it):
                heads1.start(it)
                S.wait(v, "quhi", it.back(2))
                S.wait(v, "qrrt", it)
                heads1(v.reciprocal(rr[:, :], ss[:, :]))
                head_scale(heads1, v, S, "qr", it, pQ[it.p][:, :], rr[:, :], qn[it.p][:, :], SA * UNSCALE)

            def parts(it):
                heads2.start(it)
                S.wait(v, "quhi", it)
                heads2(v.tensor_tensor(part_pair(qp[it.p][:, :], 2, 1), twice(qn[it.p][:, :]),
                                       bcast(qp[it.p][:, :], [(4 * HD, NH), (0, 2), (1, HD)]), ALU.subtract), "qulo")
            pipeline(v, NT, [(spread, 2), (squares, 5), (norm, 2), (scale, 5), (evacuate, 3), (split, 2), (parts, 5),
                             (combine, 1)])

        @blk.tensor
        def _(e):
            e.wait_ge(S.sem("qwlo"), len(jobs))

            def project(it):
                S.wait(e, "quxT", it)
                S.wait(e, "qrn", it.back(2))
                terms = split_terms((xT[it.p][:, 0:KD, :], xT[it.p][:, KD:, :]), wq, KD)
                for j, (x, w, k) in enumerate(terms):
                    last = e.matmul(pQ[it.p][:, :], x[:, k, :], w[:, k * D:(k + 1) * D],
                                    start=j == 0, stop=j == len(terms) - 1)
                S.done(last, "quproj")

            def turn(it):
                S.wait(e, "quxl", it)
                S.wait(e, "quxT", it.back(2))
                S.done(transposes(e, pT[it.p], xhl[it.p], K["ident"][:, :], 2 * KD), "quT")

            def stack(it):
                S.wait(e, "qulo", it)
                S.wait(e, "quqt", it.back(2))
                S.done(transposes(e, pS[it.p], qp[it.p], K["ident"][:, :], NH // 2), "quS")
            pipeline(e, NT, [(turn, 3), (project, 4), (stack, 6)])


def phase_attention(nc, S, sb, ps, a, R, K, out):
    G = NH // 4
    NG = BATCH * G
    with ExitStack() as keep:
        o = sb(keep, "o", [P, NT * D])
        ident = sb(keep, "ident32", [P, P])
        with ExitStack() as mem:
            q = [sb(mem, f"atq{i}", [P, 4, 2, P], f16) for i in range(2)]
            k = [sb(mem, f"atk{i}", [P, 4, 2, 2, P], f16) for i in range(2)]
            vv = [sb(mem, f"atv{i}", [P, 4, 4 * (HD + 1)]) for i in range(2)]
            pr = [sb(mem, f"atp{i}", [P, 2 * SEQ]) for i in range(4)]
            oT = [sb(mem, f"atoT{i}", [P, SEQ]) for i in range(2)]
            rc = sb(mem, "atrc", [P, 4, 4])
            pS = [ps(mem, f"atpS{i}", [P, 2 * SEQ]) for i in range(2)]
            pO = [ps(mem, f"atpO{i}", [P, SEQ]) for i in range(2)]
            pX = ps(mem, "atpX", [P, 4, P])
            blk = mem.enter_context(nc.Block())

            @blk.sync
            def _(e):
                e.dma_start(ident[:, :], a["c_ident32"]).then_inc(S.sem("at_ident"), 16)
                e.wait_ge(S.sem("at_init"), 1)

                def load(it):
                    b, g = it.n // G, it.n % G
                    S.wait(e, "atqk", it.back(2), 8)
                    S.wait(e, "atpv", it.back(2), 4)
                    S.static(e)
                    tiles = R["qst"].rearrange("(b t) p c -> b p t c", b=BATCH)
                    S.moved(e.dma_start(q[it.p][:, :, :, :].rearrange("p t j n -> p t (j n)"),
                                        tiles[bass.ds(b, 1), :, :, bass.ds(g * 2 * P, 2 * P)].rearrange("b p t c -> (b p) t c")),
                            "atin", it)
                    tiles = R["kst"].rearrange("(b t) p c -> b p t c", b=BATCH)
                    for s in range(2):
                        r = slice(64 * s, 64 * s + 64)
                        S.moved(e.dma_start(k[it.p][r, :, s, :, :].rearrange("p t j n -> p t (j n)"),
                                            tiles[bass.ds(b, 1), r, :, bass.ds(g * 2 * P, 2 * P)].rearrange("b p t c -> (b p) t c")),
                                "atin", it)
                    tiles = R["vst"].rearrange("(b t) p c -> b p t c", b=BATCH)
                    V = 4 * (HD + 1)
                    S.moved(e.dma_start(vv[it.p][:, :, :], tiles[bass.ds(b, 1), :, :, bass.ds(g * V, V)].rearrange("b p t c -> (b p) t c")),
                            "atin", it)
                pipeline(e, NG, [(load, 0)])

            @blk.tensor
            def _(e):
                e.wait_ge(S.sem("at_ident"), 16)

                def scores(it, m):
                    for j in range(2):
                        u = 2 * m + j
                        if not isinstance(it.n, int) or it.n * 8 + u >= 2:
                            e.wait_ge(S.sem("atexp"), it.n * 8 + (u - 1))
                        for s in range(2):
                            last = e.matmul(pS[j][:, s * SEQ:(s + 1) * SEQ], k[it.p][:, m, s, j, :],
                                            q[it.p][:, :, j, :], start=True, stop=True)
                        S.done(last, "atqk")

                def weigh(it, m):
                    e.wait_ge(S.sem("atexp"), it.n * 8 + (2 * m + 2))
                    if m == 0:
                        S.wait(e, "atoT", it.back(2))
                    for i in range(4):
                        n = HD + 1
                        last = e.matmul(pO[it.p][32 * i:32 * i + n, :], vv[it.p][:, m, i * n:(i + 1) * n],
                                        pr[(2 * m + i // 2) % 4][:, (i % 2) * SEQ:(i % 2 + 1) * SEQ],
                                        start=m == 0, stop=m == 3)
                    S.done(last, "atpv")

                def first(it):
                    S.wait_moved(e, "atin", it, 4)
                    scores(it, 0)

                def rest(it):
                    for m in range(1, 4):
                        scores(it, m)
                        weigh(it, m - 1)

                def turn(it):
                    S.wait(e, "atoT", it)
                    S.wait(e, "ato", it.back(1))
                    for t in range(4):
                        last = e.transpose(pX[:, t, :], oT[it.p][:, t * P:(t + 1) * P], ident[:, :])
                    S.done(last, "atX")
                pipeline(e, NG, [(first, 1), (lambda it: weigh(it, 3), 2), (rest, 1), (turn, 2)])

            @blk.scalar
            def _(e):
                def exps(it):
                    for u in range(8):
                        e.wait_ge(S.sem("atqk"), it.n * 8 + (u + 1))
                        if not isinstance(it.n, int) or it.n * 4 + u // 2 >= 2:
                            e.wait_ge(S.sem("atpv"), it.n * 4 + (u // 2 - 1))
                        S.done(e.activation(pr[u % 4][:, :], pS[u % 2][:, :], ACT.Exp, scale=HD ** -0.5 / SA ** 2), "atexp")
                pipeline(e, NG, [(exps, 1)])

            @blk.vector
            def _(v):
                init = Line(S, v, "atinit")
                init.start(It(0, 0))
                for i in range(2):
                    init(v.memset(k[i][:, :, :, :, :].rearrange("p t s j n -> p (t s j n)"), 0.0))
                    init(v.memset(pO[i][:, :], 0.0), "at_init" if i else None)
                line = Line(S, v, "atdve")

                def into(b, g):
                    x = o[:, :].rearrange("p (b t h c) -> p b t h c", b=BATCH, t=4, h=G)
                    return x[:, bass.ds(b, 1), :, bass.ds(g, 1), :].rearrange("p b t h (i d) -> p (b t) (h i) d", i=4)

                def evacuate(it):
                    v.wait_ge(S.sem("atpv"), it.n * 4 + 4)
                    S.wait(v, "atX", it.back(2))
                    S.done(v.tensor_copy(oT[it.p][:, :], pO[it.p][:, :]), "atoT")

                def normalise(it):
                    line.start(it)
                    b, g = it.n // G, it.n % G
                    S.wait(v, "atX", it)
                    x = pX[:, 0, 0:1]
                    line(v.reciprocal(rc[:, :, :], bass.AP(x.tensor, x.offset + HD, [list(x.ap[0]), [P, 4], [32, 4]])))
                    line(v.tensor_tensor(
                        into(b, g), bass.AP(x.tensor, x.offset, [list(x.ap[0]), [P, 4], [32, 4], [1, HD]]),
                        bcast(rc[:, 0, 0:1], [(4, 4), (1, 4), (0, HD)]), ALU.mult), "ato")
                pipeline(v, NG, [(evacuate, 2), (normalise, 2)])

        phase_last(nc, S, sb, ps, a, R, K, o, ident, out)


def phase_last(nc, S, sb, ps, a, R, K, o, ident, out):
    BIG = 1e30
    with ExitStack() as mem:
        sl = sb(mem, "lasl", [NTILE, DSL * GRID])
        ssum = sb(mem, "lassum", [NTILE, DSL])
        ssg = sb(mem, "lassg", [NTILE, DSL])
        sgn = sb(mem, "lasgn", [P, D])
        gam = sb(mem, "lagam", [P, D])
        bet = sb(mem, "labet", [P, D])
        tab = sb(mem, "latab", [P, 2 * DSL * GRID + 1])
        xin = [sb(mem, f"laxin{i}", [P, D]) for i in range(2)]
        x3 = sb(mem, "lax3", [P, D])
        z = sb(mem, "laz", [P, D])
        xf = [sb(mem, f"laxf{i}", [P, D]) for i in range(2)]
        sg = [sb(mem, f"lasg{i}", [P, D]) for i in range(2)]
        st, mv = sb(mem, "last", [P, 6]), sb(mem, "lamv", [P, 2])
        ve, rstd = sb(mem, "lave", [P, 1]), sb(mem, "larstd", [P, 1])
        ve2, rstd2 = sb(mem, "lave2", [P, 1]), sb(mem, "larstd2", [P, 1])
        ts, cs = sb(mem, "lats", [P, NTILE]), sb(mem, "lacs", [P, NCL])
        key, best = sb(mem, "lakey", [P, NTILE]), sb(mem, "labest", [P, 1])
        oh = sb(mem, "laoh", [P, NT * NTILE])
        oh16 = sb(mem, "laoh16", [P, NT * NTILE], f16)
        sel = sb(mem, "lasel", [P, D])
        xs = sb(mem, "laxs", [P, NT * DSL])
        lo, hi = sb(mem, "lalo", [P, NT]), sb(mem, "lahi", [P, NT])
        w1, w2 = sb(mem, "law1", [P, NT * NTILE]), sb(mem, "law2", [P, NT * NTILE])
        ext = [sb(mem, f"laext{i}", [P, NTILE]) for i in range(2)]
        col = [sb(mem, f"lacol{i}", [NTILE, 1]) for i in range(2)]
        colb = [sb(mem, f"lacolb{i}", [NTILE, P]) for i in range(2)]
        mn, mx = sb(mem, "lamn", [P, NT]), sb(mem, "lamx", [P, NT])
        num = sb(mem, "lanum", [P, NT * DSL])
        u = sb(mem, "lau", [P, NT * DSL])
        gi = sb(mem, "lagi", [P, NT * DSL])
        og = sb(mem, "laog", [P, NT * DSL * GRID])
        ohT = [sb(mem, f"laohT{i}", [P, P]) for i in range(2)]
        pick = sb(mem, "lapick", [P, 2, DSL * GRID])
        bs = sb(mem, "labs", [P, NT * 2 * DSL])
        osc = sb(mem, "laosc", [P, NT])
        dl = sb(mem, "ladl", [P, NT * DSL])
        res = [sb(mem, f"lares{i}", [P, D]) for i in range(2)]
        pEB = ps(mem, "lapEB", [P, 512])
        pE = pEB[0:NTILE, 0:2 * P].rearrange("p (a n) -> p a n", a=2)
        pB = pEB[:, 2 * P:3 * P].rearrange("p (a n) -> p a n", a=2)
        pH = [ps(mem, f"lapH{i}", [P, 1024], f16)[:, 0:P] for i in range(2)]
        pT = [[ps(mem, f"lapT{i}{j}", [P, 512]) for j in range(2)] for i in range(2)]
        blk = mem.enter_context(nc.Block())
        TG = DSL * GRID

        @blk.sync
        def _(e):
            e.dma_start(sl[:, :], a["slopes"]).then_inc(S.sem("la_sl"), 16)
            for t, name in ((gam, "gamma"), (bet, "beta")):
                e.dma_start(t[:, :], bass.AP(a[name].tensor, 0, [[0, P], [1, D]])).then_inc(S.sem("la_gb"), 16)
            for r in (slice(0, NTILE), slice(NTILE, P)):
                e.dma_start(tab[r, 0:TG], a["bases"]).then_inc(S.sem("la_tab"), 16)
                e.dma_start(tab[r, TG:2 * TG], a["slopes"]).then_inc(S.sem("la_tab"), 16)
                e.dma_start(tab[r, 2 * TG:], a["oscale"]).then_inc(S.sem("la_tab"), 16)
            e.wait_ge(S.sem("la_ssg"), 1)
            e.dma_start(R["sign"].rearrange("(t j) -> t j", j=DSL), ssg[:, :]).then_inc(S.sem("la_sign"), 16)
            e.wait_ge(S.sem("la_sign"), 16)
            e.dma_start(sgn[:, :], bass.AP(R["sign"].tensor, 0, [[0, P], [1, D]])).then_inc(S.sem("la_signb"), 16)

            def load(it):
                S.wait(e, "lax3", it.back(2))
                S.static(e)
                S.moved(e.dma_start(xin[it.p][:, :], R["x2"][bass.ds(it.n * P, P), :]), "laxin", it)
            pipeline(e, NT, [(load, 0)])

            def store(it):
                S.wait(e, "lares", it)
                S.static(e)
                S.moved(e.dma_start(out[bass.ds(it.n * P, P), :], res[it.p][:, :]), "laout", it)
            pipeline(e, NT, [(store, 0)])
            for p in range(2):
                S.wait_moved(e, "laout", It(NT // 2 - 1, p))

        @blk.gpsimd
        def _(e):
            def roots(it):
                S.wait(e, "lave", it)
                S.done(e.tensor_tensor(rstd[:, :], ve[:, :], K["mhalf"][:, :], ALU.pow), "larstd")
                S.wait(e, "lave2", it)
                S.done(e.tensor_tensor(rstd2[:, :], ve2[:, :], K["mhalf"][:, :], ALU.pow), "larstd2")
            pipeline(e, NT, [(roots, 0)])

        @blk.scalar
        def _(e):
            e.wait_ge(S.sem("la_ssum"), 1)
            e.activation(ssg[:, :], ssum[:, :], ACT.Sign).then_inc(S.sem("la_ssg"), 1)

            def signs(it):
                S.wait(e, "laxf", it)
                S.wait(e, "lam", it.back(2))
                S.done(e.activation(sg[it.p][:, :], xf[it.p][:, :], ACT.Sign), "lasg")
            pipeline(e, NT, [(signs, 0)])

            def turn(it):
                S.wait(e, "laH", it)
                S.wait(e, "laT", it.back(2))
                S.done(e.activation(ohT[it.p][:, :], pH[it.p], ACT.Copy), "laohT")
            pipeline(e, NT // 2, [(turn, 0)])

        @blk.vector
        def _(v):
            line = Line(S, v, "la0")
            line.start(It(0, 0))
            v.wait_ge(S.sem("la_sl"), 16)
            line(v.tensor_reduce(ssum[:, :], sl[:, :].rearrange("t (j g) -> t j g", g=GRID), AX.X, ALU.add))
            line(v.tensor_scalar(ssum[:, :], ssum[:, :], 1.0 / GRID, None, ALU.mult), "la_ssum")
            v.wait_ge(S.sem("la_gb"), 32)
            v.wait_ge(S.sem("la_signb"), 16)
            front, back = Line(S, v, "la1"), Line(S, v, "la2")

            def norm(it):
                front.start(it)
                at = bass.ds(it.n * D, D)
                S.wait_moved(v, "laxin", it)
                front(v.scalar_tensor_tensor(x3[:, :], o[:, at], K["gate"][:, 2:3], xin[it.p][:, :],
                                             ALU.mult, ALU.add), "lax3")
                front(v.bn_stats(st[:, :], x3[:, :]))
                S.static(v)
                front(v.bn_aggr(mv[:, :], st[:, :]))
                front(v.tensor_scalar(ve[:, :], mv[:, 1:2], EPS, None, ALU.add), "lave")
                S.wait(v, "larstd", it)
                front(v.tensor_scalar(z[:, :], x3[:, :], mv[:, 0:1], rstd[:, :], ALU.subtract, ALU.mult))
                front(v.scalar_tensor_tensor(o[:, at], z[:, :], K["gate"][:, 3:4], x3[:, :], ALU.mult, ALU.add))
                S.static(v)
                front(v.bn_stats(st[:, :], z[:, :]))
                S.static(v)
                front(v.bn_aggr(mv[:, :], st[:, :]))
                front(v.tensor_scalar(ve2[:, :], mv[:, 1:2], EPS, None, ALU.add), "lave2")
                S.wait(v, "larstd2", it)
                front(v.tensor_scalar(xf[it.p][:, :], z[:, :], mv[:, 0:1], rstd2[:, :], ALU.subtract, ALU.mult))
                front(v.tensor_tensor(xf[it.p][:, :], xf[it.p][:, :], gam[:, :], ALU.mult))
                front(v.tensor_tensor(xf[it.p][:, :], xf[it.p][:, :], bet[:, :], ALU.add), "laxf")

            def choose(it):
                back.start(it)
                S.wait(v, "lasg", it)
                back(v.tensor_tensor(sel[:, :], sg[it.p][:, :], sgn[:, :], ALU.mult), "lam")
                back(v.tensor_reduce(ts[:, :], sel[:, :].rearrange("p (t j) -> p t j", j=DSL), AX.X, ALU.add))
                back(v.tensor_reduce(cs[:, :], ts[:, :].rearrange("p (c t) -> p c t", t=NTILE // NCL), AX.X, ALU.add))
                back(v.scalar_tensor_tensor(cs[:, :], cs[:, :], 8.0, K["iota"][:, 0:NCL], ALU.mult, ALU.subtract))
                back(v.tensor_scalar(cs[:, :], cs[:, :], 256.0, None, ALU.mult))
                back(v.scalar_tensor_tensor(
                    key[:, :].rearrange("p (c t) -> p c t", c=NCL), ts[:, :].rearrange("p (c t) -> p c t", c=NCL), 8.0,
                    bcast(K["iota"][:, 0:1], [(0, NCL), (1, NTILE // NCL)]), ALU.mult, ALU.subtract))
                back(v.tensor_tensor(key[:, :].rearrange("p (c t) -> p c t", c=NCL), key[:, :].rearrange("p (c t) -> p c t", c=NCL),
                                     bcast(cs[:, 0:1], [(1, NCL), (0, NTILE // NCL)]), ALU.add))
                back(v.tensor_reduce(best[:, :], key[:, :], AX.X, ALU.max))
                back(v.tensor_scalar(oh[:, bass.ds(it.n * NTILE, NTILE)], key[:, :], best[:, :], None, ALU.is_equal), "laoh")
                back(v.tensor_tensor(sel[:, :].rearrange("p (t j) -> p t j", j=DSL), xf[it.p][:, :].rearrange("p (t j) -> p t j", j=DSL),
                                     wide(it), ALU.mult))
                back(v.tensor_reduce(xs[:, bass.ds(it.n * DSL, DSL)], sel[:, :].rearrange("p (t j) -> p j t", j=DSL), AX.X, ALU.add))
                back(v.tensor_reduce(lo[:, bass.ds(it.n, 1)], xs[:, bass.ds(it.n * DSL, DSL)], AX.X, ALU.min))
                back(v.tensor_reduce(hi[:, bass.ds(it.n, 1)], xs[:, bass.ds(it.n * DSL, DSL)], AX.X, ALU.max))

            def wide(it):
                return oh[:, :].rearrange("p (n t a) -> p n t a", t=NTILE, a=1)[:, bass.ds(it.n, 1), :, :]\
                    .rearrange("p n t a -> p (n t) a").to_broadcast((P, NTILE, DSL))
            pipeline(v, NT, [(norm, 0), (choose, 1)])

            tail = Line(S, v, "la3")
            tail.start(It(0, 0))
            tail(v.tensor_copy(oh16[:, :], oh[:, :]), "laoh16")
            three = lambda t: t[:, :].rearrange("p (n t) -> p n t", n=NT)
            for i, (val, op, big) in enumerate(((lo, ALU.min, BIG), (hi, ALU.max, -BIG))):
                tail(v.tensor_scalar(w1[:, :], oh[:, :], -big, big, ALU.mult, ALU.add))
                tail(v.tensor_tensor(three(w2), three(oh), bcast(val[:, 0:1], [(1, NT), (0, NTILE)]), ALU.mult))
                tail(v.tensor_tensor(w1[:, :], w1[:, :], w2[:, :], ALU.add))
                tail(v.tensor_reduce(ext[i][:, :], w1[:, :].rearrange("p (n t) -> p t n", n=NT), AX.X, op), f"laext{i}")
            for i, op in enumerate((ALU.min, ALU.max)):
                v.wait_ge(S.sem("laE"), 2)
                tail(v.tensor_reduce(col[i][:, :], pE[:, i, :], AX.X, op))
                tail(v.tensor_copy(colb[i][:, :], bcast(col[i][:, :], [(0, P)])), f"lacol{i}")
            for i, to in enumerate((mn, mx)):
                v.wait_ge(S.sem("laB"), 2)
                tail(v.tensor_tensor(three(w1), three(oh), bcast(pB[:, i, 0:1], [(0, NT), (1, NTILE)]), ALU.mult))
                tail(v.tensor_reduce(to[:, :], three(w1), AX.X, ALU.add))
            eight = lambda t: t[:, :].rearrange("p (n j) -> p n j", j=DSL)
            tail(v.tensor_tensor(eight(num), eight(xs), bcast(mn[:, 0:1], [(1, NT), (0, DSL)]), ALU.subtract))
            tail(v.tensor_tensor(mx[:, :], mx[:, :], mn[:, :], ALU.subtract))
            tail(v.tensor_scalar(mx[:, :], mx[:, :], 1e-8, None, ALU.add))
            tail(v.reciprocal(mx[:, :], mx[:, :]))
            tail(v.tensor_tensor(eight(u), eight(num), bcast(mx[:, 0:1], [(1, NT), (0, DSL)]), ALU.mult))
            tail(v.tensor_scalar(u[:, :], u[:, :], 0.0, float(np.float32(1.0 - 1e-6)), ALU.max, ALU.min))
            tail(v.tensor_scalar(u[:, :], u[:, :], float(GRID), None, ALU.mult))
            sixteen = og[:, :].rearrange("p (n g) -> p n g", g=GRID)
            grid = bcast(K["iota"][:, 0:1], [(0, NT * DSL), (1, GRID)])
            tail(v.tensor_tensor(sixteen, bcast(u[:, 0:1], [(1, NT * DSL), (0, GRID)]), grid, ALU.is_ge))
            tail(v.tensor_reduce(gi[:, :], sixteen, AX.X, ALU.add))
            tail(v.tensor_scalar(gi[:, :], gi[:, :], -1.0, None, ALU.add))
            tail(v.tensor_tensor(sixteen, bcast(gi[:, 0:1], [(1, NT * DSL), (0, GRID)]), grid, ALU.is_equal))
            tail(v.tensor_tensor(u[:, :], u[:, :], gi[:, :], ALU.subtract))
            rows = Line(S, v, "la4")

            def pickup(it):
                rows.start(it)
                S.wait(v, "laT", it)
                for j in range(2):
                    n = it.n * 2 + j
                    g = og[:, :].rearrange("p (a n g) -> p a n g", a=1, n=NT)[:, :, bass.ds(n, 1), :]\
                        .rearrange("p a n g -> p a (n g)").to_broadcast((P, 2, TG))
                    t = pT[it.p][j]
                    rows(v.tensor_tensor(pick[:, :, :], t[:, 0:2 * TG].rearrange("p (a g) -> p a g", a=2), g, ALU.mult))
                    rows(v.tensor_reduce(bs[:, bass.ds(n * 2 * DSL, 2 * DSL)],
                                         pick[:, :, :].rearrange("p a (j g) -> p (a j) g", g=GRID), AX.X, ALU.add))
                    rows(v.tensor_copy(osc[:, bass.ds(n, 1)], t[:, 2 * TG:2 * TG + 1]), "lapick" if j else None)
            pipeline(v, NT // 2, [(pickup, 0)])
            two = bs[:, :].rearrange("p (n a j) -> p n a j", a=2, j=DSL)
            tail(v.tensor_tensor(eight(dl), two[:, :, 1, :], eight(u), ALU.mult))
            tail(v.tensor_tensor(eight(dl), two[:, :, 0, :], eight(dl), ALU.add))
            tail(v.tensor_scalar(osc[:, :], osc[:, :], K["gate"][:, 3:4], None, ALU.mult))
            tail(v.tensor_tensor(eight(dl), eight(dl), bcast(osc[:, 0:1], [(1, NT), (0, DSL)]), ALU.mult))
            fin = Line(S, v, "la5")

            def finish(it):
                fin.start(it)
                S.wait_moved(v, "laout", it.back(2))
                d = dl[:, :].rearrange("p (n a j) -> p n a j", n=NT, a=1)[:, bass.ds(it.n, 1), :, :]\
                    .rearrange("p n a j -> p (n a) j").to_broadcast((P, NTILE, DSL))
                fin(v.tensor_tensor(res[it.p][:, :].rearrange("p (t j) -> p t j", j=DSL), wide(it), d, ALU.mult))
                fin(v.tensor_tensor(res[it.p][:, :], res[it.p][:, :], o[:, bass.ds(it.n * D, D)], ALU.add), "lares")
            pipeline(v, NT, [(finish, 0)])

        @blk.tensor
        def _(e):
            for i in range(2):
                e.wait_ge(S.sem(f"laext{i}"), 1)
                e.transpose(pE[:, i, :], ext[i][:, :], ident[:, :]).then_inc(S.sem("laE"), 1)
            for i in range(2):
                e.wait_ge(S.sem("lacol1"), 1)
                e.transpose(pB[:, i, :], colb[i][:, :], ident[0:NTILE, 0:NTILE]).then_inc(S.sem("laB"), 1)
            e.wait_ge(S.sem("la_tab"), 96)
            e.wait_ge(S.sem("laoh16"), 1)

            def turn(it):
                S.wait(e, "laohT", it.back(2))
                S.static(e)
                S.done(e.transpose(pH[it.p], oh16[:, bass.ds(it.n * P, P)], K["ident"][:, :]), "laH")

            def look(it):
                S.wait(e, "laohT", it)
                S.wait(e, "lapick", it.back(2))
                for j in range(2):
                    r = slice(NTILE * j, NTILE * j + NTILE)
                    last = e.matmul(pT[it.p][j][:, 0:2 * TG + 1], ohT[it.p][r, :], tab[r, :], start=True, stop=True)
                S.done(last, "laT")
            pipeline(e, NT // 2, [(turn, 0), (look, 1)])


def layout(x, itok, ctx, gx, gf, sw1, sb1, sw2, sb2, rw1, rb1, rw2, rb2, cen, bias, wq, wk, wv,
           gamma, beta, bases, slopes, oscale):
    def rows(w):
        w = w.reshape(w.shape[:-2] + (w.shape[-2] // P, P, w.shape[-1]))
        return np.ascontiguousarray(np.swapaxes(w, -3, -2)).reshape(w.shape[:-3] + (P, -1))

    def second(w, b):
        z = np.zeros(w.shape[:-2] + (FB * P - FF - 1, w.shape[-1]), w.dtype)
        return rows(np.concatenate([w, b[..., None, :], z], axis=-2))

    def column(b):
        z = np.zeros(b.shape[:-1] + (FB * P - FF,), b.dtype)
        b = np.concatenate([b, z], axis=-1)
        return np.ascontiguousarray(b.reshape(-1, P).T)

    kv = np.concatenate([wk, wv], axis=0).reshape(NH, HD, 2, D)
    wkh, wvh = (kv[:, :, s].reshape(NH * HD, D) for s in range(2))
    rowi = np.arange(P)
    return {
        "x": x.reshape(TOK, D),
        "ids": np.ascontiguousarray(itok.reshape(NT, P).T),
        "gates": np.concatenate([gx[0:1], gf[0:1], gx[1:2], gf[1:2]]),
        "ctxT": rows(np.ascontiguousarray(ctx.transpose(0, 2, 1))),
        "sw1": rows(sw1), "sb1": column(sb1), "sw2": second(sw2, sb2),
        "rw1": rows(rw1), "rb1": column(rb1), "rw2": second(rw2, rb2),
        "cenT": rows(np.ascontiguousarray(cen.T)), "bias": bias.reshape(1, NR),
        "wqT": rows(np.ascontiguousarray(wq.T)), "wkT": rows(np.ascontiguousarray(wkh.T)),
        "wvT": rows(np.ascontiguousarray(wvh.T)),
        "gamma": gamma.reshape(1, D), "beta": beta.reshape(1, D),
        "bases": bases.reshape(NTILE, DSL * GRID), "slopes": slopes.reshape(NTILE, DSL * GRID),
        "oscale": oscale.reshape(NTILE, 1),
        "c_ident": np.eye(P, dtype=np.float16),
        "c_ident32": np.eye(P, dtype=np.float32),
        "c_tri": (rowi[:, None] < rowi[None, :]).astype(np.float16),
        "c_ones": np.ones((P, P), np.float16),
        "c_iota": np.tile(np.arange(16, dtype=np.float32), (P, 1)),
        "c_tok": (np.arange(NT)[None, :] * P + rowi[:, None]).astype(np.int32),
        "c_iotan": np.arange(N2, dtype=np.float32)[None, :],
    }


def kernel(**inputs):
    import concourse.bacc as bacc
    from concourse.bass_utils import run_bass_kernel_spmd

    names = ["x", "itok_BxS_13_99985", "ctx_2048", "g_xattn", "g_ffn",
             "L0_ffn_shared_w1", "L0_ffn_shared_b1", "L0_ffn_shared_w2", "L0_ffn_shared_b2",
             "L0_ffn_routed_w1", "L0_ffn_routed_b1", "L0_ffn_routed_w2", "L0_ffn_routed_b2",
             "L0_ffn_centroids", "L0_ffn_bias", "L1_xattn_Wq", "L1_xattn_Wk", "L1_xattn_Wv",
             "L1_ffn_ln_gamma", "L1_ffn_ln_beta", "L1_ffn_spline_bases", "L1_ffn_spline_slopes", "L1_ffn_output_scale"]
    arrays = layout(*[np.asarray(inputs[n]) for n in names])
    arrays = {name: np.ascontiguousarray(v) for name, v in arrays.items()}
    nc = bacc.Bacc("TRN2", target_bir_lowering=False, num_devices=1)
    a = {name: nc.dram_tensor(name, v.shape, mybir.dt.from_np(v.dtype), kind="ExternalInput").ap()
         for name, v in arrays.items()}
    out = nc.dram_tensor("out", (TOK, D), f32, kind="ExternalOutput").ap()
    build(nc, a, out)
    r = run_bass_kernel_spmd(nc, [arrays], core_ids=[0])
    return r.results[0]["out"].reshape(BATCH, SEQ, D)
```

```python
import numpy as np
import concourse.bass as bass
from concourse import mybir
from contextlib import ExitStack

f32 = mybir.dt.float32
f16 = mybir.dt.float16
i32 = mybir.dt.int32
u32 = mybir.dt.uint32
ALU = mybir.AluOpType
ACT = mybir.ActivationFunctionType
AX = mybir.AxisListType

P = 128
BATCH, SEQ, D = 4, 512, 512
TOK = BATCH * SEQ
NT = TOK // P
KD = D // P
E1, RANGE1, TOP1 = 4, 25000 // 4, 3
FF, FB = 352, 3
FLAST = FF - 2 * P
NS, NR, KR = 2, 16, 4
NH, HD = 32, 16
GRID, NTILE, DSL, NCL = 16, 64, 8, 8
EPS = 1e-5
EPS_RMS = 1e-6
CAP = TOK
N1 = NT + E1
N2 = NT * KR + NR
SA, SW = 16.0, 64.0
UNSCALE = 1.0 / (SA * SW)


class It:

    def __init__(self, half, parity):
        self.half, self.p = half, parity
        self.n = half * 2 + parity

    def back(self, k):
        q = self.p - k
        return It(self.half + (q // 2), q % 2)


class Single:

    def __init__(self, n):
        self.n, self.half, self.p = n, n, 0

    def back(self, k):
        return Single(self.n - k)


class Sync:

    def __init__(self, nc):
        self.nc, self.sems, self.phase = nc, {}, 0

    def sem(self, name):
        if name not in self.sems:
            self.sems[name] = self.nc.alloc_semaphore(f"{name}_{self.phase}")
        return self.sems[name]

    def clear(self):
        self.nc.clear_and_free_semaphores(list(self.sems.values()))
        self.nc.all_engine_barrier()
        self.sems, self.phase = {}, self.phase + 1

    def done(self, ins, name):
        ins.then_inc(self.sem(name), 1)

    def moved(self, ins, name, it):
        ins.then_inc(self.sem(f"{name}{it.p}"), 16)

    def wait(self, eng, name, it, each=1):
        self.reach(eng, name, it, (it.n + 1) * each)

    def wait_moved(self, eng, name, it, each=1):
        self.reach(eng, f"{name}{it.p}", it, (it.half + 1) * (16 * each))

    def reach(self, eng, name, it, value):
        if not isinstance(it.n, int) or it.n >= 0:
            eng.wait_ge(self.sem(name), value)
            if not isinstance(it.n, int) and eng_name(eng) == "SP":
                self.static(eng)

    def static(self, eng):
        eng.sem_inc(self.sem("spare_" + eng_name(eng)), 1)


def eng_name(eng):
    return str(eng.engine).split(".")[-1]


class Line:

    def __init__(self, sync, eng, name):
        self.s, self.eng, self.link, self.per, self.k = sync, eng, name, None, 0

    def start(self, it):
        if self.k and self.per is None:
            self.per = self.k
        assert self.per is None or self.k in (0, self.per)
        self.it, self.k = it, 0

    def __call__(self, ins, name=None):
        if name:
            self.s.done(ins, name)
            self.s.wait(self.eng, name, self.it)
        else:
            self.k += 1
            ins.then_inc(self.s.sem(self.link), 1)
            first = self.per is None
            self.eng.wait_ge(self.s.sem(self.link), self.k if first else self.it.n * self.per + self.k)


def pipeline(eng, n, stages, unroll=2):
    stages = [s if len(s) == 4 else (s[0], s[1], 0, n) for s in stages]
    most = max(lag for _, lag, _, _ in stages)
    beats = max(lag + stop for _, lag, _, stop in stages)

    def beat(it, active):
        for stage in active:
            stage[0](it.back(stage[1]))

    def active(i):
        return [s for s in stages if s[2] <= i - s[1] < s[3]]
    i, first = 0, (most + 3) // 2 * 2
    while i < beats:
        end = i
        while end < beats and active(end) == active(i):
            end += 1
        full = (end - i) // unroll if i >= first and i % 2 == 0 else 0
        if full > 1:
            now, start = active(i), i // 2
            with eng.Fori(0, full) as h:
                for j in range(unroll):
                    beat(It(h * (unroll // 2) + (start + j // 2), j % 2), now)
            i += unroll * full
        else:
            beat(It(i // 2, i % 2), active(i))
            i += 1


def bcast(ap, dims):
    return bass.AP(ap.tensor, ap.offset, [list(ap.ap[0])] + [[s, c] for s, c in dims])


def build(nc, a, out):
    with ExitStack() as ctx:
        S = Sync(nc)

        def sb(mem, name, shape, dt=f32):
            return mem.enter_context(nc.sbuf_tensor("sb_" + name, shape, dt))

        def ps(mem, name, shape, dt=f32):
            return mem.enter_context(nc.psum_tensor("ps_" + name, shape, dt))

        def dram(name, shape, dt=f32):
            return nc.dram_tensor(name, shape, dt).ap()

        R = {
            "list1": dram("list1", (N1 * P, 1), i32),
            "list2": dram("list2", (NR * CAP + N2 * P, 1), i32),
            "y1s": dram("y1s", (N1 * P, D)),
            "xn2": dram("xn2", (TOK, 2 * D), f16),
            "x2a": dram("x2a", (TOK, D)),
            "ys": dram("ys", (N2 * P, D)),
            "kst": dram("kst", (NT, P, 4 * D), f16),
            "vst": dram("vst", (NT, P, NH * (HD + 1))),
            "qst": dram("qst", (NT, P, 4 * D), f16),
            "x2": dram("x2", (TOK, D)),
            "sign": dram("sign", (D,)),
        }
        K = {
            "ident": sb(ctx, "ident", [P, P], f16),
            "tri": sb(ctx, "tri", [P, P], f16),
            "ones": sb(ctx, "ones", [P, P], f16),
            "iota": sb(ctx, "iota", [P, 16]),
            "tok": sb(ctx, "tok", [P, NT], i32),
            "gate": sb(ctx, "gate", [P, 8]),
            "pos1": sb(ctx, "pos1", [P, NT], i32),
            "pos2": sb(ctx, "pos2", [P, NT * KR], i32),
            "g2f": sb(ctx, "g2f", [P, NT * KR]),
            "tab1": sb(ctx, "tab1", [1, N1], i32),
            "tab2": sb(ctx, "tab2", [1, 2, N2], i32),
            "mhalf": sb(ctx, "mhalf", [P, 1]),
            "iotan": sb(ctx, "iotan", [1, N2]),
        }
        with ExitStack() as mem:
            W, W1, W2 = KD * D, KD * FF, FB * D
            shared = {name: [sb(mem, f"sh{name}{i}", [P, cols], f16) for i in range(2)]
                      for name, cols in (("w1", NS * W1), ("w2", NS * W2), ("cen", KD * NR))}
            with ExitStack() as mem2:
                part = {name: [sb(mem2, f"{name}{i}", [P, n * W], f16) for i in range(2)]
                        for name, n in (("ctx", BATCH), ("wk", 1), ("wv", 1))}
                phase_setup(nc, S, sb, ps, a, R, K, part)
                S.clear()
                phase_layer1(nc, S, sb, ps, a, R, K, part, shared)
                S.clear()
            phase_shared(nc, S, sb, ps, a, R, K, shared)
            S.clear()
        for phase in (phase_routed, phase_queries):
            phase(nc, S, sb, ps, a, R, K)
            S.clear()
        phase_attention(nc, S, sb, ps, a, R, K, out)


def make_table(line, v, mem, sb, tag, e, n, count, K, expert, row, pos, posi):
    cols = pos.shape[1]
    gt = sb(mem, tag + "gt", [P, e, 16])
    lim = sb(mem, tag + "lim", [P, 16])
    nt = sb(mem, tag + "nt", [P, e])
    cum = [sb(mem, tag + f"cum{i}", [P, e]) for i in range(2)]
    skip = sb(mem, tag + "skip", [P, e])
    end = sb(mem, tag + "end", [P, e])
    ge = sb(mem, tag + "ge", [1, n, e])
    ef = sb(mem, tag + "ef", [1, n])
    st = sb(mem, tag + "st", [1, n])
    gp = sb(mem, tag + "gp", [P, cols, e])
    sp = sb(mem, tag + "sp", [P, cols])
    line(v.tensor_scalar(lim[:, :], K["iota"][:, :], float(P), None, ALU.mult))
    line(v.tensor_tensor(gt[:, :, :], bcast(count, [(count.ap[1][0], e), (0, 16)]),
                         bcast(lim[:, 0:1], [(0, e), (1, 16)]), ALU.is_gt))
    line(v.tensor_reduce(nt[:, :], gt[:, :, :], AX.X, ALU.add))
    line(v.tensor_scalar(nt[:, :], nt[:, :], 1.0, None, ALU.max))
    line(v.tensor_copy(cum[0][:, :], nt[:, :]))
    cur, d = 0, 1
    while d < e:
        line(v.tensor_copy(cum[1 - cur][:, 0:d], cum[cur][:, 0:d]))
        line(v.tensor_tensor(cum[1 - cur][:, d:e], cum[cur][:, d:e], cum[cur][:, 0:e - d], ALU.add))
        cur, d = 1 - cur, 2 * d
    line(v.tensor_scalar(skip[:, :], nt[:, :], -float(P), float(CAP), ALU.mult, ALU.add))
    line(v.tensor_scalar(end[:, :], K["iota"][:, 0:e], float(CAP), float(CAP), ALU.mult, ALU.add))
    line(v.tensor_tensor(ge[:, :, :], bcast(K["iotan"][0:1, 0:1], [(1, n), (0, e)]),
                         bcast(cum[cur][0:1, 0:1], [(0, n), (1, e)]), ALU.is_ge))
    line(v.tensor_reduce(ef[:, :], ge[:, :, :], AX.X, ALU.add))
    line(v.tensor_scalar(expert, ef[:, :], float(e - 1), None, ALU.min))
    if row is not None:
        line(v.tensor_tensor(ge[:, :, :], ge[:, :, :], bcast(skip[0:1, 0:1], [(0, n), (1, e)]), ALU.mult))
        line(v.tensor_reduce(st[:, :], ge[:, :, :], AX.X, ALU.add))
        line(v.scalar_tensor_tensor(row, K["iotan"][0:1, 0:n], float(P), st[:, :], ALU.mult, ALU.add))
    line(v.tensor_tensor(gp[:, :, :], bcast(pos, [(1, cols), (0, e)]), bcast(end[:, 0:1], [(0, cols), (1, e)]), ALU.is_ge))
    line(v.tensor_tensor(gp[:, :, :], gp[:, :, :], bcast(skip[:, 0:1], [(0, cols), (1, e)]), ALU.mult))
    line(v.tensor_reduce(sp[:, :], gp[:, :, :], AX.X, ALU.add))
    line(v.tensor_tensor(posi, pos, sp[:, :], ALU.subtract))


def phase_setup(nc, S, sb, ps, a, R, K, part):
    with ExitStack() as mem:
        ids = sb(mem, "ids", [P, NT], i32)
        idf = sb(mem, "idf", [P, NT])
        ge = sb(mem, "ge", [P, E1 + 1, NT])
        oh = sb(mem, "oh", [P, E1, NT], f16)
        tot = sb(mem, "tot", [P, E1, NT])
        inc = [sb(mem, f"inc{i}", [P, E1, NT]) for i in range(2)]
        pos = sb(mem, "pos", [P, E1, NT])
        sel = sb(mem, "sel", [P, E1, NT])
        posf = sb(mem, "posf", [P, NT])
        zero = sb(mem, "zero", [P, (NR * CAP + N2 * P) // P], i32)
        posb = [sb(mem, f"posb{i}", [P, 1], i32) for i in range(NT)]
        toks = [sb(mem, f"toks{i}", [P, 1], i32) for i in range(NT)]
        g4 = sb(mem, "g4", [P, 4])
        pp = ps(mem, "pp", [P, 2, E1 * NT])
        W = KD * D
        stage = [sb(mem, f"sustage{i}", [P, W]) for i in range(2)]
        jobs = [(a["ctxT"][i], part["ctx"][0][:, i * W:(i + 1) * W], part["ctx"][1][:, i * W:(i + 1) * W], W)
                for i in range(BATCH)]
        jobs += [(a[w + "T"], part[w][0][:, :], part[w][1][:, :], W) for w in ("wk", "wv")]
        blk = mem.enter_context(nc.Block())

        @blk.sync
        def _(e):
            loads = [("ident", K["ident"]), ("tri", K["tri"]), ("ones", K["ones"]), ("iota", K["iota"]),
                     ("tok", K["tok"]), ("iotan", K["iotan"])]
            for name, t in loads:
                e.dma_start(t[:, :], a["c_" + name]).then_inc(S.sem("su_consts"), 16)
            e.dma_start(ids[:, :], a["ids"]).then_inc(S.sem("su_ids"), 16)
            e.dma_start(g4[:, :], bass.AP(a["gates"].tensor, 0, [[0, P], [1, 4]])).then_inc(S.sem("su_gates"), 16)
            e.wait_ge(S.sem("su_zero"), 1)
            for name in ("list1", "list2"):
                rows = R[name].shape[0]
                e.dma_start(R[name].rearrange("(p c) o -> p (c o)", p=P), zero[:, 0:rows // P])\
                    .then_inc(S.sem("su_list0"), 16)
            load_split(S, e, None, None, jobs, stage, "su")
            e.wait_ge(S.sem("su_list0"), 32)

        @blk.vector
        def _(v):
            line = Line(S, v, "su_dve")
            line.start(It(0, 0))
            line(v.memset(zero[:, :], 0), "su_zero")
            line(v.memset(K["mhalf"][:, :], -0.5))
            line(v.memset(ge[:, 0, :], 1.0))
            line(v.memset(ge[:, E1, :], 0.0))
            v.wait_ge(S.sem("su_consts"), 16 * 6)
            v.wait_ge(S.sem("su_ids"), 16)
            line(v.tensor_copy(idf[:, :], ids[:, :]))
            for i in range(1, E1):
                line(v.tensor_scalar(ge[:, i, :], idf[:, :], float(i * RANGE1), None, ALU.is_ge))
            line(v.tensor_tensor(oh[:, :, :], ge[:, 0:E1, :], ge[:, 1:E1 + 1, :], ALU.subtract), "su_onehot")
            v.wait_ge(S.sem("su_count"), 1)
            line(v.tensor_copy(tot[:, :, :].rearrange("p e t -> p (e t)"), pp[:, 1, :]))
            line(v.tensor_copy(inc[0][:, :, :], tot[:, :, :]))
            cur, d = 0, 1
            while d < NT:
                line(v.tensor_copy(inc[1 - cur][:, :, 0:d], inc[cur][:, :, 0:d]))
                line(v.tensor_tensor(inc[1 - cur][:, :, d:], inc[cur][:, :, d:], inc[cur][:, :, 0:NT - d], ALU.add))
                cur, d = 1 - cur, 2 * d
            line(v.tensor_tensor(pos[:, :, :], inc[cur][:, :, :], tot[:, :, :], ALU.subtract))
            line(v.tensor_tensor(pos[:, :, :].rearrange("p e t -> p (e t)"), pp[:, 0, :],
                                 pos[:, :, :].rearrange("p e t -> p (e t)"), ALU.add))
            for i in range(1, E1):
                line(v.tensor_scalar(pos[:, i, :], pos[:, i, :], float(i * CAP), None, ALU.add))
            line(v.tensor_tensor(sel[:, :, :], pos[:, :, :], oh[:, :, :], ALU.mult))
            line(v.tensor_reduce(posf[:, :], sel[:, :, :].rearrange("p e t -> p t e"), AX.X, ALU.add))
            make_table(line, v, mem, sb, "t1", E1, N1, inc[cur][:, :, NT - 1], K, K["tab1"][0:1, :], None,
                       posf[:, :], K["pos1"][:, :])
            for i in range(NT):
                v.tensor_copy(toks[i][:, :], K["tok"][:, i:i + 1])
                line(v.tensor_copy(posb[i][:, :], K["pos1"][:, i:i + 1]))
            line(v.memset(sel[:, 0, 0:1], 0.0), "su_pos")
            load_split(S, None, None, v, jobs, stage, "su")

        @blk.tensor
        def _(e):
            e.wait_ge(S.sem("su_consts"), 16 * 6)
            e.wait_ge(S.sem("su_onehot"), 1)
            o = oh[:, :, :].rearrange("p e t -> p (e t)")
            e.matmul(pp[:, 0, :], K["tri"][:, :], o, start=True, stop=True)
            e.matmul(pp[:, 1, :], K["ones"][:, :], o, start=True, stop=True).then_inc(S.sem("su_count"), 1)

        @blk.scalar
        def _(e):
            e.wait_ge(S.sem("su_gates"), 16)
            e.activation(K["gate"][:, 0:4], g4[:, :], ACT.Tanh).then_inc(S.sem("su_tanh"), 1)
            e.wait_ge(S.sem("su_tanh"), 1)
            e.activation(K["gate"][:, 4:5], K["gate"][:, 0:1], ACT.Copy, scale=UNSCALE)
            e.activation(K["gate"][:, 5:6], K["gate"][:, 1:2], ACT.Copy, scale=1.0 / SA)
            e.activation(K["gate"][:, 6:7], K["gate"][:, 1:2], ACT.Copy, scale=UNSCALE)
            load_split(S, None, e, None, jobs, stage, "su")

        @blk.gpsimd
        def _(e):
            e.wait_ge(S.sem("su_pos"), 1)
            e.wait_ge(S.sem("su_list0"), 32)
            for i in range(NT):
                e.indirect_dma_start(out=R["list1"], out_offset=bass.IndirectOffsetOnAxis(ap=posb[i][:, :], axis=0),
                                     in_=toks[i][:, :], in_offset=None).then_inc(S.sem("su_scatter"), 16)
            e.wait_ge(S.sem("su_scatter"), 16 * NT)


def split_jobs(S, jobs, stage, tag):
    def load(e, n):
        src, hi, lo, cols = jobs[n]
        it = It(n // 2, n % 2)
        S.wait(e, tag + "lo", it.back(2))
        S.moved(e.dma_start(stage[it.p][:, 0:cols], src), tag + "w", it)

    def high(e, n):
        src, hi, lo, cols = jobs[n]
        it = It(n // 2, n % 2)
        S.wait_moved(e, tag + "w", it)
        S.done(e.activation(hi, stage[it.p][:, 0:cols], ACT.Copy, scale=SW), tag + "hi")

    def low(e, n):
        src, hi, lo, cols = jobs[n]
        it = It(n // 2, n % 2)
        S.wait(e, tag + "hi", it)
        S.done(e.scalar_tensor_tensor(lo, stage[it.p][:, 0:cols], SW, hi, ALU.mult, ALU.subtract), tag + "lo")
    return load, high, low


def load_split(S, sync_, act, dve, jobs, stage, tag):
    for e, part in zip((sync_, act, dve), split_jobs(S, jobs, stage, tag)):
        if e:
            for n in range(len(jobs)):
                part(e, n)


def spread_out(e, part, jobs, start):
    return [(lambda it: part(e, it.n - start), 0, start + n, start + n + 1) for n in range(len(jobs))]


def row_stats(line, v, S, T, x, tag):
    line(v.bn_stats(T["st"][:, :], x))
    S.static(v)
    line(v.bn_aggr(T["mv"][:, :], T["st"][:, :]))
    line(v.tensor_scalar(T["ve"][:, :], T["mv"][:, 1:2], EPS, None, ALU.add), tag + "var")


def normed(line, v, S, T, x, tag, it):
    S.wait(v, tag + "rstd", it)
    line(v.tensor_scalar(T["rs"][:, :], T["rstd"][:, :], SA, None, ALU.mult))
    line(v.tensor_scalar(T["xs"][it.p][:, :], x, T["mv"][:, 0:1], T["rs"][:, :], ALU.subtract, ALU.mult), tag + "xs")


def pool_rstd(e, S, T, K, tag, it):
    S.wait(e, tag + "var", it)
    S.done(e.tensor_tensor(T["rstd"][:, :], T["ve"][:, :], K["mhalf"][:, :], ALU.pow), tag + "rstd")


def transposes(e, dst, src, ident, n):
    for j in range(n):
        last = e.transpose(dst[:, j, :], src[:, j * P:(j + 1) * P], ident)
    return last


def head_squares(line, v, S, tag, it, sq, ss):
    S.wait(v, tag + "sq", it)
    line(v.tensor_reduce(ss, sq.rearrange("p (h d) -> p h d", d=HD), AX.X, ALU.add))
    line(v.tensor_scalar(ss, ss, 1.0 / HD, EPS_RMS, ALU.mult, ALU.add), tag + "ms")


def head_scale(line, v, S, tag, it, p_raw, rr, out, scale):
    line(v.tensor_scalar(rr, rr, scale, None, ALU.mult))
    line(v.tensor_tensor(out.rearrange("p (h d) -> p h d", d=HD), p_raw.rearrange("p (h d) -> p h d", d=HD),
                         bcast(rr, [(1, NH), (0, HD)]), ALU.mult), tag + "n")


def part_pair(ap, first, step):
    return bass.AP(ap.tensor, ap.offset + first * HD, [list(ap.ap[0]), [4 * HD, NH], [step * HD, 2], [1, HD]])


def twice(ap):
    return bcast(ap, [(HD, NH), (0, 2), (1, HD)])


def key_stages(nc, S, sb, ps, mem, R, K, part):
    W = KD * D
    sq = sb(mem, "kysq", [P, D])
    ss = sb(mem, "kyss", [P, NH])
    rr = sb(mem, "kyrr", [P, NH])
    raw = [sb(mem, f"kyraw{i}", [P, D]) for i in range(2)]
    kn = [sb(mem, f"kykn{i}", [P, D]) for i in range(2)]
    kp = [sb(mem, f"kykp{i}", [P, 4 * D], f16) for i in range(2)]
    kt = [sb(mem, f"kykt{i}", [P, 4 * D], f16) for i in range(2)]
    vt = [sb(mem, f"kyvt{i}", [P, NH * (HD + 1)]) for i in range(2)]
    pK = ps(mem, "kypK", [P, D])
    pV = ps(mem, "kypV", [P, D])
    pT = ps(mem, "kypT", [P, NH // 2, P], f16)

    def sync(e):
        def store(it):
            S.wait(e, "kyvt", it)
            S.static(e)
            S.moved(e.dma_start(R["vst"][bass.ds(it.n, 1)].rearrange("a p c -> (a p) c"), vt[it.p][:, :]), "kyvout", it)
            S.wait(e, "kykt", it)
            S.static(e)
            S.moved(e.dma_start(R["kst"][bass.ds(it.n, 1)].rearrange("a p c -> (a p) c"), kt[it.p][:, :]), "kykout", it)
        return [(store, 7, 0, NT)]

    def scalar(e):
        def square(it):
            S.wait(e, "kyproj", it)
            S.wait(e, "kyn", it.back(2))
            S.done(e.activation(raw[it.p][:, :], pK[:, :], ACT.Copy, scale=1.0 / SW ** 2), "kyraw")
            S.wait(e, "kyms", it.back(1))
            S.done(e.activation(sq[:, :], pK[:, :], ACT.Square, scale=1.0 / SW ** 2), "kysq")

        def values(it):
            S.wait_moved(e, "kyvout", it.back(2))
            S.done(e.activation(vt[it.p][:, :].rearrange("p (h d) -> p h d", d=HD + 1)[:, :, 0:HD],
                                pV[:, :].rearrange("p (h d) -> p h d", d=HD), ACT.Copy, scale=1.0 / SW ** 2), "kyvt")

        def parts(it):
            S.wait(e, "kyn", it)
            S.wait(e, "kyT", it.back(2))
            S.done(e.activation(part_pair(kp[it.p][:, :], 0, 2), twice(kn[it.p][:, :]), ACT.Copy), "kyhi")

        def evacuate(it):
            S.wait(e, "kyT", it)
            S.wait_moved(e, "kykout", it.back(2))
            S.done(e.activation(kt[it.p][:, :], pT[:, :, :].rearrange("p j n -> p (j n)"), ACT.Copy), "kykt")
        return [(square, 4, 0, NT), (values, 4, 0, NT), (parts, 5, 0, NT), (evacuate, 6, 0, NT)]

    def gpsimd(e):
        def root(it):
            S.wait(e, "kyms", it)
            S.wait(e, "kyn", it.back(1))
            S.done(e.tensor_tensor(rr[:, :], ss[:, :], bcast(K["mhalf"][:, :], [(0, NH)]), ALU.pow), "kyrt")
        return [(root, 4, 0, NT)]

    def init(line, v):
        line(v.memset(vt[0][:, :], 1.0))
        line(v.memset(vt[1][:, :], 1.0), "ky_init")

    def vector(v):
        heads0, heads1, heads2 = (Line(S, v, f"kydve{i}") for i in range(3))

        def squares(it):
            heads0.start(it)
            S.wait(v, "kyrt", it.back(1))
            head_squares(heads0, v, S, "ky", it, sq[:, :], ss[:, :])

        def scale(it):
            heads1.start(it)
            S.wait(v, "kyhi", it.back(2))
            S.wait(v, "kyrt", it)
            S.wait(v, "kyraw", it)
            head_scale(heads1, v, S, "ky", it, raw[it.p][:, :], rr[:, :], kn[it.p][:, :], SA)

        def parts(it):
            heads2.start(it)
            S.wait(v, "kyhi", it)
            heads2(v.tensor_tensor(part_pair(kp[it.p][:, :], 1, 2), twice(kn[it.p][:, :]),
                                   bcast(kp[it.p][:, :], [(4 * HD, NH), (0, 2), (1, HD)]), ALU.subtract), "kylo")
        return [(squares, 4, 0, NT), (scale, 5, 0, NT), (parts, 5, 0, NT)]

    def tensor(e):
        def project(it):
            S.wait(e, "kyraw", it.back(1))
            S.wait(e, "kysq", it.back(1))
            S.wait(e, "kyvt", it.back(1))
            at = (it.n // 4) * W + (it.n % 4) * P
            for out, w in ((pK, part["wk"]), (pV, part["wv"])):
                terms = split_terms(part["ctx"], w, KD)
                for j, (x, y, k) in enumerate(terms):
                    last = e.matmul(out[:, :], x[:, bass.ds(at + k * D, P)], y[:, k * D:(k + 1) * D],
                                    start=j == 0, stop=j == len(terms) - 1)
            S.done(last, "kyproj")

        def turn(it):
            S.wait(e, "kylo", it)
            S.wait(e, "kykt", it.back(1))
            S.done(transposes(e, pT, kp[it.p], K["ident"][:, :], NH // 2), "kyT")
        return (turn, 6, 0, NT), (project, 3, 0, NT)
    return {"sync": sync, "scalar": scalar, "gpsimd": gpsimd, "init": init, "vector": vector, "tensor": tensor}


def phase_layer1(nc, S, sb, ps, a, R, K, part, shared):
    with ExitStack() as mem:
        ch, cl = part["ctx"]
        idx = [sb(mem, f"l1idx{i}", [P, 1], i32) for i in range(2)]
        x = [sb(mem, f"l1x{i}", [P, D]) for i in range(2)]
        T = {"st": sb(mem, "l1st", [P, 6]), "mv": sb(mem, "l1mv", [P, 2]), "ve": sb(mem, "l1ve", [P, 1]),
             "rstd": sb(mem, "l1rstd", [P, 1]), "rs": sb(mem, "l1rs", [P, 1]),
             "xs": [sb(mem, f"l1xs{i}", [P, D]) for i in range(2)]}
        xhl = [sb(mem, f"l1xhl{i}", [P, 2 * D], f16) for i in range(2)]
        xT = [sb(mem, f"l1xT{i}", [P, 2 * KD, P], f16) for i in range(2)]
        sg = [sb(mem, f"l1sg{i}", [P, KD * P]) for i in range(2)]
        sq = [sb(mem, f"l1sq{i}", [P, KD * P]) for i in range(2)]
        h = [sb(mem, f"l1h{i}", [P, KD * P]) for i in range(2)]
        hh = [sb(mem, f"l1hh{i}", [P, KD * P], f16) for i in range(2)]
        hl = [sb(mem, f"l1hl{i}", [P, KD * P], f16) for i in range(2)]
        y = [sb(mem, f"l1y{i}", [P, D]) for i in range(2)]
        pT = ps(mem, "l1pT", [P, 2 * KD, P], f16)
        pP = [ps(mem, f"l1pP{i}", [P, KD * P]) for i in range(2)]
        pY = ps(mem, "l1pY", [P, D])
        W = KD * D
        W1, W2 = KD * FF, FB * D
        stage = [sb(mem, f"l1stage{i}", [P, W2]) for i in range(2)]
        jobs = [(a[src][i], shared[w][0][:, i * n:(i + 1) * n], shared[w][1][:, i * n:(i + 1) * n], n)
                for src, w, n in (("sw1", "w1", W1), ("sw2", "w2", W2)) for i in range(NS)]
        jobs += [(a["cenT"], shared["cen"][0][:, :], shared["cen"][1][:, :], KD * NR)]
        load, high_part, low_part = split_jobs(S, jobs, stage, "sh")
        keys = key_stages(nc, S, sb, ps, mem, R, K, part)
        blk = mem.enter_context(nc.Block())

        @blk.sync
        def _(e):
            def indices(it):
                S.wait_moved(e, "l1gather", it.back(2))
                S.static(e)
                S.moved(e.dma_start(idx[it.p][:, :], R["list1"][bass.ds(it.n * P, P), :]), "l1idx", it)

            def store(it):
                S.wait(e, "l1y", it)
                S.static(e)
                S.moved(e.dma_start(R["y1s"][bass.ds(it.n * P, P), :], y[it.p][:, :]), "l1store", it)
            pipeline(e, N1, [(indices, 0), (store, 6)] + keys["sync"](e) + spread_out(e, load, jobs, 1))
            for p in range(2):
                S.wait_moved(e, "kyvout", It(NT // 2 - 1, p))
                S.wait_moved(e, "kykout", It(NT // 2 - 1, p))
                S.wait_moved(e, "l1store", It(N1 // 2 - 1, p))

        @blk.gpsimd
        def _(e):
            def gather(it):
                S.wait_moved(e, "l1idx", it)
                S.wait(e, "l1xs", it.back(2))
                S.static(e)
                S.moved(e.indirect_dma_start(
                    out=x[it.p][:, :], out_offset=None, in_=a["x"],
                    in_offset=bass.IndirectOffsetOnAxis(ap=idx[it.p][:, :], axis=0)), "l1gather", it)
            pipeline(e, N1, [(lambda it: pool_rstd(e, S, T, K, "l1", it), 1), (gather, 0)] + keys["gpsimd"](e))

        @blk.scalar
        def _(e):
            e.wait_ge(S.sem("ky_init"), 1)

            def yout(it):
                S.wait(e, "l1mm2", it)
                S.wait_moved(e, "l1store", it.back(2))
                S.done(e.activation(y[it.p][:, :], pY[:, :], ACT.Copy, scale=K["gate"][:, 4:5]), "l1y")

            def high(it):
                S.wait(e, "l1xs", it)
                S.wait(e, "l1T", it.back(2))
                S.done(e.activation(xhl[it.p][:, 0:D], T["xs"][it.p][:, :], ACT.Copy), "l1xh")

            def hidden(it):
                S.wait(e, "l1mm1", it)
                S.wait(e, "l1h", it.back(2))
                S.done(e.activation(sg[it.p][:, :], pP[it.p][:, :], ACT.Sigmoid, scale=UNSCALE), "l1sg")
                S.done(e.activation(sq[it.p][:, :], pP[it.p][:, :], ACT.Square, scale=UNSCALE * SA ** 0.5), "l1sq")
                S.wait(e, "l1h", it)
                S.wait(e, "l1mm2", it.back(2))
                S.done(e.activation(hh[it.p][:, :], h[it.p][:, :], ACT.Copy), "l1hh")
            square, values, parts, out = keys["scalar"](e)
            pipeline(e, N1, [(yout, 5), square, parts, (high, 1), values, out, (hidden, 3)]
                     + spread_out(e, high_part, jobs, 2))

        @blk.vector
        def _(v):
            init = Line(S, v, "kyinit")
            init.start(It(0, 0))
            keys["init"](init, v)
            stats, front, low, mid, back = (Line(S, v, f"l1dve{i}") for i in range(5))

            def spread(it):
                stats.start(it)
                S.wait_moved(v, "l1gather", it)
                row_stats(stats, v, S, T, x[it.p][:, :], "l1")

            def norm(it):
                front.start(it)
                normed(front, v, S, T, x[it.p][:, :], "l1", it)

            def parts(it):
                low.start(it)
                S.wait(v, "l1xh", it)
                low(v.tensor_tensor(xhl[it.p][:, D:], T["xs"][it.p][:, :], xhl[it.p][:, 0:D], ALU.subtract), "l1xl")

            def evacuate(it):
                mid.start(it)
                S.wait(v, "l1T", it)
                S.wait(v, "l1mm1", it.back(2))
                mid(v.tensor_copy(xT[it.p][:, :, :], pT[:, :, :]), "l1xT")

            def hidden(it):
                back.start(it)
                S.wait(v, "l1sq", it)
                S.wait(v, "l1hh", it.back(2))
                back(v.tensor_tensor(h[it.p][:, :], sg[it.p][:, :], sq[it.p][:, :], ALU.mult), "l1h")
                S.wait(v, "l1hh", it)
                back(v.tensor_tensor(hl[it.p][:, :], h[it.p][:, :], hh[it.p][:, :], ALU.subtract), "l1hl")
            squares, scale, klow = keys["vector"](v)
            pipeline(v, N1, [scale, (spread, 1), squares, (norm, 1), klow, (evacuate, 2), (parts, 1), (hidden, 3)] + spread_out(v, low_part, jobs, 2))

        @blk.tensor
        def _(e):
            def up(it):
                ex = e.value_load(K["tab1"][0:1, bass.ds(it.n, 1)], min_val=0, max_val=E1 - 1)
                S.wait(e, "l1xT", it)
                S.wait(e, "l1sq", it.back(2))
                for f in range(KD):
                    terms = [(w, x0, k) for k in range(KD) for w, x0 in ((ch, 0), (ch, KD), (cl, 0))]
                    for j, (w, x0, k) in enumerate(terms):
                        last = e.matmul(pP[it.p][:, f * P:(f + 1) * P], w[:, bass.ds(ex * W + (k * D + f * P), P)],
                                        xT[it.p][:, x0 + k, :], start=j == 0, stop=j == len(terms) - 1)
                S.done(last, "l1mm1")

            def turn(it):
                S.wait(e, "l1xl", it)
                S.wait(e, "l1xT", it.back(1))
                S.done(transposes(e, pT, xhl[it.p], K["ident"][:, :], 2 * KD), "l1T")

            def down(it):
                ex = e.value_load(K["tab1"][0:1, bass.ds(it.n, 1)], min_val=0, max_val=E1 - 1)
                S.wait(e, "l1hl", it)
                S.wait(e, "l1y", it.back(1))
                terms = [(hx, w, k) for k in range(KD) for hx, w in ((hh, ch), (hh, cl), (hl, ch))]
                for j, (hx, w, k) in enumerate(terms):
                    last = e.matmul(pY[:, :], hx[it.p][:, k * P:(k + 1) * P], w[:, bass.ds(ex * W + k * D, D)],
                                    start=j == 0, stop=j == len(terms) - 1)
                S.done(last, "l1mm2")
            key_turn, key_project = keys["tensor"](e)
            pipeline(e, N1, [(turn, 2), (up, 3), key_turn, key_project, (down, 4)])


def split_terms(first, second, blocks):
    return [(x, w, k) for k in range(blocks) for x, w in ((first[0], second[0]), (first[0], second[1]), (first[1], second[0]))]


def phase_shared(nc, S, sb, ps, a, R, K, shared):
    W1, W2 = KD * FF, FB * D
    with ExitStack() as mem:
        w1, w2, cen = shared["w1"], shared["w2"], shared["cen"]
        b1r = sb(mem, "shb1r", [P, NS * FB])
        b1 = sb(mem, "shb1", [P, NS * FB])
        bias = sb(mem, "shbias", [P, NR])
        base = sb(mem, "shbase", [P, NR])
        pidx = [sb(mem, f"shpidx{i}", [P, 1], i32) for i in range(2)]
        tokb = [sb(mem, f"shtok{i}", [P, 1], i32) for i in range(2)]
        posb = [sb(mem, f"shposb{i}", [P, KR], i32) for i in range(2)]
        xin = [sb(mem, f"shxin{i}", [P, D]) for i in range(2)]
        y1 = [sb(mem, f"shy1{i}", [P, D]) for i in range(2)]
        x1 = [sb(mem, f"shx1{i}", [P, D]) for i in range(2)]
        r1 = sb(mem, "shr1", [P, NT * D])
        T = {"st": sb(mem, "shst", [P, 6]), "mv": sb(mem, "shmv", [P, 2]), "ve": sb(mem, "shve", [P, 1]),
             "rstd": sb(mem, "shrstd", [P, 1]), "rs": sb(mem, "shrs", [P, 1]),
             "xs": [sb(mem, f"shxs{i}", [P, D]) for i in range(2)]}
        xhl = [sb(mem, f"shxhl{i}", [P, 2 * D], f16) for i in range(2)]
        xT = [sb(mem, f"shxT{i}", [P, 2 * KD, P], f16) for i in range(2)]
        h = [sb(mem, f"shh{i}", [P, NS, FB * P]) for i in range(2)]
        hh = [sb(mem, f"shhh{i}", [P, NS, FB * P], f16) for i in range(2)]
        hl = [sb(mem, f"shhl{i}", [P, NS, FB * P], f16) for i in range(2)]
        xo = [sb(mem, f"shxo{i}", [P, D]) for i in range(2)]
        sig = [sb(mem, f"shsig{i}", [P, NR]) for i in range(2)]
        sc = sb(mem, "shsc", [P, NR])
        top = sb(mem, "shtop", [P, 8])
        ti = sb(mem, "shti", [P, 8], u32)
        tf = sb(mem, "shtf", [P, 8])
        oh = [sb(mem, f"shoh{i}", [P, KR, NR]) for i in range(2)]
        m = [sb(mem, f"shm{i}", [P, NR], f16) for i in range(2)]
        pos = sb(mem, "shpos", [P, NR])
        pk = sb(mem, "shpk", [P, KR, NR])
        pf = sb(mem, "shpf", [P, KR])
        pos2f = sb(mem, "shpos2f", [P, NT * KR])
        gs = sb(mem, "shgs", [P, 1])
        gr = sb(mem, "shgr", [P, 1])
        pT = [ps(mem, f"shpT{i}", [P, 2 * KD, P], f16) for i in range(2)]
        pH = [ps(mem, f"shpH{i}", [P, FB * P]) for i in range(NS)]
        pY = [ps(mem, f"shpY{i}", [P, D]) for i in range(2)]
        pR = ps(mem, "shpR", [P, NR])
        pC = ps(mem, "shpC", [P, 2, NR])
        blk = mem.enter_context(nc.Block())

        @blk.sync
        def _(e):
            e.dma_start(b1r[:, :], a["sb1"]).then_inc(S.sem("sh_small"), 16)
            e.dma_start(bias[:, :], bass.AP(a["bias"].tensor, 0, [[0, P], [1, NR]])).then_inc(S.sem("sh_small"), 16)

            def load(it):
                S.wait(e, "shx1", it.back(2))
                S.static(e)
                S.moved(e.dma_start(xin[it.p][:, :], a["x"][bass.ds(it.n * P, P), :]), "shxin", it)

            def store_norm(it):
                S.wait(e, "shxl", it)
                S.static(e)
                S.moved(e.dma_start(R["xn2"][bass.ds(it.n * P, P), :], xhl[it.p][:, :]), "shxnout", it)

            def store(it):
                S.wait(e, "shxo", it)
                S.static(e)
                S.moved(e.dma_start(R["x2a"][bass.ds(it.n * P, P), :], xo[it.p][:, :]), "shstore", it)
            pipeline(e, NT, [(load, 0), (store_norm, 2), (store, 6)])
            for p in range(2):
                S.wait_moved(e, "shstore", It(NT // 2 - 1, p))
                S.wait_moved(e, "shxnout", It(NT // 2 - 1, p))

        @blk.gpsimd
        def _(e):
            def gather(it):
                S.wait_moved(e, "shgather", it.back(2))
                S.static(e)
                S.done(e.tensor_copy(pidx[it.p][:, :], K["pos1"][:, bass.ds(it.n, 1)]), "shpidx")
                S.wait(e, "shpidx", it)
                S.wait(e, "shx1", it.back(2))
                S.static(e)
                S.moved(e.indirect_dma_start(
                    out=y1[it.p][:, :], out_offset=None, in_=R["y1s"],
                    in_offset=bass.IndirectOffsetOnAxis(ap=pidx[it.p][:, :], axis=0)), "shgather", it)

            def scatter(it):
                S.wait_moved(e, "shscatter", it.back(2), KR)
                S.static(e)
                S.done(e.tensor_copy(tokb[it.p][:, :], K["tok"][:, bass.ds(it.n, 1)]), "shtokb")
                S.wait(e, "shtokb", it)
                S.wait(e, "shposb", it)
                S.static(e)
                for k in range(KR):
                    S.moved(e.indirect_dma_start(
                        out=R["list2"], out_offset=bass.IndirectOffsetOnAxis(ap=posb[it.p][:, k:k + 1], axis=0),
                        in_=tokb[it.p][:, :], in_offset=None), "shscatter", it)

            def first_residual(it):
                S.wait_moved(e, "shgather", it)
                S.wait_moved(e, "shxin", it)
                S.wait(e, "shr1", it.back(2))
                S.static(e)
                S.done(e.tensor_tensor(x1[it.p][:, :], y1[it.p][:, :], xin[it.p][:, :], ALU.add), "shx1")

            pipeline(e, NT, [(lambda it: pool_rstd(e, S, T, K, "sh", it), 2), (gather, 0),
                             (first_residual, 1), (scatter, 6)])
            for p in range(2):
                S.wait_moved(e, "shscatter", It(NT // 2 - 1, p), KR)

        @blk.scalar
        def _(e):
            e.wait_ge(S.sem("sh_small"), 32)
            S.done(e.activation(b1[:, :], b1r[:, :], ACT.Copy, scale=SA), "sh_b1")
            e.wait_ge(S.sem("sh_b1"), 1)
            e.wait_ge(S.sem("sh_init"), 1)

            def high(it):
                S.wait(e, "shxs", it)
                S.wait(e, "shT", it.back(2))
                S.wait_moved(e, "shxnout", it.back(2))
                S.done(e.activation(xhl[it.p][:, 0:D], T["xs"][it.p][:, :], ACT.Copy), "shxh")

            def hidden(it):
                S.wait(e, "shrouted", it)
                S.done(e.activation(sig[it.p][:, :], pR[:, :], ACT.Sigmoid, scale=UNSCALE), "shsig")
                S.wait(e, "shup", it)
                S.wait(e, "shhl", it.back(2))
                for s in range(NS):
                    for f in range(FB):
                        n = FLAST if f == FB - 1 else P
                        last = e.activation(h[it.p][0:n, s, f * P:(f + 1) * P], pH[s][0:n, f * P:(f + 1) * P],
                                            ACT.Relu, bias=b1[0:n, s * FB + f:s * FB + f + 1], scale=UNSCALE * SA)
                S.done(last, "shh")
                S.wait(e, "shh", it)
                S.wait(e, "shdown", it.back(2))
                S.done(e.activation(hh[it.p][:, :, :], h[it.p][:, :, :], ACT.Copy), "shhh")

            def evacuate(it):
                S.wait(e, "shT", it)
                S.wait(e, "shup", it.back(2))
                S.done(e.activation(xT[it.p][:, :, :], pT[it.p][:, :, :], ACT.Copy), "shxT")
            pipeline(e, NT, [(high, 2), (evacuate, 3), (hidden, 4)])

        @blk.vector
        def _(v):
            init = Line(S, v, "shinit")
            init.start(It(0, 0))
            for i in range(2):
                init(v.memset(h[i][FLAST:P, :, :], 0.0))
                init(v.memset(h[i][FLAST:FLAST + 1, :, 2 * P:], SA))
            init(v.tensor_scalar(base[:, :], K["iota"][:, :], float(CAP), None, ALU.mult))
            init(v.memset(sc[:, :], 0.0), "sh_init")
            v.wait_ge(S.sem("sh_small"), 32)
            stats, front, low, rt, back, last_, fin = (Line(S, v, f"shdve{i}") for i in range(7))

            def spread(it):
                stats.start(it)
                S.wait(v, "shx1", it)
                row_stats(stats, v, S, T, x1[it.p][:, :], "sh")

            def norm(it):
                front.start(it)
                normed(front, v, S, T, x1[it.p][:, :], "sh", it)
                front(v.scalar_tensor_tensor(r1[:, bass.ds(it.n * D, D)], T["xs"][it.p][:, :], K["gate"][:, 5:6],
                                             x1[it.p][:, :], ALU.mult, ALU.add), "shr1")

            def parts(it):
                low.start(it)
                S.wait(v, "shxh", it)
                low(v.tensor_tensor(xhl[it.p][:, D:], T["xs"][it.p][:, :], xhl[it.p][:, 0:D], ALU.subtract), "shxl")

            def choose(it):
                rt.start(it)
                S.wait(v, "shsig", it)
                rt(v.tensor_tensor(sc[:, :], sig[it.p][:, :], bias[:, :], ALU.add))
                S.static(v)
                rt(v.max(top[:, :], sc[:, :]))
                S.static(v)
                rt(v.max_index(ti[:, :], top[:, :], sc[:, :]))
                rt(v.tensor_copy(tf[:, :], ti[:, :]))
                rt(v.tensor_tensor(oh[it.p][:, :, :], bcast(K["iota"][:, 0:1], [(0, KR), (1, NR)]),
                                   bcast(tf[:, 0:1], [(1, KR), (0, NR)]), ALU.is_equal))
                with nc.allow_low_precision(reason="sums of at most one one"):
                    rt(v.tensor_reduce(m[it.p][:, :], oh[it.p][:, :, :].rearrange("p k e -> p e k"), AX.X, ALU.add), "shm")
                rt(v.tensor_reduce(gs[:, :], top[:, 0:KR], AX.X, ALU.add))
                rt(v.tensor_scalar(gs[:, :], gs[:, :], 1e-8, None, ALU.max))
                rt(v.reciprocal(gr[:, :], gs[:, :]))
                rt(v.tensor_scalar(K["g2f"][:, bass.ds(it.n * KR, KR)], top[:, 0:KR],
                                   gr[:, :], K["gate"][:, 1:2], ALU.mult, ALU.mult))

            def place(it):
                last_.start(it)
                S.wait(v, "shcount", it)
                last_(v.tensor_tensor(pos[:, :], pC[:, 0, :], base[:, :], ALU.add))
                last_(v.tensor_tensor(base[:, :], pC[:, 1, :], base[:, :], ALU.add), "shbase")
                last_(v.tensor_tensor(pk[:, :, :], oh[it.p][:, :, :], bcast(pos[:, 0:1], [(0, KR), (1, NR)]), ALU.mult))
                last_(v.tensor_reduce(pf[:, :], pk[:, :, :], AX.X, ALU.add))
                last_(v.tensor_copy(pos2f[:, bass.ds(it.n * KR, KR)], pf[:, :]))
                S.wait_moved(v, "shscatter", it.back(2), KR)
                last_(v.tensor_copy(posb[it.p][:, :], pf[:, :]), "shposb")

            def hidden(it):
                back.start(it)
                S.wait(v, "shhh", it)
                S.wait(v, "shdown", it.back(2))
                back(v.tensor_tensor(hl[it.p][:, :, :], h[it.p][:, :, :], hh[it.p][:, :, :], ALU.subtract), "shhl")

            def finish(it):
                fin.start(it)
                S.wait(v, "shdown", it)
                S.wait_moved(v, "shstore", it.back(2))
                fin(v.scalar_tensor_tensor(xo[it.p][:, :], pY[it.p][:, :], K["gate"][:, 6:7], r1[:, bass.ds(it.n * D, D)],
                                           ALU.mult, ALU.add), "shxo")
            pipeline(v, NT, [(spread, 2), (finish, 6), (norm, 2), (place, 5), (parts, 2),
                             (choose, 4), (hidden, 4)])
            v.wait_ge(S.sem("shbase"), NT)
            tail = Line(S, v, "shtail")
            tail.start(It(0, 0))
            cnt = sb(mem, "shcnt", [P, NR])
            tail(v.scalar_tensor_tensor(cnt[:, :], K["iota"][:, :], -float(CAP), base[:, :], ALU.mult, ALU.add))
            make_table(tail, v, mem, sb, "t2", NR, N2, cnt[:, :], K, K["tab2"][0:1, 0, :], K["tab2"][0:1, 1, :],
                       pos2f[:, :], K["pos2"][:, :])

        @blk.tensor
        def _(e):
            def up(it):
                S.wait(e, "shxT", it)
                S.wait(e, "shsig", it.back(1))
                xs = (xT[it.p][:, 0:KD, :], xT[it.p][:, KD:, :])
                terms = split_terms(xs, cen, KD)
                for j, (x, w, k) in enumerate(terms):
                    last = e.matmul(pR[:, :], x[:, k, :], w[:, k * NR:(k + 1) * NR], start=j == 0, stop=j == len(terms) - 1)
                S.done(last, "shrouted")
                S.wait(e, "shh", it.back(1))
                for s in range(NS):
                    for f in range(FB):
                        n = FLAST if f == FB - 1 else P
                        terms = split_terms(w1, xs, KD)
                        for j, (w, x, k) in enumerate(terms):
                            o = s * W1 + k * FF + f * P
                            last = e.matmul(pH[s][0:n, f * P:(f + 1) * P], w[:, o:o + n], x[:, k, :],
                                            start=j == 0, stop=j == len(terms) - 1)
                S.done(last, "shup")

            def turn(it):
                S.wait(e, "shxl", it)
                S.wait(e, "shxT", it.back(2))
                S.done(transposes(e, pT[it.p], xhl[it.p], K["ident"][:, :], 2 * KD), "shT")

            def down(it):
                S.wait(e, "shhl", it)
                S.wait(e, "shxo", it.back(2))
                terms = [(x, w, k, s) for s in range(NS) for x, w, k in split_terms((hh[it.p], hl[it.p]), w2, FB)]
                for j, (x, w, k, s) in enumerate(terms):
                    n = FLAST + 1 if k == FB - 1 else P
                    last = e.matmul(pY[it.p][:, :], x[0:n, s, k * P:(k + 1) * P], w[0:n, s * W2 + k * D:s * W2 + (k + 1) * D],
                                    start=j == 0, stop=j == len(terms) - 1)
                S.done(last, "shdown")

            def count(it):
                S.wait(e, "shm", it)
                S.wait(e, "shbase", it.back(1))
                e.matmul(pC[:, 0, :], K["tri"][:, :], m[it.p][:, :], start=True, stop=True)
                S.done(e.matmul(pC[:, 1, :], K["ones"][:, :], m[it.p][:, :], start=True, stop=True), "shcount")
            pipeline(e, NT, [(turn, 3), (count, 5), (up, 4), (down, 5)])


def phase_routed(nc, S, sb, ps, a, R, K):
    W1, W2 = KD * FF, FB * D
    EW = 2 * (W1 + W2)
    NP = 4
    with ExitStack() as mem:
        wt = sb(mem, "rowt", [P, NR * EW], f16)
        raw = wt[:, :].bitcast(f32)
        b1 = sb(mem, "rob1", [P, FF])
        piece = [sb(mem, f"ropiece{i}", [P, W2 // NP]) for i in range(2)]
        last_row = R["list2"].shape[0] - P
        direct = NR - 2
        pieces = [("rw1", W1 // NP, c, c, W1) for c in range(0, W1, W1 // NP)]
        pieces += [("rw2", W2 // NP, c, 2 * W1 + c, W2) for c in range(0, W2, W2 // NP)]
        idx = [sb(mem, f"roidx{i}", [P, 1], i32) for i in range(2)]
        xg = [sb(mem, f"roxg{i}", [P, 2 * D], f16) for i in range(2)]
        xT = [sb(mem, f"roxT{i}", [P, 2 * KD, P], f16) for i in range(2)]
        h = sb(mem, "roh", [P, FF + 1])
        hhl = [sb(mem, f"rohhl{i}", [P, 2, FF + 2], f16) for i in range(2)]
        hT = sb(mem, "rohT", [P, 2 * FB, P], f16)
        y = sb(mem, "roy", [P, D])
        pT = [ps(mem, f"ropT{i}", [P, 2 * KD, P], f16) for i in range(2)]
        pH = [ps(mem, f"ropH{i}", [P, FF]) for i in range(2)]
        pUw = ps(mem, "ropU", [P, FB * P])
        pU = pUw[:, :].bitcast(f16).rearrange("p (b n) -> p b n", n=P)
        pY = [ps(mem, f"ropY{i}", [P, D]) for i in range(2)]
        halves = ((0, 0, W1), (2 * W1, W1, W2))
        blk = mem.enter_context(nc.Block())

        def expert(n):
            return n * EW, (n + 2) * (EW // 2)

        @blk.sync
        def _(e):
            def weights(n, it):
                at = expert(n)[1]
                S.wait(e, "rohi", it.back(2), 2)
                S.moved(e.dma_start(raw[:, bass.ds(at, W1)], a["rw1"][bass.ds(n, 1)].rearrange("e p c -> (e p) c")), "roraw", it)
                S.moved(e.dma_start(raw[:, bass.ds(at + W1, W2)], a["rw2"][bass.ds(n, 1)].rearrange("e p c -> (e p) c")), "roraw", it)

            def small(it):
                for j, (src, cols, at, _, _) in enumerate(pieces):
                    n = (it.n - direct) * 2 * NP + j
                    if n >= 2:
                        e.wait_ge(S.sem("ropl"), n - 1)
                    e.dma_start(piece[j % 2][:, 0:cols], a[src][it.n][:, at:at + cols]).then_inc(S.sem(f"ropiece{j % 2}"), 16)

            def indices(it):
                row = e.value_load(K["tab2"][0:1, 1, bass.ds(it.n, 1)], min_val=0, max_val=last_row)
                S.wait_moved(e, "rogather", it.back(2))
                S.static(e)
                S.moved(e.dma_start(idx[it.p][:, :], R["list2"][bass.ds(row, P), :]), "roidx", it)

            def store(it):
                S.wait(e, "roy", it)
                S.static(e)
                S.moved(e.dma_start(R["ys"][bass.ds(it.n * P, P), :], y[:, :]), "rostore", it)
            def bias(it):
                ex = e.value_load(K["tab2"][0:1, 0, bass.ds(it.n, 1)], min_val=0, max_val=NR - 1)
                S.wait(e, "robias", it.back(1))
                S.static(e)
                e.dma_start(b1[:, :], a["rb1"][bass.ds(ex, 1), :].to_broadcast((P, FF))).then_inc(S.sem("rob1"), 16)
            ahead = 1
            weights(0, It(0, 0))
            for n in range(1, ahead):
                weights(n, It(n // 2, n % 2))
            pipeline(e, N2, [(bias, 3), (indices, 0), (store, 6),
                             (lambda it: weights(it.n, it), -ahead, ahead, direct), (small, 0, direct, NR)])
            for p in range(2):
                S.wait_moved(e, "rostore", It(N2 // 2 - 1, p))

        @blk.gpsimd
        def _(e):
            def gather(it):
                S.wait_moved(e, "roidx", it)
                S.wait(e, "roT", it.back(2))
                S.static(e)
                S.moved(e.indirect_dma_start(
                    out=xg[it.p][:, :], out_offset=None, in_=R["xn2"],
                    in_offset=bass.IndirectOffsetOnAxis(ap=idx[it.p][:, :], axis=0)), "rogather", it)
            pipeline(e, N2, [(gather, 0)])

        @blk.scalar
        def _(e):
            e.wait_ge(S.sem("ro_init"), 1)

            def high(it):
                S.wait_moved(e, "roraw", it, 2)
                S.wait(e, "rolo", it.back(2), 2)
                to, at = expert(it.n)
                S.static(e)
                for o, x, cols in halves:
                    S.done(e.activation(wt[:, bass.ds(to + o, cols)], raw[:, bass.ds(at + x, cols)], ACT.Copy, scale=SW), "rohi")

            def small(it):
                for j, (src, cols, at, o, _) in enumerate(pieces):
                    n = (it.n - direct) * 2 * NP + j
                    e.wait_ge(S.sem(f"ropiece{j % 2}"), 16 * (n // 2 + 1))
                    if j == 0:
                        e.wait_ge(S.sem("rolo"), 2 * (it.n - 1))
                    S.done(e.activation(wt[:, it.n * EW + o:it.n * EW + o + cols], piece[j % 2][:, 0:cols], ACT.Copy, scale=SW), "roph")

            def yout(it):
                S.wait(e, "rodown", it)
                S.wait_moved(e, "rostore", it.back(1))
                S.done(e.activation(y[:, :], pY[it.p][:, :], ACT.Copy, scale=UNSCALE), "roy")

            def hidden(it):
                S.wait(e, "robias", it)
                S.done(e.activation(h[:, 0:FF], h[:, 0:FF], ACT.Relu, scale=SA), "roh")
                S.wait(e, "roh", it)
                S.wait(e, "roU", it.back(2))
                S.done(e.activation(hhl[it.p][:, 0, 0:FF + 1], h[:, :], ACT.Copy), "rohh")
            pipeline(e, N2, [(yout, 6), (hidden, 3), (high, 0, 0, direct), (small, 0, direct, NR)])

        @blk.vector
        def _(v):
            init = Line(S, v, "roinit")
            init.start(It(0, 0))
            init(v.memset(h[:, FF:], SA))
            init(v.memset(pUw[:, :], 0.0), "ro_init")
            mid, pre, back, last = (Line(S, v, f"rodve{i}") for i in range(4))

            def evacuate(it):
                mid.start(it)
                S.wait(v, "roT", it)
                S.wait(v, "roup", it.back(2))
                mid(v.tensor_copy(xT[it.p][:, :, :], pT[it.p][:, :, :]), "roxT")

            def hidden(it):
                pre.start(it)
                S.wait(v, "roup", it)
                S.wait(v, "rohl", it.back(1))
                v.wait_ge(S.sem("rob1"), (it.n + 1) * 16)
                pre(v.scalar_tensor_tensor(h[:, 0:FF], pH[it.p][:, :], UNSCALE, b1[:, :], ALU.mult, ALU.add), "robias")

            def parts(it):
                back.start(it)
                S.wait(v, "rohh", it)
                back(v.tensor_tensor(hhl[it.p][:, 1, 0:FF + 1], h[:, :], hhl[it.p][:, 0, 0:FF + 1], ALU.subtract), "rohl")

            def turned(it):
                last.start(it)
                S.wait(v, "roU", it)
                S.wait(v, "rodown", it.back(1))
                last(v.tensor_copy(hT[:, :, :], pU[:, :, :]), "rohT")

            def low(it):
                to, at = expert(it.n)
                for i, (o, x, cols) in enumerate(halves):
                    v.wait_ge(S.sem("rohi"), it.n * 2 + i + 1)
                    S.done(v.scalar_tensor_tensor(wt[:, bass.ds(to + o + cols, cols)], raw[:, bass.ds(at + x, cols)], SW,
                                                  wt[:, bass.ds(to + o, cols)], ALU.mult, ALU.subtract), "rolo")

            def small(it):
                for j, (src, cols, at, o, half) in enumerate(pieces):
                    v.wait_ge(S.sem("roph"), (it.n - direct) * 2 * NP + j + 1)
                    o = it.n * EW + o
                    last = v.scalar_tensor_tensor(wt[:, o + half:o + half + cols], piece[j % 2][:, 0:cols], SW,
                                                  wt[:, o:o + cols], ALU.mult, ALU.subtract)
                    S.done(last, "ropl")
            pipeline(v, N2, [(evacuate, 2), (hidden, 3), (turned, 4), (parts, 3), (low, 0, 0, direct), (small, 0, direct, NR)])

        @blk.tensor
        def _(e):
            ex = {}

            def look(it):
                for name, tile in (("up", it), ("down", it.back(2))):
                    if not isinstance(tile.n, int) or 0 <= tile.n < N2:
                        ex[name] = e.value_load(K["tab2"][0:1, 0, bass.ds(tile.n, 1)], min_val=0, max_val=NR - 1)

            def ready(it):
                S.wait(e, "rolo", it, 2)

            def small_ready(it):
                e.wait_ge(S.sem("ropl"), 2 * NP * (it.n - direct + 1))

            def up(it):
                S.wait(e, "roxT", it)
                S.wait(e, "robias", it.back(2))
                xs = (xT[it.p][:, 0:KD, :], xT[it.p][:, KD:, :])
                terms = split_terms(xs, (0, W1), KD)
                for j, (x, w, k) in enumerate(terms):
                    last = e.matmul(pH[it.p][:, :], x[:, k, :], wt[:, bass.ds(ex["up"] * EW + (w + k * FF), FF)],
                                    start=j == 0, stop=j == len(terms) - 1)
                S.done(last, "roup")

            def turn_hidden(it):
                S.wait(e, "rohl", it)
                S.wait(e, "rohT", it.back(1))
                for i in range(2):
                    for f in range(FB):
                        n = FLAST + 1 if f == FB - 1 else P
                        last = e.transpose(pU[0:n, i * FB + f, :], hhl[it.p][:, i, f * P:f * P + n], K["ident"][:, :])
                S.done(last, "roU")

            def turn(it):
                S.wait_moved(e, "rogather", it)
                S.wait(e, "roxT", it.back(2))
                S.done(transposes(e, pT[it.p], xg[it.p], K["ident"][:, :], 2 * KD), "roT")

            def down(it):
                S.wait(e, "rohT", it)
                S.wait(e, "roy", it.back(2))
                terms = split_terms((0, FB), (0, W2), FB)
                for j, (x, w, k) in enumerate(terms):
                    n = FLAST + 1 if k == FB - 1 else P
                    last = e.matmul(pY[it.p][:, :], hT[0:n, x + k, :],
                                    wt[0:n, bass.ds(ex["down"] * EW + (2 * W1 + w + k * D), D)],
                                    start=j == 0, stop=j == len(terms) - 1)
                S.done(last, "rodown")
            pipeline(e, N2, [(look, 3, 0, N2 + 2), (turn, 2), (ready, 3, 0, direct), (small_ready, 3, direct, NR), (up, 3),
                             (turn_hidden, 4), (down, 5)],
                     unroll=4)


def phase_queries(nc, S, sb, ps, a, R, K):
    W = KD * D
    with ExitStack() as mem:
        wq = [sb(mem, f"quw{i}", [P, W], f16) for i in range(2)]
        stage = [sb(mem, f"qustage{i}", [P, W]) for i in range(2)]
        pidx = [sb(mem, f"qupidx{i}", [P, KR], i32) for i in range(2)]
        xin = [sb(mem, f"quxin{i}", [P, D]) for i in range(2)]
        yg = [sb(mem, f"quyg{i}", [P, KR, D]) for i in range(2)]
        x2 = [sb(mem, f"qux2{i}", [P, D]) for i in range(2)]
        T = {"st": sb(mem, "qust", [P, 6]), "mv": sb(mem, "qumv", [P, 2]), "ve": sb(mem, "quve", [P, 1]),
             "rstd": sb(mem, "qurstd", [P, 1]), "rs": sb(mem, "qurs", [P, 1]),
             "xs": [sb(mem, f"quxs{i}", [P, D]) for i in range(2)]}
        xhl = [sb(mem, f"quxhl{i}", [P, 2 * D], f16) for i in range(2)]
        xT = [sb(mem, f"quxT{i}", [P, 2 * KD, P], f16) for i in range(2)]
        sq = sb(mem, "qusq", [P, D])
        ss = sb(mem, "quss", [P, NH])
        rr = sb(mem, "qurr", [P, NH])
        qn = [sb(mem, f"quqn{i}", [P, D]) for i in range(2)]
        qp = [sb(mem, f"quqp{i}", [P, 4 * D], f16) for i in range(2)]
        qt = [sb(mem, f"quqt{i}", [P, 4 * D], f16) for i in range(2)]
        pT = [ps(mem, f"qupT{i}", [P, 2 * KD, P], f16) for i in range(2)]
        pQ = [ps(mem, f"qupQ{i}", [P, D]) for i in range(2)]
        pS = [ps(mem, f"qupS{i}", [P, NH // 2, P], f16) for i in range(2)]
        jobs = [(a["wqT"], wq[0][:, :], wq[1][:, :], W)]
        blk = mem.enter_context(nc.Block())

        @blk.sync
        def _(e):
            load_split(S, e, None, None, jobs, stage, "qw")

            def load(it):
                S.wait(e, "qux2", it.back(2))
                S.static(e)
                S.moved(e.dma_start(xin[it.p][:, :], R["x2a"][bass.ds(it.n * P, P), :]), "quxin", it)

            def store_x(it):
                S.wait(e, "qux2", it)
                S.static(e)
                S.moved(e.dma_start(R["x2"][bass.ds(it.n * P, P), :], x2[it.p][:, :]), "quxout", it)

            def store(it):
                S.wait(e, "quqt", it)
                S.static(e)
                S.moved(e.dma_start(R["qst"][bass.ds(it.n, 1)].rearrange("a p c -> (a p) c"), qt[it.p][:, :]), "ququt", it)
            pipeline(e, NT, [(load, 0), (store_x, 1), (store, 7)])
            for p in range(2):
                S.wait_moved(e, "quxout", It(NT // 2 - 1, p))
                S.wait_moved(e, "ququt", It(NT // 2 - 1, p))

        @blk.gpsimd
        def _(e):
            def gather(it):
                S.wait_moved(e, "qugather", it.back(2), KR)
                S.wait(e, "qux2", it.back(2))
                S.static(e)
                S.done(e.tensor_copy(pidx[it.p][:, :], K["pos2"][:, bass.ds(it.n * KR, KR)]), "qupidx")
                S.wait(e, "qupidx", it)
                S.static(e)
                for k in range(KR):
                    S.moved(e.indirect_dma_start(
                        out=yg[it.p][:, k, :], out_offset=None, in_=R["ys"],
                        in_offset=bass.IndirectOffsetOnAxis(ap=pidx[it.p][:, k:k + 1], axis=0)), "qugather", it)

            def low(it):
                S.wait(e, "quxh", it)
                S.static(e)
                S.done(e.tensor_tensor(xhl[it.p][:, D:], T["xs"][it.p][:, :], xhl[it.p][:, 0:D], ALU.subtract), "quxl")
            pipeline(e, NT, [(lambda it: pool_rstd(e, S, T, K, "qu", it), 2), (gather, 0), (low, 2)])

        @blk.scalar
        def _(e):
            load_split(S, None, e, None, jobs, stage, "qw")

            def high(it):
                S.wait(e, "quxs", it)
                S.wait(e, "quT", it.back(2))
                S.done(e.activation(xhl[it.p][:, 0:D], T["xs"][it.p][:, :], ACT.Copy), "quxh")

            def square(it):
                S.wait(e, "quproj", it)
                S.wait(e, "qrms", it.back(1))
                S.done(e.activation(sq[:, :], pQ[it.p][:, :], ACT.Square, scale=UNSCALE), "qrsq")

            def root(it):
                S.wait(e, "qrms", it)
                S.done(e.activation(ss[:, :], ss[:, :], ACT.Sqrt), "qrrt")

            def parts(it):
                S.wait(e, "qrn", it)
                S.wait(e, "quS", it.back(2))
                S.done(e.activation(part_pair(qp[it.p][:, :], 0, 1), twice(qn[it.p][:, :]), ACT.Copy), "quhi")

            def evacuate(it):
                S.wait(e, "quS", it)
                S.wait_moved(e, "ququt", it.back(2))
                S.done(e.activation(qt[it.p][:, :], pS[it.p][:, :, :].rearrange("p j n -> p (j n)"), ACT.Copy), "quqt")

            def evacuate_x(it):
                S.wait(e, "quT", it)
                S.wait(e, "quproj", it.back(2))
                S.done(e.activation(xT[it.p][:, :, :], pT[it.p][:, :, :], ACT.Copy), "quxT")
            pipeline(e, NT, [(square, 5), (parts, 6), (root, 5), (evacuate_x, 3), (high, 2), (evacuate, 7)])

        @blk.vector
        def _(v):
            load_split(S, None, None, v, jobs, stage, "qw")
            sum_, stats, front, heads0, heads1, heads2 = (Line(S, v, f"qudve{i}") for i in range(6))

            def combine(it):
                sum_.start(it)
                S.wait_moved(v, "qugather", it, KR)
                S.wait_moved(v, "quxin", it)
                S.wait_moved(v, "quxout", it.back(2))
                for k in range(KR):
                    sum_(v.scalar_tensor_tensor(x2[it.p][:, :], yg[it.p][:, k, :], K["g2f"][:, bass.ds(it.n * KR + k, 1)],
                                                (xin if k == 0 else x2)[it.p][:, :], ALU.mult, ALU.add),
                         "qux2" if k == KR - 1 else None)

            def spread(it):
                stats.start(it)
                S.wait(v, "qux2", it)
                row_stats(stats, v, S, T, x2[it.p][:, :], "qu")

            def norm(it):
                front.start(it)
                S.wait(v, "quxl", it.back(2))
                normed(front, v, S, T, x2[it.p][:, :], "qu", it)

            def squares(it):
                heads0.start(it)
                head_squares(heads0, v, S, "qr", it, sq[:, :], ss[:, :])

            def scale(it):
                heads1.start(it)
                S.wait(v, "quhi", it.back(2))
                S.wait(v, "qrrt", it)
                heads1(v.reciprocal(rr[:, :], ss[:, :]))
                head_scale(heads1, v, S, "qr", it, pQ[it.p][:, :], rr[:, :], qn[it.p][:, :], SA * UNSCALE)

            def parts(it):
                heads2.start(it)
                S.wait(v, "quhi", it)
                heads2(v.tensor_tensor(part_pair(qp[it.p][:, :], 2, 1), twice(qn[it.p][:, :]),
                                       bcast(qp[it.p][:, :], [(4 * HD, NH), (0, 2), (1, HD)]), ALU.subtract), "qulo")
            pipeline(v, NT, [(spread, 2), (squares, 5), (norm, 2), (parts, 6), (scale, 5), (combine, 1)])

        @blk.tensor
        def _(e):
            e.wait_ge(S.sem("qwlo"), len(jobs))

            def project(it):
                S.wait(e, "quxT", it)
                S.wait(e, "qrn", it.back(2))
                terms = split_terms((xT[it.p][:, 0:KD, :], xT[it.p][:, KD:, :]), wq, KD)
                for j, (x, w, k) in enumerate(terms):
                    last = e.matmul(pQ[it.p][:, :], x[:, k, :], w[:, k * D:(k + 1) * D],
                                    start=j == 0, stop=j == len(terms) - 1)
                S.done(last, "quproj")

            def turn(it):
                S.wait(e, "quxl", it)
                S.wait(e, "quxT", it.back(2))
                S.done(transposes(e, pT[it.p], xhl[it.p], K["ident"][:, :], 2 * KD), "quT")

            def stack(it):
                S.wait(e, "qulo", it)
                S.wait(e, "quqt", it.back(2))
                S.done(transposes(e, pS[it.p], qp[it.p], K["ident"][:, :], NH // 2), "quS")
            pipeline(e, NT, [(turn, 3), (project, 4), (stack, 7)])


def phase_attention(nc, S, sb, ps, a, R, K, out):
    G = NH // 4
    NG = BATCH * G
    with ExitStack() as keep:
        o = sb(keep, "o", [P, NT * D])
        ident = sb(keep, "ident32", [P, P])
        oh = sb(keep, "laoh", [P, NT * NTILE])
        xs = sb(keep, "laxs", [P, NT * DSL])
        lo, hi = sb(keep, "lalo", [P, NT]), sb(keep, "lahi", [P, NT])
        kept = (oh, xs, lo, hi)
        with ExitStack() as mem:
            q = [sb(mem, f"atq{i}", [P, 4, 2, P], f16) for i in range(2)]
            k = [sb(mem, f"atk{i}", [P, 4, 2, 2, P], f16) for i in range(2)]
            vv = [sb(mem, f"atv{i}", [P, 4, 4 * (HD + 1)]) for i in range(2)]
            pr = [sb(mem, f"atp{i}", [P, 2 * SEQ]) for i in range(4)]
            oT = [sb(mem, f"atoT{i}", [P, SEQ]) for i in range(2)]
            rc = sb(mem, "atrc", [P, 4, 4])
            pS = [ps(mem, f"atpS{i}", [P, 2 * SEQ]) for i in range(2)]
            pO = [ps(mem, f"atpO{i}", [P, SEQ]) for i in range(2)]
            pX = ps(mem, "atpX", [P, 4, P])
            choice = choice_stages(nc, S, sb, mem, a, R, K, o, kept)
            blk = mem.enter_context(nc.Block())

            @blk.sync
            def _(e):
                e.dma_start(ident[:, :], a["c_ident32"]).then_inc(S.sem("at_ident"), 16)
                e.wait_ge(S.sem("at_init"), 1)
                def load(it):
                    b, g = it.n // G, it.n % G
                    S.wait(e, "atqk", it.back(2), 8)
                    S.wait(e, "atpv", it.back(2), 4)
                    S.static(e)
                    tiles = R["qst"].rearrange("(b t) p c -> b p t c", b=BATCH)
                    S.moved(e.dma_start(q[it.p][:, :, :, :].rearrange("p t j n -> p t (j n)"),
                                        tiles[bass.ds(b, 1), :, :, bass.ds(g * 2 * P, 2 * P)].rearrange("b p t c -> (b p) t c")),
                            "atin", it)
                    tiles = R["kst"].rearrange("(b t) p c -> b p t c", b=BATCH)
                    for s in range(2):
                        r = slice(64 * s, 64 * s + 64)
                        S.moved(e.dma_start(k[it.p][r, :, s, :, :].rearrange("p t j n -> p t (j n)"),
                                            tiles[bass.ds(b, 1), r, :, bass.ds(g * 2 * P, 2 * P)].rearrange("b p t c -> (b p) t c")),
                                "atin", it)
                    tiles = R["vst"].rearrange("(b t) p c -> b p t c", b=BATCH)
                    V = 4 * (HD + 1)
                    S.moved(e.dma_start(vv[it.p][:, :, :], tiles[bass.ds(b, 1), :, :, bass.ds(g * V, V)].rearrange("b p t c -> (b p) t c")),
                            "atin", it)
                for it in (It(0, 0), It(0, 1)):
                    load(it)
                choice["sync"][0](e)
                pipeline(e, NG, [(load, 0, 2, NG)] + choice["sync"][1](e))

            @blk.tensor
            def _(e):
                e.wait_ge(S.sem("at_ident"), 16)

                def scores(it, m):
                    for j in range(2):
                        u = 2 * m + j
                        if not isinstance(it.n, int) or it.n * 8 + u >= 2:
                            e.wait_ge(S.sem("atexp"), it.n * 8 + (u - 1))
                        for s in range(2):
                            last = e.matmul(pS[j][:, s * SEQ:(s + 1) * SEQ], k[it.p][:, m, s, j, :],
                                            q[it.p][:, :, j, :], start=True, stop=True)
                        S.done(last, "atqk")

                def weigh(it, m):
                    e.wait_ge(S.sem("atexp"), it.n * 8 + (2 * m + 2))
                    if m == 0:
                        S.wait(e, "atoT", it.back(2))
                    for i in range(4):
                        n = HD + 1
                        last = e.matmul(pO[it.p][32 * i:32 * i + n, :], vv[it.p][:, m, i * n:(i + 1) * n],
                                        pr[(2 * m + i // 2) % 4][:, (i % 2) * SEQ:(i % 2 + 1) * SEQ],
                                        start=m == 0, stop=m == 3)
                    S.done(last, "atpv")

                def first(it):
                    S.wait_moved(e, "atin", it, 4)
                    scores(it, 0)

                def rest(it):
                    for m in range(1, 4):
                        scores(it, m)
                        weigh(it, m - 1)

                def turn(it):
                    S.wait(e, "atoT", it)
                    S.wait(e, "ato", it.back(1))
                    for t in range(4):
                        last = e.transpose(pX[:, t, :], oT[it.p][:, t * P:(t + 1) * P], ident[:, :])
                    S.done(last, "atX")
                pipeline(e, NG, [(first, 1), (lambda it: weigh(it, 3), 2), (rest, 1), (turn, 2)])

            @blk.gpsimd
            def _(e):
                pipeline(e, NG, choice["gpsimd"](e))

            @blk.scalar
            def _(e):
                choice["scalar"][0](e)

                def exps(it):
                    for u in range(8):
                        e.wait_ge(S.sem("atqk"), it.n * 8 + (u + 1))
                        if not isinstance(it.n, int) or it.n * 4 + u // 2 >= 2:
                            e.wait_ge(S.sem("atpv"), it.n * 4 + (u // 2 - 1))
                        S.done(e.activation(pr[u % 4][:, :], pS[u % 2][:, :], ACT.Exp, scale=HD ** -0.5 / SA ** 2), "atexp")
                pipeline(e, NG, [(exps, 1)] + choice["scalar"][1](e))

            @blk.vector
            def _(v):
                init = Line(S, v, "atinit")
                init.start(It(0, 0))
                for i in range(2):
                    init(v.memset(k[i][:, :, :, :, :].rearrange("p t s j n -> p (t s j n)"), 0.0))
                    init(v.memset(pO[i][:, :], 0.0), "at_init" if i else None)
                choice["vector"][0](v)
                line = Line(S, v, "atdve")

                def into(b, g):
                    x = o[:, :].rearrange("p (b t h c) -> p b t h c", b=BATCH, t=4, h=G)
                    return x[:, bass.ds(b, 1), :, bass.ds(g, 1), :].rearrange("p b t h (i d) -> p (b t) (h i) d", i=4)

                def evacuate(it):
                    v.wait_ge(S.sem("atpv"), it.n * 4 + 4)
                    S.wait(v, "atX", it.back(2))
                    S.done(v.tensor_copy(oT[it.p][:, :], pO[it.p][:, :]), "atoT")

                def normalise(it):
                    line.start(it)
                    b, g = it.n // G, it.n % G
                    S.wait(v, "atX", it)
                    x = pX[:, 0, 0:1]
                    line(v.reciprocal(rc[:, :, :], bass.AP(x.tensor, x.offset + HD, [list(x.ap[0]), [P, 4], [32, 4]])))
                    line(v.tensor_tensor(
                        into(b, g), bass.AP(x.tensor, x.offset, [list(x.ap[0]), [P, 4], [32, 4], [1, HD]]),
                        bcast(rc[:, 0, 0:1], [(4, 4), (1, 4), (0, HD)]), ALU.mult), "ato")
                more = choice["vector"][1](v)
                pipeline(v, NG, [(evacuate, 2), more["score"], more["inner"], more["residual, norm"], (normalise, 2)])

        S.clear()
        phase_last(nc, S, sb, ps, a, R, K, o, ident, kept, out)


def choice_stages(nc, S, sb, mem, a, R, K, o, kept):
    oh, xs, lo, hi = kept
    sl = sb(mem, "lasl", [NTILE, DSL * GRID])
    ssum = sb(mem, "lassum", [NTILE, DSL])
    ssg = sb(mem, "lassg", [NTILE, DSL])
    sgn = sb(mem, "lasgn", [P, D])
    gam = sb(mem, "lagam", [P, D])
    bet = sb(mem, "labet", [P, D])
    xin = sb(mem, "laxin", [P, D])
    x3 = sb(mem, "lax3", [P, D])
    z = sb(mem, "laz", [P, D])
    xf = sb(mem, "laxf", [P, D])
    sg = sb(mem, "lasg", [P, D])
    st = [sb(mem, f"last{i}", [P, 6]) for i in range(2)]
    mv = [sb(mem, f"lamv{i}", [P, 2]) for i in range(2)]
    ts, cs = sb(mem, "lats", [P, NTILE]), sb(mem, "lacs", [P, NCL])
    key, best = sb(mem, "lakey", [P, NTILE]), sb(mem, "labest", [P, 1])
    sel = sb(mem, "lasel", [P, D])
    ve = [sb(mem, f"lave{i}", [P, 1]) for i in range(2)]
    rstd = [sb(mem, f"larstd{i}", [P, 1]) for i in range(2)]
    m = sb(mem, "lam", [P, D])

    def steps(first, second, lag):
        def stage(it):
            work = second if it.p else first
            if work:
                work(Single(it.half))
        return (stage, lag, 0, 2 * NT)

    def sync_first(e):
        e.dma_start(sl[:, :], a["slopes"]).then_inc(S.sem("la_sl"), 16)
        for t, name in ((gam, "gamma"), (bet, "beta")):
            e.dma_start(t[:, :], bass.AP(a[name].tensor, 0, [[0, P], [1, D]])).then_inc(S.sem("la_gb"), 16)
        e.wait_ge(S.sem("la_ssg"), 1)
        e.dma_start(R["sign"].rearrange("(t j) -> t j", j=DSL), ssg[:, :]).then_inc(S.sem("la_sign"), 16)
        e.wait_ge(S.sem("la_sign"), 16)
        e.dma_start(sgn[:, :], bass.AP(R["sign"].tensor, 0, [[0, P], [1, D]])).then_inc(S.sem("la_signb"), 16)

    def sync(e):
        def load(t):
            S.wait(e, "lax3", t.back(1))
            S.static(e)
            S.moved(e.dma_start(xin[:, :], R["x2"][bass.ds(t.n * P, P), :]), "laxin", t)
        return [steps(None, load, 8)]

    def gpsimd(e):
        line = Line(S, e, "lapool")

        def root(i):
            def work(t):
                S.wait(e, f"lave{i}", t)
                S.done(e.tensor_tensor(rstd[i][:, :], ve[i][:, :], K["mhalf"][:, :], ALU.pow), f"larstd{i}")
            return work

        def affine(t):
            line.start(t)
            S.wait(e, "laz2", t)
            line(e.tensor_tensor(xf[:, :], xf[:, :], gam[:, :], ALU.mult))
            line(e.tensor_tensor(xf[:, :], xf[:, :], bet[:, :], ALU.add), "laxf")
        return [steps(root(0), root(1), 10), steps(affine, None, 12)]

    def scalar_first(e):
        e.wait_ge(S.sem("la_ssum"), 1)
        e.activation(ssg[:, :], ssum[:, :], ACT.Sign).then_inc(S.sem("la_ssg"), 1)

    def scalar(e):
        def signs(t):
            S.wait(e, "laxf", t)
            S.wait(e, "lam", t.back(1))
            S.done(e.activation(sg[:, :], xf[:, :], ACT.Sign), "lasg")
        return [steps(None, signs, 12)]

    def vector_first(v):
        line = Line(S, v, "la0")
        line.start(It(0, 0))
        v.wait_ge(S.sem("la_sl"), 16)
        line(v.tensor_reduce(ssum[:, :], sl[:, :].rearrange("t (j g) -> t j g", g=GRID), AX.X, ALU.add))
        line(v.tensor_scalar(ssum[:, :], ssum[:, :], 1.0 / GRID, None, ALU.mult), "la_ssum")
        v.wait_ge(S.sem("la_gb"), 32)
        v.wait_ge(S.sem("la_signb"), 16)

    def vector(v):
        one, two, three, four, five = (Line(S, v, f"ladve{i}") for i in range(5))

        def stats(line, i, x):
            S.static(v)
            line(v.bn_stats(st[i][:, :], x))
            S.static(v)
            line(v.bn_aggr(mv[i][:, :], st[i][:, :]))
            line(v.tensor_scalar(ve[i][:, :], mv[i][:, 1:2], EPS, None, ALU.add), f"lave{i}")

        def residual(t):
            one.start(t)
            S.wait_moved(v, "laxin", t)
            one(v.scalar_tensor_tensor(x3[:, :], o[:, bass.ds(t.n * D, D)], K["gate"][:, 2:3], xin[:, :],
                                       ALU.mult, ALU.add), "lax3")
            stats(one, 0, x3[:, :])

        def norm(t):
            two.start(t)
            S.wait(v, "larstd0", t)
            two(v.tensor_scalar(z[:, :], x3[:, :], mv[0][:, 0:1], rstd[0][:, :], ALU.subtract, ALU.mult))
            stats(two, 1, z[:, :])
            two(v.scalar_tensor_tensor(o[:, bass.ds(t.n * D, D)], z[:, :], K["gate"][:, 3:4], x3[:, :], ALU.mult, ALU.add))

        def inner(t):
            three.start(t)
            S.wait(v, "larstd1", t)
            three(v.tensor_scalar(xf[:, :], z[:, :], mv[1][:, 0:1], rstd[1][:, :], ALU.subtract, ALU.mult), "laz2")

        def score(t):
            four.start(t)
            S.wait(v, "lasg", t)
            four(v.tensor_tensor(m[:, :], sg[:, :], sgn[:, :], ALU.mult), "lam")
            four(v.tensor_reduce(ts[:, :], m[:, :].rearrange("p (t j) -> p t j", j=DSL), AX.X, ALU.add))
            four(v.tensor_reduce(cs[:, :], ts[:, :].rearrange("p (c t) -> p c t", t=NTILE // NCL), AX.X, ALU.add))
            four(v.scalar_tensor_tensor(cs[:, :], cs[:, :], 8.0, K["iota"][:, 0:NCL], ALU.mult, ALU.subtract))
            four(v.tensor_scalar(cs[:, :], cs[:, :], 256.0, None, ALU.mult))
            four(v.scalar_tensor_tensor(
                key[:, :].rearrange("p (c t) -> p c t", c=NCL), ts[:, :].rearrange("p (c t) -> p c t", c=NCL), 8.0,
                bcast(K["iota"][:, 0:1], [(0, NCL), (1, NTILE // NCL)]), ALU.mult, ALU.subtract))
            four(v.tensor_tensor(key[:, :].rearrange("p (c t) -> p c t", c=NCL), key[:, :].rearrange("p (c t) -> p c t", c=NCL),
                                 bcast(cs[:, 0:1], [(1, NCL), (0, NTILE // NCL)]), ALU.add))
            four(v.tensor_reduce(best[:, :], key[:, :], AX.X, ALU.max))
            four(v.tensor_scalar(oh[:, bass.ds(t.n * NTILE, NTILE)], key[:, :], best[:, :], None, ALU.is_equal))
            four(v.tensor_tensor(sel[:, :].rearrange("p (t j) -> p t j", j=DSL), xf[:, :].rearrange("p (t j) -> p t j", j=DSL),
                                 chosen(oh, t), ALU.mult))
            four(v.tensor_reduce(xs[:, bass.ds(t.n * DSL, DSL)], sel[:, :].rearrange("p (t j) -> p j t", j=DSL), AX.X, ALU.add))
            four(v.tensor_reduce(lo[:, bass.ds(t.n, 1)], xs[:, bass.ds(t.n * DSL, DSL)], AX.X, ALU.min))
            four(v.tensor_reduce(hi[:, bass.ds(t.n, 1)], xs[:, bass.ds(t.n * DSL, DSL)], AX.X, ALU.max))
        return {"residual, norm": steps(residual, norm, 10), "score": steps(score, None, 14), "inner": steps(inner, None, 12)}
    return {"sync": (sync_first, sync), "gpsimd": gpsimd, "scalar": (scalar_first, scalar), "vector": (vector_first, vector)}


def chosen(oh, t):
    return oh[:, :].rearrange("p (n t a) -> p n t a", t=NTILE, a=1)[:, bass.ds(t.n, 1), :, :]\
        .rearrange("p n t a -> p (n t) a").to_broadcast((P, NTILE, DSL))


def phase_last(nc, S, sb, ps, a, R, K, o, ident, kept, out):
    BIG = 1e30
    oh, xs, lo, hi = kept
    with ExitStack() as mem:
        tab = sb(mem, "latab", [P, 2 * DSL * GRID + 1])
        oh16 = sb(mem, "laoh16", [P, NT * NTILE], f16)
        w1, w2 = sb(mem, "law1", [P, NT * NTILE]), sb(mem, "law2", [P, NT * NTILE])
        ext = [sb(mem, f"laext{i}", [P, NTILE]) for i in range(2)]
        col = [sb(mem, f"lacol{i}", [NTILE, 1]) for i in range(2)]
        colb = [sb(mem, f"lacolb{i}", [NTILE, P]) for i in range(2)]
        mn, mx = sb(mem, "lamn", [P, NT]), sb(mem, "lamx", [P, NT])
        num = sb(mem, "lanum", [P, NT * DSL])
        u = sb(mem, "lau", [P, NT * DSL])
        gi = sb(mem, "lagi", [P, NT * DSL])
        og = sb(mem, "laog", [P, NT * DSL * GRID])
        ohT = [sb(mem, f"laohT{i}", [P, P]) for i in range(2)]
        pick = sb(mem, "lapick", [P, 2, DSL * GRID])
        bs = sb(mem, "labs", [P, NT * 2 * DSL])
        osc = sb(mem, "laosc", [P, NT])
        dl = sb(mem, "ladl", [P, NT * DSL])
        res = [sb(mem, f"lares{i}", [P, D]) for i in range(2)]
        pEB = ps(mem, "lapEB", [P, 512])
        pE = pEB[0:NTILE, 0:2 * P].rearrange("p (a n) -> p a n", a=2)
        pB = pEB[:, 2 * P:3 * P].rearrange("p (a n) -> p a n", a=2)
        pH = [ps(mem, f"lapH{i}", [P, 1024], f16)[:, 0:P] for i in range(2)]
        pT = [[ps(mem, f"lapT{i}{j}", [P, 512]) for j in range(2)] for i in range(2)]
        blk = mem.enter_context(nc.Block())
        TG = DSL * GRID

        def finish(e, parity):
            line = Line(S, e, f"lafin{parity}")

            def tile(it):
                n = it.n * 2 + parity
                line.start(it)
                d = dl[:, :].rearrange("p (n a j) -> p n a j", n=NT, a=1)[:, bass.ds(n, 1), :, :]\
                    .rearrange("p n a j -> p (n a) j").to_broadcast((P, NTILE, DSL))
                line(e.tensor_tensor(res[parity][:, :].rearrange("p (t j) -> p t j", j=DSL), chosen(oh, Single(n)), d, ALU.mult))
                S.static(e)
                line(e.tensor_tensor(o[:, bass.ds(n * D, D)], res[parity][:, :], o[:, bass.ds(n * D, D)], ALU.add), f"lares{parity}")
            pipeline(e, NT // 2, [(tile, 0)])

        @blk.gpsimd
        def _(e):
            e.wait_ge(S.sem("ladelta"), 1)
            finish(e, 1)

        @blk.sync
        def _(e):
            for r in (slice(0, NTILE), slice(NTILE, P)):
                e.dma_start(tab[r, 0:TG], a["bases"]).then_inc(S.sem("la_tab"), 16)
                e.dma_start(tab[r, TG:2 * TG], a["slopes"]).then_inc(S.sem("la_tab"), 16)
                e.dma_start(tab[r, 2 * TG:], a["oscale"]).then_inc(S.sem("la_tab"), 16)

            def store(it):
                e.wait_ge(S.sem(f"lares{it.p}"), it.half + 1)
                S.static(e)
                S.moved(e.dma_start(out[bass.ds(it.n * P, P), :], o[:, bass.ds(it.n * D, D)]), "laout", it)
            pipeline(e, NT, [(store, 0)])
            for p in range(2):
                S.wait_moved(e, "laout", It(NT // 2 - 1, p))

        @blk.scalar
        def _(e):
            def turn(it):
                S.wait(e, "laH", it)
                S.wait(e, "laT", it.back(2))
                S.done(e.activation(ohT[it.p][:, :], pH[it.p], ACT.Copy), "laohT")
            pipeline(e, NT // 2, [(turn, 0)])

        @blk.vector
        def _(v):
            tail = Line(S, v, "la3")
            tail.start(It(0, 0))
            tail(v.tensor_copy(oh16[:, :], oh[:, :]), "laoh16")
            three = lambda t: t[:, :].rearrange("p (n t) -> p n t", n=NT)
            for i, (val, op, big) in enumerate(((lo, ALU.min, BIG), (hi, ALU.max, -BIG))):
                tail(v.tensor_scalar(w1[:, :], oh[:, :], -big, big, ALU.mult, ALU.add))
                tail(v.tensor_tensor(three(w2), three(oh), bcast(val[:, 0:1], [(1, NT), (0, NTILE)]), ALU.mult))
                tail(v.tensor_tensor(w1[:, :], w1[:, :], w2[:, :], ALU.add))
                tail(v.tensor_reduce(ext[i][:, :], w1[:, :].rearrange("p (n t) -> p t n", n=NT), AX.X, op), f"laext{i}")
            for i, op in enumerate((ALU.min, ALU.max)):
                v.wait_ge(S.sem("laE"), 2)
                tail(v.tensor_reduce(col[i][:, :], pE[:, i, :], AX.X, op))
                tail(v.tensor_copy(colb[i][:, :], bcast(col[i][:, :], [(0, P)])), f"lacol{i}")
            for i, to in enumerate((mn, mx)):
                v.wait_ge(S.sem("laB"), 2)
                tail(v.tensor_tensor(three(w1), three(oh), bcast(pB[:, i, 0:1], [(0, NT), (1, NTILE)]), ALU.mult))
                tail(v.tensor_reduce(to[:, :], three(w1), AX.X, ALU.add))
            eight = lambda t: t[:, :].rearrange("p (n j) -> p n j", j=DSL)
            tail(v.tensor_tensor(eight(num), eight(xs), bcast(mn[:, 0:1], [(1, NT), (0, DSL)]), ALU.subtract))
            tail(v.tensor_tensor(mx[:, :], mx[:, :], mn[:, :], ALU.subtract))
            tail(v.tensor_scalar(mx[:, :], mx[:, :], 1e-8, None, ALU.add))
            tail(v.reciprocal(mx[:, :], mx[:, :]))
            tail(v.tensor_tensor(eight(u), eight(num), bcast(mx[:, 0:1], [(1, NT), (0, DSL)]), ALU.mult))
            tail(v.tensor_scalar(u[:, :], u[:, :], 0.0, float(np.float32(1.0 - 1e-6)), ALU.max, ALU.min))
            tail(v.tensor_scalar(u[:, :], u[:, :], float(GRID), None, ALU.mult))
            sixteen = og[:, :].rearrange("p (n g) -> p n g", g=GRID)
            grid = bcast(K["iota"][:, 0:1], [(0, NT * DSL), (1, GRID)])
            tail(v.tensor_tensor(sixteen, bcast(u[:, 0:1], [(1, NT * DSL), (0, GRID)]), grid, ALU.is_ge))
            tail(v.tensor_reduce(gi[:, :], sixteen, AX.X, ALU.add))
            tail(v.tensor_scalar(gi[:, :], gi[:, :], -1.0, None, ALU.add))
            tail(v.tensor_tensor(sixteen, bcast(gi[:, 0:1], [(1, NT * DSL), (0, GRID)]), grid, ALU.is_equal))
            tail(v.tensor_tensor(u[:, :], u[:, :], gi[:, :], ALU.subtract))
            rows = Line(S, v, "la4")

            def pickup(it):
                rows.start(it)
                S.wait(v, "laT", it)
                for j in range(2):
                    n = it.n * 2 + j
                    g = og[:, :].rearrange("p (a n g) -> p a n g", a=1, n=NT)[:, :, bass.ds(n, 1), :]\
                        .rearrange("p a n g -> p a (n g)").to_broadcast((P, 2, TG))
                    t = pT[it.p][j]
                    rows(v.tensor_tensor(pick[:, :, :], t[:, 0:2 * TG].rearrange("p (a g) -> p a g", a=2), g, ALU.mult))
                    rows(v.tensor_reduce(bs[:, bass.ds(n * 2 * DSL, 2 * DSL)],
                                         pick[:, :, :].rearrange("p a (j g) -> p (a j) g", g=GRID), AX.X, ALU.add))
                    rows(v.tensor_copy(osc[:, bass.ds(n, 1)], t[:, 2 * TG:2 * TG + 1]), "lapick" if j else None)
            pipeline(v, NT // 2, [(pickup, 0)])
            two = bs[:, :].rearrange("p (n a j) -> p n a j", a=2, j=DSL)
            tail(v.tensor_tensor(eight(dl), two[:, :, 1, :], eight(u), ALU.mult))
            tail(v.tensor_tensor(eight(dl), two[:, :, 0, :], eight(dl), ALU.add))
            tail(v.tensor_scalar(osc[:, :], osc[:, :], K["gate"][:, 3:4], None, ALU.mult))
            tail(v.tensor_tensor(eight(dl), eight(dl), bcast(osc[:, 0:1], [(1, NT), (0, DSL)]), ALU.mult))
            tail(v.memset(w1[:, 0:1], 0.0), "ladelta")
            finish(v, 0)

        @blk.tensor
        def _(e):
            for i in range(2):
                e.wait_ge(S.sem(f"laext{i}"), 1)
                e.transpose(pE[:, i, :], ext[i][:, :], ident[:, :]).then_inc(S.sem("laE"), 1)
            for i in range(2):
                e.wait_ge(S.sem("lacol1"), 1)
                e.transpose(pB[:, i, :], colb[i][:, :], ident[0:NTILE, 0:NTILE]).then_inc(S.sem("laB"), 1)
            e.wait_ge(S.sem("la_tab"), 96)
            e.wait_ge(S.sem("laoh16"), 1)

            def turn(it):
                S.wait(e, "laohT", it.back(2))
                S.static(e)
                S.done(e.transpose(pH[it.p], oh16[:, bass.ds(it.n * P, P)], K["ident"][:, :]), "laH")

            def look(it):
                S.wait(e, "laohT", it)
                S.wait(e, "lapick", it.back(2))
                for j in range(2):
                    r = slice(NTILE * j, NTILE * j + NTILE)
                    last = e.matmul(pT[it.p][j][:, 0:2 * TG + 1], ohT[it.p][r, :], tab[r, :], start=True, stop=True)
                S.done(last, "laT")
            pipeline(e, NT // 2, [(turn, 0), (look, 1)])


def layout(x, itok, ctx, gx, gf, sw1, sb1, sw2, sb2, rw1, rb1, rw2, rb2, cen, bias, wq, wk, wv,
           gamma, beta, bases, slopes, oscale):
    def rows(w):
        w = w.reshape(w.shape[:-2] + (w.shape[-2] // P, P, w.shape[-1]))
        return np.ascontiguousarray(np.swapaxes(w, -3, -2)).reshape(w.shape[:-3] + (P, -1))

    def second(w, b):
        z = np.zeros(w.shape[:-2] + (FB * P - FF - 1, w.shape[-1]), w.dtype)
        return rows(np.concatenate([w, b[..., None, :], z], axis=-2))

    def column(b):
        z = np.zeros(b.shape[:-1] + (FB * P - FF,), b.dtype)
        b = np.concatenate([b, z], axis=-1)
        return np.ascontiguousarray(b.reshape(-1, P).T)

    kv = np.concatenate([wk, wv], axis=0).reshape(NH, HD, 2, D)
    wkh, wvh = (kv[:, :, s].reshape(NH * HD, D) for s in range(2))
    rowi = np.arange(P)
    return {
        "x": x.reshape(TOK, D),
        "ids": np.ascontiguousarray(itok.reshape(NT, P).T),
        "gates": np.concatenate([gx[0:1], gf[0:1], gx[1:2], gf[1:2]]),
        "ctxT": rows(np.ascontiguousarray(ctx.transpose(0, 2, 1))),
        "sw1": rows(sw1), "sb1": column(sb1), "sw2": second(sw2, sb2),
        "rw1": rows(rw1), "rb1": rb1, "rw2": second(rw2, rb2),
        "cenT": rows(np.ascontiguousarray(cen.T)), "bias": bias.reshape(1, NR),
        "wqT": rows(np.ascontiguousarray(wq.T)), "wkT": rows(np.ascontiguousarray(wkh.T)),
        "wvT": rows(np.ascontiguousarray(wvh.T)),
        "gamma": gamma.reshape(1, D), "beta": beta.reshape(1, D),
        "bases": bases.reshape(NTILE, DSL * GRID), "slopes": slopes.reshape(NTILE, DSL * GRID),
        "oscale": oscale.reshape(NTILE, 1),
        "c_ident": np.eye(P, dtype=np.float16),
        "c_ident32": np.eye(P, dtype=np.float32),
        "c_tri": (rowi[:, None] < rowi[None, :]).astype(np.float16),
        "c_ones": np.ones((P, P), np.float16),
        "c_iota": np.tile(np.arange(16, dtype=np.float32), (P, 1)),
        "c_tok": (np.arange(NT)[None, :] * P + rowi[:, None]).astype(np.int32),
        "c_iotan": np.arange(N2, dtype=np.float32)[None, :],
    }


def kernel(**inputs):
    import concourse.bacc as bacc
    from concourse.bass_utils import run_bass_kernel_spmd

    names = ["x", "itok_BxS_13_99985", "ctx_2048", "g_xattn", "g_ffn",
             "L0_ffn_shared_w1", "L0_ffn_shared_b1", "L0_ffn_shared_w2", "L0_ffn_shared_b2",
             "L0_ffn_routed_w1", "L0_ffn_routed_b1", "L0_ffn_routed_w2", "L0_ffn_routed_b2",
             "L0_ffn_centroids", "L0_ffn_bias", "L1_xattn_Wq", "L1_xattn_Wk", "L1_xattn_Wv",
             "L1_ffn_ln_gamma", "L1_ffn_ln_beta", "L1_ffn_spline_bases", "L1_ffn_spline_slopes", "L1_ffn_output_scale"]
    arrays = layout(*[np.asarray(inputs[n]) for n in names])
    arrays = {name: np.ascontiguousarray(v) for name, v in arrays.items()}
    nc = bacc.Bacc("TRN2", target_bir_lowering=False, num_devices=1)
    a = {name: nc.dram_tensor(name, v.shape, mybir.dt.from_np(v.dtype), kind="ExternalInput").ap()
         for name, v in arrays.items()}
    out = nc.dram_tensor("out", (TOK, D), f32, kind="ExternalOutput").ap()
    build(nc, a, out)
    r = run_bass_kernel_spmd(nc, [arrays], core_ids=[0])
    return r.results[0]["out"].reshape(BATCH, SEQ, D)
```
